# Optimizing a Trainium2 kernel written in Bass

```python
import numpy as np
import jax
import jax.numpy as jnp

def _softmax(x, axis=-1):
    return jax.nn.softmax(x, axis=axis)

def _gelu(x):
    return jax.nn.gelu(x, approximate=True)

def _silu(x):
    return jax.nn.silu(x)

def _sigmoid(x):
    return jax.nn.sigmoid(x)

def _layernorm(x, axis=-1, eps=1e-05):
    m = jnp.mean(x, axis=axis, keepdims=True)
    v = jnp.var(x, axis=axis, keepdims=True)
    return (x - m) / jnp.sqrt(v + eps)

def _scatter_add(tgt, idx, src, axis=0):
    return tgt.at[idx].add(src)

def _segment_sum(src, seg, n):
    return jax.ops.segment_sum(src, seg, n)
kernel_name = 'mk_prb_d2_jaxref_r8_1ff470'

def setup_inputs(seed: int=0):
    np.random.seed(seed)
    _w = jnp.asarray

    def _L0_attn_setup():
        import jax, jax.numpy as jnp
        import numpy as np
        D_MODEL = 128
        N_HEADS = 16
        HIDDEN = max(8, D_MODEL // 2)
        EPS = 1e-12
        key = jax.random.key(seed)
        ks = jax.random.split(key, 12)
        s = 0.02
        inp = {'x': jax.random.normal(ks[0], (8, 128, D_MODEL), dtype=jnp.float32), 'Wq': jax.random.normal(ks[1], (D_MODEL, D_MODEL), dtype=jnp.float32) * s, 'bq': jnp.zeros((D_MODEL,), dtype=jnp.float32), 'Wk': jax.random.normal(ks[2], (D_MODEL, D_MODEL), dtype=jnp.float32) * s, 'bk': jnp.zeros((D_MODEL,), dtype=jnp.float32), 'Wv': jax.random.normal(ks[3], (D_MODEL, D_MODEL), dtype=jnp.float32) * s, 'bv': jnp.zeros((D_MODEL,), dtype=jnp.float32), 'Wo': jax.random.normal(ks[4], (D_MODEL, D_MODEL), dtype=jnp.float32) * s, 'bo': jnp.zeros((D_MODEL,), dtype=jnp.float32), 'g': jnp.zeros((N_HEADS,), dtype=jnp.float32), 'Wg1': jax.random.normal(ks[5], (HIDDEN, D_MODEL), dtype=jnp.float32) * s, 'bg1': jnp.zeros((HIDDEN,), dtype=jnp.float32), 'Wg2': jax.random.normal(ks[6], (N_HEADS, HIDDEN), dtype=jnp.float32) * s, 'bg2': jnp.zeros((N_HEADS,), dtype=jnp.float32)}
        return inp
    _L0_attn_in = _L0_attn_setup()

    def _L0_ffn_setup():
        import jax, jax.numpy as jnp
        import numpy as np
        B, T, C = (2, 64, 128)
        I = 512
        E = 8
        K = 2
        key = jax.random.key(seed)
        ks = jax.random.split(key, 8)
        s = 0.02
        return {'x': jax.random.normal(ks[0], (B, T, C), jnp.float32), 'Wr1': jax.random.normal(ks[1], (C, C // 4), jnp.float32) * s, 'br1': jnp.zeros((C // 4,), jnp.float32), 'Wr2': jax.random.normal(ks[2], (C // 4, E), jnp.float32) * s, 'br2': jnp.zeros((E,), jnp.float32), 'Ws1': jax.random.normal(ks[3], (C, I), jnp.float32) * s, 'bs1': jnp.zeros((I,), jnp.float32), 'Ws2': jax.random.normal(ks[4], (I, C), jnp.float32) * s, 'bs2': jnp.zeros((C,), jnp.float32), 'We1': jax.random.normal(ks[5], (E, C, I), jnp.float32) * s, 'be1': jnp.zeros((E, I), jnp.float32), 'We2': jax.random.normal(ks[6], (E, I, C), jnp.float32) * s, 'be2': jnp.zeros((E, C), jnp.float32)}
    _L0_ffn_in = _L0_ffn_setup()

    def _L1_attn_setup():
        import jax, jax.numpy as jnp
        import numpy as np
        B_, L_, D_, N_ = (4, 256, 128, 64)
        key = jax.random.key(seed)
        ks = jax.random.split(key, 8)
        H, N = (D_, N_)
        x = jax.random.normal(ks[0], (B_, L_, H), jnp.float32)
        A_re = -0.5 * jnp.ones((H, N), jnp.float32)
        A_im = jnp.pi * jnp.broadcast_to(jnp.arange(N, dtype=jnp.float32)[None, :], (H, N))
        log_dt = jax.random.uniform(ks[1], (H,), jnp.float32) * (np.log(0.1) - np.log(0.001)) + np.log(0.001)
        C_re = jax.random.normal(ks[2], (H, N), jnp.float32) * 0.5 ** 0.5
        C_im = jax.random.normal(ks[3], (H, N), jnp.float32) * 0.5 ** 0.5
        D = jax.random.normal(ks[4], (H,), jnp.float32)
        W_out = jax.random.normal(ks[5], (H, 2 * H), jnp.float32) / np.sqrt(H)
        b_out = jnp.zeros((2 * H,), jnp.float32)
        gamma = jnp.ones((H,), jnp.float32)
        beta = jnp.zeros((H,), jnp.float32)
        return dict(x=x, A_re=A_re, A_im=A_im, log_dt=log_dt, C_re=C_re, C_im=C_im, D=D, W_out=W_out, b_out=b_out, gamma=gamma, beta=beta)
    _L1_attn_in = _L1_attn_setup()

    def _L1_ffn_setup():
        import math
        import jax, jax.numpy as jnp
        import numpy as np
        HIDDEN = 128
        INTER = 512
        EXPERTS = 8
        B, T = (4, 256)
        EPS = 1e-12
        CAP_FACTOR = 1.0
        MIN_CAP = 4

        def layer_norm(x, g, b, eps=EPS):
            m = jnp.mean(x, axis=-1, keepdims=True)
            v = jnp.var(x, axis=-1, keepdims=True)
            return (x - m) * jax.lax.rsqrt(v + eps) * g + b

        def top1_gate(x, wg, capacity):
            logits = x @ wg
            gates = jax.nn.softmax(logits, axis=-1)
            E = wg.shape[-1]
            idx = jnp.argmax(gates, axis=-1)
            mask1 = jax.nn.one_hot(idx, E, dtype=gates.dtype)
            locations = jnp.cumsum(mask1, axis=0) - mask1
            mask1 = mask1 * (locations < capacity).astype(gates.dtype)
            gates1_s = jnp.sum(gates * mask1, axis=-1)
            loc_s = jnp.sum(locations * mask1, axis=-1).astype(jnp.int32)
            loc_oh = jax.nn.one_hot(loc_s, capacity, dtype=gates.dtype)
            combine = gates1_s[:, None, None] * mask1[:, :, None] * loc_oh[:, None, :]
            dispatch = jax.lax.stop_gradient((combine > 0).astype(x.dtype))
            return (combine, dispatch)
        key = jax.random.key(seed)
        ks = jax.random.split(key, 8)
        s = 0.02
        return {'x': jax.random.normal(ks[0], (B, T, HIDDEN), jnp.float32), 'attn_nw': jnp.ones((HIDDEN,), jnp.float32), 'attn_nb': jnp.zeros((HIDDEN,), jnp.float32), 'wg': jax.random.normal(ks[1], (HIDDEN, EXPERTS), jnp.float32) * s, 'inter_w': jax.random.normal(ks[2], (EXPERTS, HIDDEN, INTER), jnp.float32) * s, 'inter_b': jnp.zeros((EXPERTS, INTER), jnp.float32), 'output_w': jax.random.normal(ks[3], (EXPERTS, INTER, HIDDEN), jnp.float32) * s, 'output_b': jnp.zeros((EXPERTS, HIDDEN), jnp.float32), 'res_inter_w': jax.random.normal(ks[4], (HIDDEN, INTER), jnp.float32) * s, 'res_inter_b': jnp.zeros((INTER,), jnp.float32), 'res_output_w': jax.random.normal(ks[5], (INTER, HIDDEN), jnp.float32) * s, 'res_output_b': jnp.zeros((HIDDEN,), jnp.float32), 'res_coef': jax.random.normal(ks[6], (HIDDEN, 2), jnp.float32) * s}
    _L1_ffn_in = _L1_ffn_setup()
    _d = {'L0_attn_x': _L0_attn_in['x'], 'L0_attn_Wq': _L0_attn_in['Wq'], 'L0_attn_bq': _L0_attn_in['bq'], 'L0_attn_Wk': _L0_attn_in['Wk'], 'L0_attn_bk': _L0_attn_in['bk'], 'L0_attn_Wv': _L0_attn_in['Wv'], 'L0_attn_bv': _L0_attn_in['bv'], 'L0_attn_Wo': _L0_attn_in['Wo'], 'L0_attn_bo': _L0_attn_in['bo'], 'L0_attn_g': _L0_attn_in['g'], 'L0_attn_Wg1': _L0_attn_in['Wg1'], 'L0_attn_bg1': _L0_attn_in['bg1'], 'L0_attn_Wg2': _L0_attn_in['Wg2'], 'L0_attn_bg2': _L0_attn_in['bg2'], 'L0_ffn_Wr1': _L0_ffn_in['Wr1'], 'L0_ffn_br1': _L0_ffn_in['br1'], 'L0_ffn_Wr2': _L0_ffn_in['Wr2'], 'L0_ffn_br2': _L0_ffn_in['br2'], 'L0_ffn_Ws1': _L0_ffn_in['Ws1'], 'L0_ffn_bs1': _L0_ffn_in['bs1'], 'L0_ffn_Ws2': _L0_ffn_in['Ws2'], 'L0_ffn_bs2': _L0_ffn_in['bs2'], 'L0_ffn_We1': _L0_ffn_in['We1'], 'L0_ffn_be1': _L0_ffn_in['be1'], 'L0_ffn_We2': _L0_ffn_in['We2'], 'L0_ffn_be2': _L0_ffn_in['be2'], 'L1_attn_A_re': _L1_attn_in['A_re'], 'L1_attn_A_im': _L1_attn_in['A_im'], 'L1_attn_log_dt': _L1_attn_in['log_dt'], 'L1_attn_C_re': _L1_attn_in['C_re'], 'L1_attn_C_im': _L1_attn_in['C_im'], 'L1_attn_D': _L1_attn_in['D'], 'L1_attn_W_out': _L1_attn_in['W_out'], 'L1_attn_b_out': _L1_attn_in['b_out'], 'L1_attn_gamma': _L1_attn_in['gamma'], 'L1_attn_beta': _L1_attn_in['beta'], 'L1_ffn_attn_nw': _L1_ffn_in['attn_nw'], 'L1_ffn_attn_nb': _L1_ffn_in['attn_nb'], 'L1_ffn_wg': _L1_ffn_in['wg'], 'L1_ffn_inter_w': _L1_ffn_in['inter_w'], 'L1_ffn_inter_b': _L1_ffn_in['inter_b'], 'L1_ffn_output_w': _L1_ffn_in['output_w'], 'L1_ffn_output_b': _L1_ffn_in['output_b'], 'L1_ffn_res_inter_w': _L1_ffn_in['res_inter_w'], 'L1_ffn_res_inter_b': _L1_ffn_in['res_inter_b'], 'L1_ffn_res_output_w': _L1_ffn_in['res_output_w'], 'L1_ffn_res_output_b': _L1_ffn_in['res_output_b'], 'L1_ffn_res_coef': _L1_ffn_in['res_coef']}
    _x0 = _d['L0_attn_x']
    _d['L0_attn_x'] = jax.random.normal(jax.random.fold_in(jax.random.key(seed), 1), (32, 256, 128), dtype=_x0.dtype)
    del _x0
    return _d

def reference(L0_attn_x, L0_attn_Wq, L0_attn_bq, L0_attn_Wk, L0_attn_bk, L0_attn_Wv, L0_attn_bv, L0_attn_Wo, L0_attn_bo, L0_attn_g, L0_attn_Wg1, L0_attn_bg1, L0_attn_Wg2, L0_attn_bg2, L0_ffn_Wr1, L0_ffn_br1, L0_ffn_Wr2, L0_ffn_br2, L0_ffn_Ws1, L0_ffn_bs1, L0_ffn_Ws2, L0_ffn_bs2, L0_ffn_We1, L0_ffn_be1, L0_ffn_We2, L0_ffn_be2, L1_attn_A_re, L1_attn_A_im, L1_attn_log_dt, L1_attn_C_re, L1_attn_C_im, L1_attn_D, L1_attn_W_out, L1_attn_b_out, L1_attn_gamma, L1_attn_beta, L1_ffn_attn_nw, L1_ffn_attn_nb, L1_ffn_wg, L1_ffn_inter_w, L1_ffn_inter_b, L1_ffn_output_w, L1_ffn_output_b, L1_ffn_res_inter_w, L1_ffn_res_inter_b, L1_ffn_res_output_w, L1_ffn_res_output_b, L1_ffn_res_coef):

    def _L0_attn_ref(x, Wq, bq, Wk, bk, Wv, bv, Wo, bo, g, Wg1, bg1, Wg2, bg2):
        import jax, jax.numpy as jnp
        import numpy as np
        D_MODEL = 128
        N_HEADS = 16
        HIDDEN = max(8, D_MODEL // 2)
        EPS = 1e-12
        B, T, D = x.shape
        H, dk = (N_HEADS, D // N_HEADS)

        def proj(W, b):
            return (x @ W.T + b).reshape(B, T, H, dk).transpose(0, 2, 1, 3)
        Q = proj(Wq, bq)
        K = proj(Wk, bk)
        V = proj(Wv, bv)
        Qn = Q / jnp.maximum(jnp.linalg.norm(Q, axis=-1, keepdims=True), EPS)
        Kn = K / jnp.maximum(jnp.linalg.norm(K, axis=-1, keepdims=True), EPS)
        scores = jnp.einsum('bhqd,bhkd->bhqk', Qn, Kn) / jnp.sqrt(jnp.float32(dk))
        attn = jax.nn.softmax(scores, axis=-1)
        head_outs = jnp.einsum('bhqk,bhkd->bhqd', attn, V)
        gate_static = jax.nn.sigmoid(g)[None, :, None, None]
        h = jax.nn.gelu(x @ Wg1.T + bg1, approximate=False)
        gate_logits = (h @ Wg2.T + bg2).mean(axis=1)
        gate_dynamic = jax.nn.sigmoid(gate_logits)[:, :, None, None]
        head_outs = head_outs * (gate_static * gate_dynamic)
        out = head_outs.transpose(0, 2, 1, 3).reshape(B, T, D)
        return out @ Wo.T + bo

    def _L0_ffn_ref(x, Wr1, br1, Wr2, br2, Ws1, bs1, Ws2, bs2, We1, be1, We2, be2):
        import jax, jax.numpy as jnp
        import numpy as np
        B, T, C = (2, 64, 128)
        I = 512
        E = 8
        K = 2
        Bb, Tt, Cc = x.shape
        xf = x.reshape(-1, Cc)
        logits = jax.nn.relu(xf @ Wr1 + br1) @ Wr2 + br2
        gates = jax.nn.softmax(logits, axis=-1)
        tg, ti = jax.lax.top_k(gates, K)
        tg = jax.nn.softmax(tg / K, axis=-1)
        out = jax.nn.silu(xf @ Ws1 + bs1) @ Ws2 + bs2
        for e in range(E):
            h = jax.nn.silu(xf @ We1[e] + be1[e]) @ We2[e] + be2[e]
            w = jnp.sum(tg * (ti == e), axis=-1)
            out = out + w[:, None] * h
        return out.reshape(Bb, Tt, Cc)

    def _L1_attn_ref(x, A_re, A_im, log_dt, C_re, C_im, D, W_out, b_out, gamma, beta):
        import jax, jax.numpy as jnp
        import numpy as np
        B_, L_, D_, N_ = (4, 256, 128, 64)
        Bsz, L, H = x.shape
        A = A_re + 1j * A_im
        C = C_re + 1j * C_im
        dt = jnp.exp(log_dt)
        dtA = A * dt[:, None]
        Ct = C * (jnp.exp(dtA) - 1.0) / A
        P = jnp.exp(dtA[:, :, None] * jnp.arange(L, dtype=jnp.float32))
        K = 2.0 * jnp.einsum('hn,hnl->hl', Ct, P).real
        Kf = jnp.fft.rfft(K, n=2 * L, axis=-1)
        uf = jnp.fft.rfft(x, n=2 * L, axis=1)
        y = jnp.fft.irfft(uf * Kf.T[None], n=2 * L, axis=1)[:, :L]
        y = y + x * D
        y = jax.nn.gelu(y)
        y = y @ W_out + b_out
        y = y[..., :H] * jax.nn.sigmoid(y[..., H:])
        mu = jnp.mean(y, axis=-1, keepdims=True)
        var = jnp.var(y, axis=-1, keepdims=True)
        return (y - mu) / jnp.sqrt(var + 1e-05) * gamma + beta

    def _L1_ffn_ref(x, attn_nw, attn_nb, wg, inter_w, inter_b, output_w, output_b, res_inter_w, res_inter_b, res_output_w, res_output_b, res_coef):
        import math
        import jax, jax.numpy as jnp
        import numpy as np
        HIDDEN = 128
        INTER = 512
        EXPERTS = 8
        B, T = (4, 256)
        EPS = 1e-12
        CAP_FACTOR = 1.0
        MIN_CAP = 4

        def layer_norm(x, g, b, eps=EPS):
            m = jnp.mean(x, axis=-1, keepdims=True)
            v = jnp.var(x, axis=-1, keepdims=True)
            return (x - m) * jax.lax.rsqrt(v + eps) * g + b

        def top1_gate(x, wg, capacity):
            logits = x @ wg
            gates = jax.nn.softmax(logits, axis=-1)
            E = wg.shape[-1]
            idx = jnp.argmax(gates, axis=-1)
            mask1 = jax.nn.one_hot(idx, E, dtype=gates.dtype)
            locations = jnp.cumsum(mask1, axis=0) - mask1
            mask1 = mask1 * (locations < capacity).astype(gates.dtype)
            gates1_s = jnp.sum(gates * mask1, axis=-1)
            loc_s = jnp.sum(locations * mask1, axis=-1).astype(jnp.int32)
            loc_oh = jax.nn.one_hot(loc_s, capacity, dtype=gates.dtype)
            combine = gates1_s[:, None, None] * mask1[:, :, None] * loc_oh[:, None, :]
            dispatch = jax.lax.stop_gradient((combine > 0).astype(x.dtype))
            return (combine, dispatch)
        Bx, Tx, M = x.shape
        S = Bx * Tx
        E = wg.shape[-1]
        capacity = max(MIN_CAP, math.ceil(S / E * CAP_FACTOR))
        residual = x.reshape(S, M)
        attn_out = layer_norm(residual, attn_nw, attn_nb)
        combine, dispatch = top1_gate(attn_out, wg, capacity)
        dispatched = jnp.einsum('sec,sm->ecm', dispatch, attn_out)
        h = jax.nn.gelu(jnp.einsum('ecm,emi->eci', dispatched, inter_w) + inter_b[:, None, :], approximate=True)
        expert_out = jnp.einsum('eci,eim->ecm', h, output_w) + output_b[:, None, :]
        moe_out = jnp.einsum('sec,ecm->sm', combine, expert_out)
        rh = jax.nn.gelu(attn_out @ res_inter_w + res_inter_b, approximate=True)
        res_mlp_out = rh @ res_output_w + res_output_b
        coef = jax.nn.softmax(attn_out @ res_coef, axis=-1)
        out = res_mlp_out * coef[:, :1] + moe_out * coef[:, 1:]
        out = out + residual
        return out.reshape(Bx, Tx, M)
    x = L0_attn_x
    xn = _layernorm(x, axis=-1)
    x = x + _L0_attn_ref(xn, L0_attn_Wq, L0_attn_bq, L0_attn_Wk, L0_attn_bk, L0_attn_Wv, L0_attn_bv, L0_attn_Wo, L0_attn_bo, L0_attn_g, L0_attn_Wg1, L0_attn_bg1, L0_attn_Wg2, L0_attn_bg2) + _L0_ffn_ref(xn, L0_ffn_Wr1, L0_ffn_br1, L0_ffn_Wr2, L0_ffn_br2, L0_ffn_Ws1, L0_ffn_bs1, L0_ffn_Ws2, L0_ffn_bs2, L0_ffn_We1, L0_ffn_be1, L0_ffn_We2, L0_ffn_be2)
    xn = _layernorm(x, axis=-1)
    x = x + _L1_attn_ref(xn, L1_attn_A_re, L1_attn_A_im, L1_attn_log_dt, L1_attn_C_re, L1_attn_C_im, L1_attn_D, L1_attn_W_out, L1_attn_b_out, L1_attn_gamma, L1_attn_beta) + _L1_ffn_ref(xn, L1_ffn_attn_nw, L1_ffn_attn_nb, L1_ffn_wg, L1_ffn_inter_w, L1_ffn_inter_b, L1_ffn_output_w, L1_ffn_output_b, L1_ffn_res_inter_w, L1_ffn_res_inter_b, L1_ffn_res_output_w, L1_ffn_res_output_b, L1_ffn_res_coef)
    return x

_drawn_inputs = setup_inputs


def setup_inputs(seed=0):
    import zlib

    import numpy as np

    out = dict(_drawn_inputs(seed))
    spreads = {'L0_attn_bq': (0.0, 0.8),
     'L0_attn_bk': (0.0, 0.8),
     'L0_attn_bv': (0.0, 0.8),
     'L0_attn_bo': (0.0, 0.1),
     'L0_attn_g': (0.0, 0.8),
     'L0_attn_bg1': (0.0, 0.8),
     'L0_attn_bg2': (0.0, 0.8),
     'L0_ffn_br1': (0.0, 0.374),
     'L0_ffn_br2': (0.0, 0.1),
     'L0_ffn_bs1': (0.0, 0.304),
     'L0_ffn_bs2': (0.0, 0.1),
     'L0_ffn_be1': (0.0, 0.419),
     'L0_ffn_be2': (0.0, 0.1),
     'L1_attn_A_re': (-0.5, 0.545),
     'L1_attn_b_out': (0.0, 0.286),
     'L1_attn_gamma': (1.0, 0.2),
     'L1_attn_beta': (0.0, 0.291),
     'L1_ffn_attn_nw': (1.0, 0.6),
     'L1_ffn_attn_nb': (0.0, 0.8),
     'L1_ffn_inter_b': (0.0, 0.8),
     'L1_ffn_output_b': (0.0, 0.8),
     'L1_ffn_res_inter_b': (0.0, 0.8),
     'L1_ffn_res_output_b': (0.0, 0.399)}
    factors = {'L0_attn_Wq': 8.0,
     'L0_attn_Wk': 8.0,
     'L0_attn_Wv': 8.0,
     'L0_attn_Wo': 8.0,
     'L0_attn_Wg1': 8.0,
     'L0_attn_Wg2': 8.0,
     'L1_ffn_wg': 8.0,
     'L1_ffn_inter_w': 8.0,
     'L1_ffn_output_w': 8.0,
     'L1_ffn_res_inter_w': 4.452,
     'L1_ffn_res_output_w': 4.124,
     'L1_ffn_res_coef': 8.0}
    for name, (base, spread) in spreads.items():
        noise = np.random.default_rng([zlib.crc32(name.encode()), seed]).standard_normal(out[name].shape)
        drawn = base * np.exp(spread * noise) if base else spread * noise
        out[name] = jnp.asarray(drawn.astype(out[name].dtype))
    for name, factor in factors.items():
        out[name] = (out[name] * factor).astype(out[name].dtype)
    return out
```

```python
from contextlib import ExitStack, contextmanager

import numpy as np

import concourse.bass as bass
from concourse import mybir

F32 = mybir.dt.float32
F16 = mybir.dt.float16
ALU = mybir.AluOpType
ACT = mybir.ActivationFunctionType
AX = mybir.AxisListType

P = 128
B, T, D = 32, 256, 128
TOKENS = B * T
TILES = TOKENS // P
H, DK = 16, 8
HG = 64
E = 8
EA = E + 1
INTER = 512
KI = INTER // P
CAP = TOKENS // E
R1 = 32
NS = 64
GROUP = 4
GROUPS = TILES // GROUP
GN = GROUP * P
STACK = 4 * DK
VW = 32
PAIRS = H // 2
LOW = 16
CH = 16
KPAD = P + T
WCOLS = 32
LOT = 256
LOTS = (2 * TOKENS // LOT + E, TOKENS // LOT)
UNROLL = 4
PACK = INTER + KI * D + KI
ROW_ID, ROW_DW, ROW_W2, ROW_E1 = D, D + 1, D + 2, D + 3
ROW = D + 4
TINY = 1e-24
NEWTON = 3
ROOT_STEPS = 4 + 3 * NEWTON
EPS = 1e-5
EPS_NW = 1e-12

C_ID, C_TRI, C_JREV, C_LAG, C_MASK = 0, 128, 256, 264, 296
C_COUNT = C_MASK + 128
C_TOKEN = C_COUNT + 72
C_TABLE1 = C_TOKEN + 64
C_END = C_TABLE1 + 32
R_BQKV, R_BOUT, R_GAMMA, R_BETA = 0, 384, 640, 768
R_END = 896


class Chain:

    def __init__(self, engine, sem, first=0):
        self.engine, self.sem, self.first, self.n = engine, sem, first, 0

    def did(self, instruction):
        instruction.then_inc(self.sem, 1)
        self.n += 1

    def settle(self):
        self.engine.wait_ge(self.sem, self.first + self.n)

    def link(self, instruction):
        self.did(instruction)
        self.settle()


@contextmanager
def stage(nc, prefix, names):
    sems = {n: nc.alloc_semaphore(prefix + n) for n in names}
    with nc.Block() as block:
        yield sems, block
    nc.clear_and_free_semaphores(list(sems.values()))
    nc.all_engine_barrier()


def wait_from(engine, sem, value):
    if isinstance(value, int) and value <= 0:
        return
    engine.wait_ge(sem, value)


def staggered(engine, steps, count=GROUPS, buffers=2):
    peeled = 4
    for i in range(peeled):
        for step, lag in steps:
            if i >= lag:
                step(i - lag, (i - lag) % buffers)
    with engine.Fori(0, (count - peeled) // buffers) as r:
        for u in range(buffers):
            for step, lag in steps:
                step(r * buffers + (u + peeled - lag), (u - lag) % buffers)
    for i in range(count, count + max(lag for _, lag in steps)):
        for step, lag in steps:
            if i - lag < count:
                step(i - lag, (i - lag) % buffers)


def build(nc, a, out):
    with ExitStack() as ctx:
        def sb(name, shape, dt=F32):
            return ctx.enter_context(nc.sbuf_tensor(name, shape, dt))

        ps = ctx.enter_context(nc.psum_tensor("ps", [P, 8, 512], F32))
        stream = sb("stream", [P, TILES, D])
        xT = sb("xT", [P, TOKENS])
        cst = sb("cst", [P, C_END])
        rows = sb("rows", [P, R_END])
        ident16 = sb("ident16", [P, P], F16)
        weights = sb("weights", [P, TILES, WCOLS])
        power = sb("power", [P, 4 * H])
        post = sb("post", [P, 1])
        rowbuf = sb("rowbuf", [P, TILES, ROW])
        slots = sb("slots", [P, 2, TILES], mybir.dt.int32)
        table = sb("table", [P, LOTS[0]])
        table_int = sb("table_int", [P, LOTS[0]], mybir.dt.int32)
        slot_dram = [nc.dram_tensor(f"slots{i}", [(LOTS[i] * LOT + i * TOKENS), ROW], F32).ap() for i in range(2)]
        y_dram = [nc.dram_tensor(f"y{i}", [3 * TOKENS + LOTS[i] * LOT, D], F32).ap() for i in range(2)]
        kernel_dram = nc.dram_tensor("conv_kernel", [P, KPAD], F32).ap()
        ident = cst[:, C_ID:C_ID + P]
        m = dict(ps=ps, stream=stream, xT=xT, cst=cst, rows=rows, ident=ident, ident16=ident16,
                 weights=weights, power=power, post=post, kernel_dram=kernel_dram, rowbuf=rowbuf, slots=slots, table=table, table_int=table_int,
                 slot_dram=slot_dram, y_dram=y_dram, xn=rowbuf[:, :, 0:D])

        load_all(nc, a, m)
        conv_kernel(nc, a, m)
        with ExitStack() as layer:
            m["hsum"] = layer.enter_context(nc.sbuf_tensor("hsum", [HG, B], F32))
            m["gate"] = layer.enter_context(nc.sbuf_tensor("gate", [P, B], F32))
            norm_and_router(nc, a, m)
            top2(nc, a, m)
            attention(nc, a, m)
        grouped(nc, a, m, 0)
        shared(nc, a, m, 0)
        convolve(nc, a, m)
        glu_and_norm(nc, a, m)
        norm_and_gate1(nc, a, m)
        top1(nc, a, m)
        scatter1(nc, m)
        grouped(nc, a, m, 1)
        shared(nc, a, m, 1, out.rearrange("(t p) d -> p t d", p=P))


def load_all(nc, a, m):
    with nc.semaphore("loaded") as loaded, nc.Block() as block:
        @block.sync
        def _(sp):
            sp.dma_start(m["cst"][:, :], a["cst"]).then_inc(loaded, 16)
            sp.dma_start(m["rows"][:, :], a["rows"]).then_inc(loaded, 16)
            sp.dma_start(m["stream"][:, :, :], a["x"].rearrange("(t p) d -> p t d", p=P)).then_inc(loaded, 16)
            sp.wait_ge(loaded, 48)

        @block.vector
        def _(dve):
            dve.wait_ge(loaded, 48)
            dve.tensor_copy(m["ident16"][:, :], m["ident"])
            dve.memset(m["power"][:, :], -0.5)


def conv_kernel(nc, a, m):
    ps, cst, ident = m["ps"], m["cst"], m["ident"]
    MAGIC = 1.5 * 2.0 ** 23
    TWO_PI = 2 * np.pi
    C1 = 6.28125
    C2 = float(np.float32(np.round((TWO_PI - C1) * 2 ** 20) / 2 ** 20))
    C3 = float(np.float32(TWO_PI - C1 - C2))
    L2 = 2 * LOW
    with ExitStack() as ctx:
        def sb(name, shape, dt=F32):
            return ctx.enter_context(nc.sbuf_tensor(name, shape, dt))

        s4 = sb("s4", [P, 4 * NS + 2])
        small = sb("small", [P, 16, NS])
        big = [sb(f"big{i}", [P, L2, NS]) for i in range(5)]
        pair = sb("pair", [P, L2, 2, NS])
        pairT = sb("pairT", [P, 2, D, LOW])
        dcol = sb("dcol", [P, 8, LOW])
        pick = sb("pick", [P, LOW, 8, LOW])
        masked = sb("masked", [P, LOW, P])
        taps = sb("taps", [P, LOW, LOW])
        zero = sb("zero", [P, P])
        dt1 = sb("dt1", [P, 1])
        sem, block = ctx.enter_context(stage(nc, "k_",
            ("loaded", "dt", "args", "expo", "sine", "pair", "turned", "copied", "product", "taps",
                "zeroed", "stored", "chain")))
        are, aim, cre, cim = (s4[:, NS * i:NS * (i + 1)] for i in range(4))
        log_dt, skip = s4[:, 4 * NS:4 * NS + 1], s4[:, 4 * NS + 1:4 * NS + 2]
        phase, decay, turns, cosine, scratch = big
        lag = cst[:, C_LAG:C_LAG + L2].unsqueeze(2).broadcast_to([P, L2, NS])

        @block.sync
        def _(sp):
            sp.dma_start(s4[:, :], a["s4"]).then_inc(sem["loaded"], 16)
            sp.wait_ge(sem["zeroed"], 1)
            sp.dma_start(m["kernel_dram"][:, T:KPAD], zero[:, :]).then_inc(sem["stored"], 16)
            sp.wait_ge(sem["taps"], 1)
            for g in range(LOW):
                sp.dma_start(m["kernel_dram"][8 * g:8 * g + 8, 0:T].rearrange("h (i j) -> h i j", j=LOW),
                             taps[:, g, :]).then_inc(sem["stored"], 16)
            sp.wait_ge(sem["stored"], 16 * (1 + LOW))

        @block.scalar
        def _(act):
            act.wait_ge(sem["loaded"], 16)
            act.activation(dt1[:, :], log_dt, ACT.Exp).then_inc(sem["dt"], 1)
            act.wait_ge(sem["args"], 1)
            act.activation(decay[:, :, :], decay[:, :, :], ACT.Exp).then_inc(sem["expo"], 1)
            act.wait_ge(sem["args"], 2)
            act.activation(phase[:, :, :], phase[:, :, :], ACT.Sin)
            act.activation(cosine[:, :, :], cosine[:, :, :], ACT.Sin).then_inc(sem["sine"], 1)
            for q in range(L2 // 4):
                act.wait_ge(sem["turned"], q + 1)
                k = 4 * q % LOW
                act.copy(pairT[:, 4 * q // LOW, :, k:k + 4].rearrange("p h l -> p l h"),
                         ps[:, q % 2, :].rearrange("p (l h) -> p l h", l=4)).then_inc(sem["copied"], 1)

        @block.vector
        def _(dve):
            c = Chain(dve, sem["chain"])
            tt, ts = dve.tensor_tensor, dve.tensor_scalar
            dve.memset(zero[:, :], 0.0).then_inc(sem["zeroed"], 1)
            c.did(dve.memset(pick[:, :, :, :], 0.0))
            c.link(dve.memset(dcol[:, :, :], 0.0))
            c.did(dve.tensor_copy(pick[:, :, :, LOW - 1], ident.rearrange("p (g h) -> p g h", g=LOW)))
            dve.wait_ge(sem["dt"], 1)
            c.did(dve.tensor_copy(dcol[:, :, LOW - 1], skip.broadcast_to([P, 8])))
            dre, dim = small[:, 0, :], small[:, 1, :]
            c.did(ts(dre, are, dt1[:, :], None, ALU.mult))
            c.link(ts(dim, aim, dt1[:, :], None, ALU.mult))
            tt(decay[:, :, :], dre.unsqueeze(1).broadcast_to([P, L2, NS]), lag, ALU.mult).then_inc(sem["args"], 1)
            c.link(tt(phase[:, :, :], dim.unsqueeze(1).broadcast_to([P, L2, NS]), lag, ALU.mult))
            c.link(ts(turns[:, :, :], phase[:, :, :], 1 / TWO_PI, MAGIC, ALU.mult, ALU.add))
            c.link(ts(turns[:, :, :], turns[:, :, :], -MAGIC, None, ALU.add))
            for part in (C1, C2, C3):
                c.link(dve.scalar_tensor_tensor(phase[:, :, :], turns[:, :, :], -part, phase[:, :, :],
                                                ALU.mult, ALU.add))
            c.link(ts(scratch[:, :, :], phase[:, :, :], np.pi / 2, -TWO_PI, ALU.is_gt, ALU.mult))
            c.link(dve.scalar_tensor_tensor(cosine[:, :, :], phase[:, :, :], np.pi / 2, scratch[:, :, :],
                                            ALU.add, ALU.add))
            edge = float(np.nextafter(np.float32(np.pi), np.float32(0)))
            c.did(ts(cosine[:, :, :], cosine[:, :, :], edge, -edge, ALU.min, ALU.max))
            ts(phase[:, :, :], phase[:, :, :], edge, -edge, ALU.min, ALU.max).then_inc(sem["args"], 1)
            dve.wait_ge(sem["expo"], 1)
            dve.wait_ge(sem["sine"], 1)
            er, ei = cosine, phase
            c.did(tt(er[:, :, :], cosine[:, :, :], decay[:, :, :], ALU.mult))
            c.link(tt(ei[:, :, :], phase[:, :, :], decay[:, :, :], ALU.mult))
            s = lambda i: small[:, i, :]
            c.did(ts(s(2), er[:, LOW - 2, :], -1.0, None, ALU.add))
            c.did(tt(s(3), are, are, ALU.mult))
            c.did(tt(s(4), aim, aim, ALU.mult))
            c.link(dve.tensor_copy(s(5), ei[:, LOW - 2, :]))
            c.did(tt(s(3), s(3), s(4), ALU.add))
            c.did(tt(s(6), s(2), are, ALU.mult))
            c.did(tt(s(7), s(5), aim, ALU.mult))
            c.did(tt(s(8), s(5), are, ALU.mult))
            c.link(tt(s(9), s(2), aim, ALU.mult))
            c.did(dve.reciprocal(s(3), s(3)))
            c.did(tt(s(6), s(6), s(7), ALU.add))
            c.link(tt(s(8), s(8), s(9), ALU.subtract))
            c.did(tt(s(6), s(6), s(3), ALU.mult))
            c.link(tt(s(8), s(8), s(3), ALU.mult))
            c.did(tt(s(9), cre, s(6), ALU.mult))
            c.did(tt(s(10), cim, s(8), ALU.mult))
            c.did(tt(s(11), cre, s(8), ALU.mult))
            c.link(tt(s(12), cim, s(6), ALU.mult))
            c.did(tt(s(9), s(9), s(10), ALU.subtract))
            c.link(tt(s(11), s(11), s(12), ALU.add))
            ctr = s(9).unsqueeze(1).broadcast_to([P, LOW, NS])
            cti = s(11).unsqueeze(1).broadcast_to([P, LOW, NS])
            lo, hi = slice(0, LOW), slice(LOW, L2)
            c.did(dve.tensor_copy(pair[:, lo, 0, :], er[:, lo, :]))
            c.did(dve.tensor_copy(pair[:, lo, 1, :], ei[:, lo, :]))
            c.did(tt(decay[:, lo, :], er[:, hi, :], ctr, ALU.mult))
            c.did(tt(decay[:, hi, :], ei[:, hi, :], cti, ALU.mult))
            c.did(tt(turns[:, lo, :], er[:, hi, :], cti, ALU.mult))
            c.link(tt(turns[:, hi, :], ei[:, hi, :], ctr, ALU.mult))
            c.did(tt(decay[:, lo, :], decay[:, lo, :], decay[:, hi, :], ALU.subtract))
            c.link(tt(turns[:, lo, :], turns[:, lo, :], turns[:, hi, :], ALU.add))
            c.did(ts(pair[:, hi, 0, :], decay[:, lo, :], 2.0, None, ALU.mult))
            c.link(ts(pair[:, hi, 1, :], turns[:, lo, :], -2.0, None, ALU.mult))
            dve.engine_nop().then_inc(sem["pair"], 1)
            dve.wait_ge(sem["product"], 1)
            mask = cst[:, C_MASK:C_MASK + P].unsqueeze(1).broadcast_to([P, LOW, P])
            c.link(tt(masked[:, :, :], ps[:, 4:8, :].rearrange("p k (g c) -> p (k g) c", c=P), mask, ALU.mult))
            dve.tensor_reduce(taps[:, :, :], masked[:, :, :].rearrange("p g (h j) -> p g j h", j=LOW),
                              AX.X, ALU.add).then_inc(sem["taps"], 1)

        @block.tensor
        def _(pe):
            pe.wait_ge(sem["pair"], 1)
            for q in range(L2 // 4):
                if q >= 2:
                    pe.wait_ge(sem["copied"], q - 1)
                for k in range(4):
                    ins = pe.transpose(ps[:, q % 2, P * k:P * k + P],
                                       pair[:, 4 * q + k, :, :].rearrange("p c n -> p (c n)"), ident)
                ins.then_inc(sem["turned"], 1)
            pe.wait_ge(sem["copied"], L2 // 4)
            for g in range(LOW):
                bank = ps[:, 4 + g // 4, P * (g % 4):P * (g % 4) + P]
                lo, hi = (pairT[:, part, 8 * g:8 * g + 8, :].rearrange("p h i -> p (h i)") for part in range(2))
                pe.matmul(bank, hi, lo, start=True, stop=False)
                ins = pe.matmul(bank, pick[:, g, :, :].rearrange("p h i -> p (h i)"),
                                dcol[:, :, :].rearrange("p h j -> p (h j)"), start=False, stop=True)
            ins.then_inc(sem["product"], 1)


def norm_and_router(nc, a, m):
    ps, stream, xT, ident = m["ps"], m["stream"], m["xT"], m["ident"]
    with ExitStack() as ctx:
        def sb(name, shape, dt=F32):
            return ctx.enter_context(nc.sbuf_tensor(name, shape, dt))

        w = sb("w_router", [P, R1 + HG])
        wr2 = sb("wr2", [R1 + 1, E])
        bias = sb("b_router", [HG, 2])
        stats = sb("stats", [P, 2, GROUP, 6])
        mv = sb("mv", [P, 2, GROUP, 2])
        rstd = sb("rstd", [P, 2, GROUP])
        xn = sb("xn", [P, 2, GROUP, D])
        hidden = sb("hidden", [R1 + 1, 2, GN])
        junk = sb("junk", [HG, 4, T])
        blank = sb("blank", [P, 2, 16, ROW])
        sem, block = ctx.enter_context(stage(nc, "n_",
            ("loaded", "ones", "cleaned", "zeroed", "cleared", "numbered", "blanked0", "blanked1", "kept", "xn_ready", "turned", "xT_ready", "hidden_ready", "relu_ready", "gelu_done",
                "logits_ready", "logits_copied", "stats", "moments", "raised", "rstd")))

        chunks = [(i, k) for i in range(2) for k in range(LOTS[i] * LOT // (16 * P))]

        @block.sync
        def _(sp):
            sp.dma_start(w[:, :], a["w_router"]).then_inc(sem["loaded"], 16)
            sp.dma_start(wr2[:, :], a["wr2"]).then_inc(sem["loaded"], 16)
            sp.dma_start(bias[:, :], a["b_router"]).then_inc(sem["loaded"], 16)
            sp.wait_ge(sem["zeroed"], 1)
            for k in range(TOKENS // (16 * P)):
                sp.dma_start(m["y_dram"][1][16 * P * k:16 * P * (k + 1), :].rearrange("(p j) d -> p j d", p=P),
                             blank[:, 0, :, 0:D]).then_inc(sem["cleared"], 16)
            for n, (i, k) in enumerate(chunks):
                sp.wait_ge(sem["numbered"], n + 1)
                sp.dma_start(m["slot_dram"][i][16 * P * k:16 * P * (k + 1), :].rearrange("(p j) d -> p j d", p=P),
                             blank[:, n % 2, :, :]).then_inc(sem[f"blanked{n % 2}"], 16)
            sp.wait_ge(sem["cleared"], 16 * (TOKENS // (16 * P)))
            for u in range(2):
                sp.wait_ge(sem[f"blanked{u}"], 16 * len(chunks[u::2]))

        @block.gpsimd
        def _(pool):
            pool.wait_ge(sem["zeroed"], 1)
            for n, (i, k) in enumerate(chunks):
                if n >= 2:
                    pool.wait_ge(sem[f"blanked{n % 2}"], 16 * (n // 2))
                pool.iota(blank[:, n % 2, :, ROW_ID], pattern=[[1, 16]], base=2 * TOKENS + 16 * P * k,
                          channel_multiplier=16, allow_small_or_imprecise_dtypes=True).then_inc(sem["numbered"], 1)

            def root(g, u):
                inverse_root(pool, sem, g, rstd[:, u], m["power"])

            def keep(g, u):
                pool.wait_ge(sem["xn_ready"], g + 1)
                pool.tensor_copy(m["xn"][:, bass.ds(g * GROUP, GROUP), :], xn[:, u, :, :])\
                    .then_inc(sem["kept"], 1)

            staggered(pool, [(root, 0), (keep, 1)])

        @block.vector
        def _(dve):
            dve.memset(hidden[R1:R1 + 1, :, :], 1.0).then_inc(sem["ones"], 1)
            dve.memset(blank[:, :, :, :], 0.0).then_inc(sem["cleaned"], 1)
            dve.wait_ge(sem["cleaned"], 1)
            dve.memset(blank[:, :, :, ROW_E1:ROW], -1.0).then_inc(sem["zeroed"], 1)

            def measure(g, u):
                moments(dve, sem, g, stream, g * GROUP, stats[:, u], mv[:, u], rstd[:, u], m["post"], EPS)

            def normalise(g, u):
                dve.wait_ge(sem["rstd"], g + 1)
                wait_from(dve, sem["turned"], g - 1)
                wait_from(dve, sem["kept"], g - 1)
                for k in range(GROUP):
                    ins = dve.tensor_scalar(xn[:, u, k, :], tile_of(stream, g * GROUP + k),
                                            mv[:, u, k, 0:1], rstd[:, u, k:k + 1], ALU.subtract, ALU.mult)
                ins.then_inc(sem["xn_ready"], 1)

            def take_logits(g, u):
                dve.wait_ge(sem["logits_ready"], g + 1)
                dve.tensor_copy(m["weights"][:, bass.ds(g * GROUP, GROUP), 0:E],
                                ps[:, 6 + u, 0:GROUP * E].rearrange("p (k e) -> p k e", e=E))\
                   .then_inc(sem["logits_copied"], 1)

            staggered(dve, [(measure, 0), (normalise, 1), (take_logits, 4)])

        @block.tensor
        def _(pe):
            pe.wait_ge(sem["loaded"], 48)
            pe.wait_ge(sem["ones"], 1)

            def turn(g, u):
                pe.wait_ge(sem["xn_ready"], g + 1)
                wait_from(pe, sem["xT_ready"], g - 1)
                for k in range(GROUP):
                    ins = pe.transpose(ps[:, u, P * k:P * k + P], xn[:, u, k, :], ident)
                ins.then_inc(sem["turned"], 1)

            def make_hidden(g, u):
                pe.wait_ge(sem["xT_ready"], g + 1)
                wait_from(pe, sem["gelu_done"], g - 1)
                xg = xT[:, bass.ds(g * GN, GN)]
                pe.matmul(ps[0:R1, 2 + u, :], w[:, 0:R1], xg, start=True, stop=True)
                pe.matmul(ps[0:HG, 4 + u, :], w[:, R1:R1 + HG], xg, start=True, stop=True)\
                  .then_inc(sem["hidden_ready"], 1)

            def make_logits(g, u):
                pe.wait_ge(sem["relu_ready"], g + 1)
                wait_from(pe, sem["logits_copied"], g - 1)
                for k in range(GROUP):
                    ins = pe.matmul(ps[:, 6 + u, E * k:E * k + E], hidden[:, u, P * k:P * k + P], wr2[:, :],
                                    start=True, stop=True)
                ins.then_inc(sem["logits_ready"], 1)

            staggered(pe, [(turn, 0), (make_hidden, 1), (make_logits, 2)])

        @block.scalar
        def _(act):
            act.wait_ge(sem["loaded"], 48)

            def take_xT(g, u):
                act.wait_ge(sem["turned"], g + 1)
                act.copy(xT[:, bass.ds(g * GN, GN)], ps[:, u, :]).then_inc(sem["xT_ready"], 1)

            def activate(g, u):
                act.wait_ge(sem["hidden_ready"], g + 1)
                wait_from(act, sem["logits_ready"], g - 1)
                act.activation(hidden[0:R1, u, :], ps[0:R1, 2 + u, :], ACT.Relu, bias=bias[0:R1, 0:1])\
                   .then_inc(sem["relu_ready"], 1)
                for j in range(2):
                    ins = act.activation(junk[:, 2 * u + j, :], ps[0:HG, 4 + u, T * j:T * j + T], ACT.Gelu,
                                         bias=bias[:, 1:2],
                                         accum_out=m["hsum"][:, bass.ds(g * 2 + j, 1)])
                ins.then_inc(sem["gelu_done"], 1)

            staggered(act, [(take_xT, 0), (activate, 1)])


def first_of(c, dve, mask, value, best, tmp, jrev):
    wide = lambda t: t.unsqueeze(2).broadcast_to([P, TILES, E])
    c.link(dve.tensor_reduce(best[:, :], value[:, :, :], AX.X, ALU.max))
    c.link(dve.tensor_tensor(mask[:, :, :], value[:, :, :], wide(best[:, :]), ALU.is_equal))
    c.link(dve.tensor_tensor(mask[:, :, :], mask[:, :, :], jrev, ALU.mult))
    c.link(dve.tensor_reduce(tmp[:, :], mask[:, :, :], AX.X, ALU.max))
    c.link(dve.tensor_tensor(mask[:, :, :], jrev, wide(tmp[:, :]), ALU.is_equal))


def softmax_parts(c, dve, act_done, args_ready, logits, top, z, total):
    wide = lambda t: t.unsqueeze(2).broadcast_to(list(z.shape))
    c.link(dve.tensor_reduce(top[:, :], logits, AX.X, ALU.max))
    dve.tensor_tensor(z[:, :, :], logits, wide(top[:, :]), ALU.subtract).then_inc(args_ready, 1)
    dve.wait_ge(act_done[0], act_done[1])
    c.link(dve.tensor_reduce(total[:, :], z[:, :, :], AX.X, ALU.add))
    c.link(dve.reciprocal(total[:, :], total[:, :]))
    c.link(dve.tensor_tensor(z[:, :, :], z[:, :, :], wide(total[:, :]), ALU.mult))


def top2(nc, a, m):
    ps, cst, weights = m["ps"], m["cst"], m["weights"]
    with ExitStack() as ctx:
        def sb(name, shape, dt=F32):
            return ctx.enter_context(nc.sbuf_tensor(name, shape, dt))

        z = sb("z", [P, TILES, E])
        mask1, mask2 = sb("mask1", [P, TILES, E]), sb("mask2", [P, TILES, E])
        v = [sb(f"v{i}", [P, TILES]) for i in range(5)]
        wg2 = sb("wg2", [HG, P])
        gb = sb("gb", [P, 2])
        gs = sb("gs", [P, 1])
        ones = sb("ones2", [P, P])
        chosen, place = sb("chosen", [P, TILES, E]), sb("place2", [P, TILES, E])
        before = sb("before2", [P, E, TILES])
        lots = sb("lots", [P, 4, E])
        reached = sb("reached", [P, LOTS[0], E])
        sem, block = ctx.enter_context(stage(nc, "t_",
            ("loaded", "args", "expo", "gate", "gated", "mask", "counts", "chain")))
        jrev = cst[:, C_JREV:C_JREV + E].unsqueeze(1).broadcast_to([P, TILES, E])
        wide = lambda t: t.unsqueeze(2).broadcast_to([P, TILES, E])

        @block.sync
        def _(sp):
            sp.dma_start(wg2[:, :], a["wg2"]).then_inc(sem["loaded"], 16)
            sp.dma_start(gb[:, :], a["gate_bias"]).then_inc(sem["loaded"], 16)

        @block.tensor
        def _(pe):
            pe.wait_ge(sem["loaded"], 32)
            pe.matmul(ps[:, 0, 0:B], wg2[:, :], m["hsum"][:, :], start=True, stop=True).then_inc(sem["gate"], 1)
            count(pe, m, sem, chosen, ones)

        @block.scalar
        def _(act):
            act.wait_ge(sem["loaded"], 32)
            act.wait_ge(sem["gate"], 1)
            act.activation(m["gate"][:, :], ps[:, 0, 0:B], ACT.Sigmoid, bias=gb[:, 0:1], scale=1.0 / T)
            act.activation(gs[:, :], gb[:, 1:2], ACT.Sigmoid).then_inc(sem["gated"], 1)
            act.wait_ge(sem["args"], 1)
            act.activation(z[:, :, :], z[:, :, :], ACT.Exp).then_inc(sem["expo"], 1)
            act.wait_ge(sem["args"], 2)
            act.activation(v[2][:, :], v[2][:, :], ACT.Exp, scale=0.5).then_inc(sem["expo"], 1)

        @block.vector
        def _(dve):
            c = Chain(dve, sem["chain"])
            tt, ts = dve.tensor_tensor, dve.tensor_scalar
            dve.wait_ge(sem["gated"], 1)
            c.did(ts(m["gate"][:, :], m["gate"][:, :], gs[:, :], None, ALU.mult))
            softmax_parts(c, dve, (sem["expo"], 1), sem["args"], weights[:, :, 0:E], v[0], z, v[1])
            c.did(dve.memset(ones[:, :], 1.0))
            first_of(c, dve, mask1, z, v[0], v[4], jrev)
            c.did(ts(m["rowbuf"][:, :, ROW_E1], v[4][:, :], -1.0, float(E), ALU.mult, ALU.add))
            c.link(dve.scalar_tensor_tensor(z[:, :, :], mask1[:, :, :], -2.0, z[:, :, :], ALU.mult, ALU.add))
            first_of(c, dve, mask2, z, v[1], v[4], jrev)
            tt(chosen[:, :, :], mask1[:, :, :], mask2[:, :, :], ALU.add).then_inc(sem["mask"], 1)
            tt(v[2][:, :], v[1][:, :], v[0][:, :], ALU.subtract).then_inc(sem["args"], 1)
            dve.wait_ge(sem["expo"], 2)
            c.link(ts(v[3][:, :], v[2][:, :], 1.0, None, ALU.add))
            c.link(dve.reciprocal(v[3][:, :], v[3][:, :]))
            c.link(tt(v[2][:, :], v[2][:, :], v[3][:, :], ALU.mult))
            c.did(tt(m["rowbuf"][:, :, ROW_DW], v[3][:, :], v[2][:, :], ALU.subtract))
            c.did(dve.tensor_copy(m["rowbuf"][:, :, ROW_W2], v[2][:, :]))
            token = cst[:, C_TOKEN:C_TOKEN + TILES]
            c.did(ts(m["rowbuf"][:, :, ROW_ID], token, float(TOKENS), None, ALU.add))
            dve.wait_ge(sem["counts"], 1)
            places(c, dve, ps, ones, before, place, lots[:, 0, :])
            size, end, start, tmp = (lots[:, k, :] for k in range(4))
            c.link(ts(tmp, size, 1.0 / LOT, 0.5 - 0.5 / LOT, ALU.mult, ALU.add))
            c.link(ts(tmp, tmp, 1.5 * 2.0 ** 23, None, ALU.add))
            c.link(ts(tmp, tmp, -1.5 * 2.0 ** 23, None, ALU.add))
            c.link(dve.tensor_tensor_scan(end, ones[:, 0:E], tmp, 0.0, ALU.mult, ALU.add))
            c.link(tt(start, end, tmp, ALU.subtract))
            c.link(dve.scalar_tensor_tensor(place[:, :, :], start.unsqueeze(1).broadcast_to([P, TILES, E]),
                                            float(LOT), place[:, :, :], ALU.mult, ALU.add))
            for choice, mask in enumerate((mask1, mask2)):
                c.link(tt(z[:, :, :], mask[:, :, :], place[:, :, :], ALU.mult))
                c.link(dve.tensor_reduce(v[4][:, :], z[:, :, :], AX.X, ALU.add))
                c.link(dve.tensor_copy(m["slots"][:, choice, :], v[4][:, :]))
            n = LOTS[0]
            c.link(tt(reached[:, :, :], cst[:, C_COUNT:C_COUNT + n].unsqueeze(2).broadcast_to([P, n, E]),
                      end.unsqueeze(1).broadcast_to([P, n, E]), ALU.is_ge))
            c.link(dve.tensor_reduce(m["table"][:, :], reached[:, :, :], AX.X, ALU.add))
            c.link(ts(m["table"][:, :], m["table"][:, :], float(E - 1), None, ALU.min))
            c.did(dve.tensor_copy(m["table_int"][:, :], m["table"][:, :]))
            c.did(tt(mask1[:, :, :], mask1[:, :, :], wide(v[3][:, :]), ALU.mult))
            c.link(tt(mask2[:, :, :], mask2[:, :, :], wide(v[2][:, :]), ALU.mult))
            tt(weights[:, :, 0:E], mask1[:, :, :], mask2[:, :, :], ALU.add)
            dve.memset(weights[:, :, E:E + 2], 1.0)
            dve.memset(weights[:, :, E + 2:WCOLS], 0.0)


def attention(nc, a, m):
    ps, stream, xT, ident, ident16 = m["ps"], m["stream"], m["xT"], m["ident"], m["ident16"]
    with ExitStack() as ctx:
        def sb(name, shape, dt=F32):
            return ctx.enter_context(nc.sbuf_tensor(name, shape, dt))

        wqkv = sb("wqkv", [P, 3 * D])
        wo = sb("wo", [D, D])
        xs = sb("xs", [P, T])
        qk = sb("qk", [P, 2, 2 * D])
        sq = sb("sq", [P, 2, 2 * D])
        rn, guess, root = sb("rn", [P, 4 * H]), sb("guess", [P, 4 * H]), sb("root", [P, 4 * H])
        stack = [sb("q_stack", [P, 2 * H, 4, DK], F16), sb("k_stack", [P, 2 * H, 4, DK], F16)]
        stackT = [sb("q_stackT", [P, 2, 4, T], F16), sb("k_stackT", [P, 2, 4, T], F16)]
        vext = sb("vext", [P, 2, 2, H, VW])
        probs = sb("probs", [P, 2, 2, 2, T])
        oT = sb("oT", [P, 4, T])
        rsum = sb("rsum", [P, 2, H])
        on = sb("on", [P, 2, D])
        onT = sb("onT", [P, T])
        sem, block = ctx.enter_context(stage(nc, "a_",
            ("loaded", "v_zero", "v_ready", "xs_ready", "projected", "qkv_ready", "squared", "summed", "norms", "highs", "normal", "turned",
                "stacked", "rsum", "stackT_ready", "scores", "probs", "pv", "oT_ready", "out_turned", "on_ready",
                "on_turned", "onT_ready", "mixed", "added", "scattered")))
        xb = ps[:, 4:6, :]

        def take_stack(copy, which, par):
            copy(stackT[which][:, par, :, :], xb[:, which, :].bitcast(F16).rearrange("p (g t) -> p g t", t=T))\
                .then_inc(sem["stackT_ready"], 1)

        def over_batches(engine, body):
            body(0, 0)
            with engine.Fori(0, B // 2 - 1) as i:
                body(i * 2 + 1, 1)
                body(i * 2 + 2, 0)
            body(B - 1, 1)

        is_last = lambda b: isinstance(b, int) and b == B - 1

        @block.sync
        def _(sp):
            sp.dma_start(wqkv[:, :], a["wqkv"]).then_inc(sem["loaded"], 16)
            sp.dma_start(wo[:, :], a["wo"]).then_inc(sem["loaded"], 16)

        @block.tensor
        def _(pe):
            def project(b):
                pe.wait_ge(sem["xs_ready"], b + 1)
                for t in range(2):
                    ins = pe.matmul(xb[:, t, 0:3 * D], xs[:, P * t:P * t + P], wqkv[:, :], start=True, stop=True)
                ins.then_inc(sem["projected"], 1)

            def turn_stacks(b):
                pe.wait_ge(sem["stacked"], b + 1)
                wait_from(pe, sem["added"], b - 1)
                for which in range(2):
                    bank = xb[:, which, :].bitcast(F16)
                    for g in range(4):
                        for t in range(2):
                            ins = pe.transpose(bank[:, g * T + t * P:g * T + t * P + P],
                                               stack[which][:, t * H + 4 * g:t * H + 4 * g + 4, :, :]
                                               .rearrange("p h s d -> p (h s d)"), ident16[:, :])
                ins.then_inc(sem["turned"], 1)

            def score(b, par, p):
                if p == 0:
                    pe.wait_ge(sem["stackT_ready"], 2 * b + 2)
                wait_from(pe, sem["probs"], b * PAIRS + p - 1)
                for kt in range(2):
                    for j in range(2):
                        g, r = divmod(2 * p + j, 4)
                        rows = slice(32 * r, 32 * r + 32)
                        ins = pe.matmul(ps[:, 2 * (p % 2) + j, kt * T:kt * T + T],
                                        stackT[1][rows, par, g, kt * P:kt * P + P],
                                        stackT[0][rows, par, g, :], start=True, stop=True,
                                        tile_position=(32 * r, 0))
                ins.then_inc(sem["scores"], 1)

            def weigh(b, par, p):
                pe.wait_ge(sem["probs"], b * PAIRS + p + 1)
                if p % 4 == 0:
                    wait_from(pe, sem["oT_ready"], 2 * b - 1 + p // 4)
                for kt in range(2):
                    for j in range(2):
                        g, r = divmod(2 * p + j, 4)
                        ins = pe.matmul(ps[32 * r:32 * r + 32, 6 + g // 2, (g % 2) * T:(g % 2) * T + T],
                                        vext[:, par, kt, 2 * p + j, :], probs[:, p % 2, j, kt, :],
                                        start=(kt == 0), stop=(kt == 1), tile_position=(0, 32 * r),
                                        skip_group_check=True)
                ins.then_inc(sem["pv"], 1)

            def turn_out(b):
                pe.wait_ge(sem["oT_ready"], 2 * b + 2)
                if is_last(b):
                    pe.wait_ge(sem["added"], B - 1)
                elif not (isinstance(b, int) and b == B - 2):
                    pe.wait_ge(sem["qkv_ready"], b + 3)
                for t in range(2):
                    for g in range(4):
                        ins = pe.transpose(xb[:, t, P * g:P * g + P], oT[:, g, P * t:P * t + P], ident)
                ins.then_inc(sem["out_turned"], 1)

            def turn_normal(b):
                pe.wait_ge(sem["on_ready"], b + 1)
                for t in range(2):
                    ins = pe.transpose(xb[:, 0, P * t:P * t + P], on[:, t, :], ident)
                ins.then_inc(sem["on_turned"], 1)

            def mix(b):
                pe.wait_ge(sem["onT_ready"], b + 1)
                for t in range(2):
                    ins = pe.matmul(xb[:, 1, P * t:P * t + P], onT[:, P * t:P * t + P], wo[:, :],
                                    start=True, stop=True)
                ins.then_inc(sem["mixed"], 1)

            def body(b, par):
                first, last = isinstance(b, int) and b == 0, is_last(b)
                for p in range(PAIRS):
                    if p == 0 and not last:
                        project(b + 1)
                    if p + 1 < PAIRS:
                        score(b, par, p + 1)
                    elif not last:
                        score(b + 1, 1 - par, 0)
                    weigh(b, par, p)
                    if p == 0 and not first:
                        turn_out(b - 1)
                    if p == 3 and not first:
                        turn_normal(b - 1)
                    if p == 5 and not first:
                        mix(b - 1)
                    if p == 6 and not last:
                        turn_stacks(b + 1)

            pe.wait_ge(sem["loaded"], 32)
            pe.wait_ge(sem["v_ready"], 1)
            project(0)
            turn_stacks(0)
            score(0, 0, 0)
            over_batches(pe, body)
            turn_out(B - 1)
            turn_normal(B - 1)
            mix(B - 1)

        @block.scalar
        def _(act):
            def slice_x(b):
                wait_from(act, sem["projected"], b)
                act.copy(xs[:, :], xT[:, bass.ds(b * T, T)]).then_inc(sem["xs_ready"], 1)

            def take_k(b, par):
                act.wait_ge(sem["turned"], b + 1)
                take_stack(act.copy, 1, par)

            def body(b, par):
                for p in range(PAIRS):
                    if p == 0 and not is_last(b):
                        slice_x(b + 1)
                    if p == PAIRS - 1 and not is_last(b):
                        take_k(b + 1, 1 - par)
                    act.wait_ge(sem["scores"], b * PAIRS + p + 1)
                    wait_from(act, sem["pv"], b * PAIRS + p - 1)
                    act.activation(probs[:, p % 2, :, :, :].rearrange("p j k t -> p j (k t)"),
                                   ps[:, 2 * (p % 2):2 * (p % 2) + 2, :], ACT.Exp,
                                   scale=DK ** -0.5).then_inc(sem["probs"], 1)

            slice_x(0)
            take_k(0, 0)
            over_batches(act, body)

        @block.gpsimd
        def _(pool):
            def scatter(b):
                for t in range(2):
                    for choice in range(2):
                        scatter_tile(pool, m, 0, 2 * b + t, choice).then_inc(sem["scattered"], 16)

            for b in range(B):
                scatter(b)
            pool.wait_ge(sem["scattered"], 16 * 2 * TILES)

        @block.vector
        def _(dve):
            def take_qkv(b, par):
                dve.wait_ge(sem["projected"], b + 1)
                wait_from(dve, sem["pv"], (b - 1) * PAIRS)
                rows = m["rows"]
                wide = rows[:, R_BQKV:R_BQKV + 2 * D].unsqueeze(1).broadcast_to([P, 2, 2 * D])
                dve.tensor_tensor(qk[:, :, :], xb[:, :, 0:2 * D], wide, ALU.add)
                for t in range(2):
                    ins = dve.tensor_tensor(
                        vext[:, par, t, :, 0:DK],
                        xb[:, t, 2 * D:3 * D].rearrange("p (h d) -> p h d", d=DK),
                        rows[:, R_BQKV + 2 * D:R_BQKV + 3 * D].rearrange("p (h d) -> p h d", d=DK), ALU.add)
                ins.then_inc(sem["qkv_ready"], 1)

            def norms(b):
                dve.wait_ge(sem["qkv_ready"], b + 1)
                dve.tensor_tensor(sq[:, :, :], qk[:, :, :], qk[:, :, :], ALU.mult).then_inc(sem["squared"], 1)
                dve.wait_ge(sem["squared"], b + 1)
                dve.tensor_reduce(rn[:, :], sq[:, :, :].rearrange("p t (h d) -> p (t h) d", d=DK),
                                  AX.X, ALU.add).then_inc(sem["summed"], 1)

            def roots(b):
                dve.wait_ge(sem["summed"], b + 1)
                inverse_roots(Chain(dve, sem["norms"], b * ROOT_STEPS), rn, guess, root)

            def unit(b):
                dve.tensor_tensor(sq[:, :, :].rearrange("p t (h d) -> p (t h) d", d=DK),
                                  qk[:, :, :].rearrange("p t (h d) -> p (t h) d", d=DK),
                                  root[:, :].unsqueeze(2).broadcast_to([P, 4 * H, DK]),
                                  ALU.mult).then_inc(sem["normal"], 1)

            def split(b):
                dve.wait_ge(sem["normal"], b + 1)
                wait_from(dve, sem["turned"], b)
                highs = []
                for which, high in ((0, slice(0, 4, 2)), (1, slice(0, 4, 3))):
                    x3 = sq[:, :, :].rearrange("p t (w h d) -> p t w h d", w=2, d=DK)[:, :, which, :, :]
                    for t in range(2):
                        wide = x3[:, t].unsqueeze(2).broadcast_to([P, H, 2, DK])
                        highs.append((which, high, t, wide))
                for which, high, t, wide in highs:
                    ins = dve.tensor_copy(stack[which][:, t * H:t * H + H, high, :], wide)
                ins.then_inc(sem["highs"], 1)
                dve.wait_ge(sem["highs"], b + 1)
                for which, high, t, wide in highs:
                    low = slice(1, 4, 2) if which == 0 else slice(1, 3)
                    s = stack[which][:, t * H:t * H + H, :, :]
                    ins = dve.tensor_tensor(s[:, :, low, :], wide,
                                            s[:, :, 0:1, :].broadcast_to([P, H, 2, DK]), ALU.subtract)
                ins.then_inc(sem["stacked"], 1)

            def take_stacks(b, par):
                dve.wait_ge(sem["turned"], b + 1)
                take_stack(dve.tensor_copy, 0, par)


            def take_out(b, half):
                dve.wait_ge(sem["pv"], b * PAIRS + 4 * half + 4)
                wait_from(dve, sem["out_turned"], b)
                dve.tensor_copy(oT[:, 2 * half:2 * half + 2, :], ps[:, 6 + half, :].rearrange(
                    "p (g t) -> p g t", t=T)).then_inc(sem["oT_ready"], 1)

            def normalise(b):
                dve.wait_ge(sem["out_turned"], b + 1)
                o = xb[:, :, :].rearrange("p t (h e) -> p t h e", e=VW)
                dve.reciprocal(rsum[:, :, :], o[:, :, :, DK]).then_inc(sem["rsum"], 1)
                dve.wait_ge(sem["rsum"], b + 1)
                for t in range(2):
                    ins = dve.tensor_tensor(on[:, t, :].rearrange("p (h d) -> p h d", d=DK), o[:, t, :, 0:DK],
                                            rsum[:, t, :].unsqueeze(2).broadcast_to([P, H, DK]), ALU.mult)
                ins.then_inc(sem["on_ready"], 1)

            def gate(b):
                dve.wait_ge(sem["on_turned"], b + 1)
                dve.tensor_scalar(onT[:, :], xb[:, 0, 0:T], m["gate"][:, bass.ds(b, 1)], None, ALU.mult)\
                   .then_inc(sem["onT_ready"], 1)

            def add(b):
                dve.wait_ge(sem["mixed"], b + 1)
                s = stream[:, bass.ds(2 * b, 2), :]
                dve.tensor_tensor(s, s, xb[:, 1, 0:T].rearrange("p (t d) -> p t d", d=D), ALU.add)\
                   .then_inc(sem["added"], 1)

            def body(b, par):
                first = isinstance(b, int) and b == 0
                if not is_last(b):
                    take_qkv(b + 1, 1 - par)
                    norms(b + 1)
                if not first:
                    normalise(b - 1)
                if not is_last(b):
                    roots(b + 1)
                if not first:
                    gate(b - 1)
                if not is_last(b):
                    unit(b + 1)
                    split(b + 1)
                if not first:
                    add(b - 1)
                take_out(b, 0)
                if not is_last(b):
                    take_stacks(b + 1, 1 - par)
                take_out(b, 1)

            dve.memset(vext[:, :, :, :, :], 0.0).then_inc(sem["v_zero"], 1)
            dve.wait_ge(sem["v_zero"], 1)
            dve.memset(vext[:, :, :, :, DK:DK + 1], 1.0).then_inc(sem["v_ready"], 1)
            dve.wait_ge(sem["v_ready"], 1)
            take_qkv(0, 0)
            norms(0)
            roots(0)
            unit(0)
            split(0)
            take_stacks(0, 0)
            over_batches(dve, body)
            normalise(B - 1)
            gate(B - 1)
            add(B - 1)


def count(pe, m, sem, chosen, ones):
    pe.wait_ge(sem["mask"], 1)
    flat = chosen[:, :, :].rearrange("p t e -> p (t e)")
    pe.matmul(m["ps"][:, 1, :], m["cst"][:, C_TRI:C_TRI + P], flat, start=True, stop=True)
    pe.matmul(m["ps"][:, 2, :], ones[:, :], flat, start=True, stop=True).then_inc(sem["counts"], 1)


def places(c, dve, ps, ones, before, place, total):
    totals = ps[:, 2, :].rearrange("p (t e) -> p e t", e=E)
    for e in range(E):
        ins = dve.tensor_tensor_scan(before[:, e, :], ones[:, 0:TILES], totals[:, e, :], 0.0, ALU.mult, ALU.add)
    c.link(ins)
    c.link(dve.tensor_copy(total, before[:, :, TILES - 1]))
    c.link(dve.tensor_tensor(before[:, :, :], before[:, :, :], totals, ALU.subtract))
    c.link(dve.tensor_tensor(place[:, :, :], ps[:, 1, :].rearrange("p (t e) -> p t e", e=E),
                             before[:, :, :].rearrange("p e t -> p t e"), ALU.add))


def scatter_tile(pool, m, layer, tile, choice):
    where = m["slots"][:, choice, tile:tile + 1]
    return pool.indirect_dma_start(m["slot_dram"][layer], bass.IndirectOffsetOnAxis(ap=where, axis=0),
                                   m["rowbuf"][:, tile, :], None)


def scatter1(nc, m):
    with nc.semaphore("scattered1") as scattered, nc.Block() as block:
        @block.gpsimd
        def _(pool):
            for t in range(TILES):
                scatter_tile(pool, m, 1, t, 0).then_inc(scattered, 16)
            pool.wait_ge(scattered, 16 * TILES)


def grouped(nc, a, m, layer):
    ps, ident = m["ps"], m["ident"]
    lots = LOTS[layer]
    act_func = (ACT.Silu, ACT.Gelu_apprx_tanh)[layer]
    HALVES = LOT // P
    with ExitStack() as ctx:
        def sb(name, shape, dt=F32):
            return ctx.enter_context(nc.sbuf_tensor(f"{name}_{layer}", shape, dt))

        packs = sb("packs", [P, E, PACK])
        own = sb("own", [P, UNROLL, PACK])
        nwb = sb("nwb_g", [P, 2])
        rows = sb("slot_rows", [P, UNROLL, HALVES, ROW])
        xs = sb("slot_x", [P, 2, LOT])
        hidden = sb("slot_h", [P, 2, KI, LOT])
        first = sb("first", [P, UNROLL, HALVES])
        weight = sb("weight", [P, UNROLL, HALVES])
        where = sb("where", [P, UNROLL, HALVES], mybir.dt.int32)
        y = sb("slot_y", [P, UNROLL, HALVES, D])
        sem, block = ctx.enter_context(stage(nc, f"r{layer}_",
            ["loaded", "own_ready", "turned", "x_ready", "upped", "hidden_ready", "downed",
                "first_ready", "picked", "weight_ready", "y_ready", "y_seen", "y_free"]
               + [f"rows{j}" for j in range(UNROLL)] + [f"sent{j}" for j in range(UNROLL)]))
        slots = m["slot_dram"][layer][0:lots * LOT, :].rearrange("(t p j) d -> p t (j d)", p=P, j=HALVES)

        @block.sync
        def _(sp):
            sp.dma_start(packs[:, :, :], a[f"experts{layer}"][:, 0:E, :]).then_inc(sem["loaded"], 16)
            sp.dma_start(nwb[:, :], a["nwb"]).then_inc(sem["loaded"], 16)
            with sp.Fori(0, lots // UNROLL) as i:
                for j in range(UNROLL):
                    sp.wait_ge(sem["downed"], i * UNROLL + j + 1)
                    sp.wait_ge(sem["weight_ready"], i * UNROLL + j + 1)
                    sp.dma_start(rows[:, j, :, :].rearrange("p h d -> p (h d)"), slots[:, bass.ds(i * UNROLL + j, 1), :].rearrange(
                        "p t d -> p (t d)")).then_inc(sem[f"rows{j}"], 16)

        def rows_loaded(t, j):
            return t * (16 // UNROLL) + (16 - 16 // UNROLL * j)

        @block.vector
        def _(dve):
            def get_own(t, j):
                dve.wait_ge(sem["downed"], t + 1)
                e = dve.value_load(m["table_int"][0:1, bass.ds(t, 1)], min_val=0, max_val=E - 1)
                dve.tensor_copy(own[:, j, :], packs[:, bass.ds(e, 1), :].rearrange("p e n -> p (e n)"))\
                    .then_inc(sem["own_ready"], 1)
                dve.wait_ge(sem[f"rows{j}"], rows_loaded(t, j))
                dve.wait_ge(sem["y_free"], t + 1)
                dve.tensor_scalar(first[:, j, :], rows[:, j, :, ROW_E1], m["table"][:, bass.ds(t, 1)], None,
                                  ALU.is_equal).then_inc(sem["first_ready"], 1)
                dve.wait_ge(sem["first_ready"], t + 1)
                dve.scalar_tensor_tensor(where[:, j, :], first[:, j, :], -float(TOKENS), rows[:, j, :, ROW_ID],
                                         ALU.mult, ALU.add)
                dve.tensor_tensor(weight[:, j, :], first[:, j, :], rows[:, j, :, ROW_DW], ALU.mult)\
                    .then_inc(sem["picked"], 1)
                dve.wait_ge(sem["picked"], t + 1)
                dve.tensor_tensor(weight[:, j, :], weight[:, j, :], rows[:, j, :, ROW_W2], ALU.add)\
                    .then_inc(sem["weight_ready"], 1)

            def take_x(t, j):
                dve.wait_ge(sem["turned"], t + 1)
                dve.wait_ge(sem["upped"], (t + 1) * 2)
                x, xT = xs[:, j % 2, :], ps[:, 4 + j % 2, 0:LOT]
                if layer:
                    ins = dve.tensor_scalar(x, xT, nwb[:, 0:1], nwb[:, 1:2], ALU.mult, ALU.add)
                else:
                    ins = dve.tensor_copy(x, xT)
                ins.then_inc(sem["x_ready"], 1)

            def put_y(t, j):
                dve.wait_ge(sem["weight_ready"], t + UNROLL + 1)
                dve.wait_ge(sem["downed"], t + UNROLL + 1)
                for h in range(HALVES):
                    ins = dve.tensor_scalar(y[:, j, h, :], ps[:, 6 + j % 2, P * h:P * h + P],
                                            weight[:, j, h:h + 1], None, ALU.mult)
                ins.then_inc(sem["y_ready"], 1)

            dve.sem_inc(sem["x_ready"], 2)
            dve.sem_inc(sem["y_ready"], 2)
            dve.sem_inc(sem["weight_ready"], UNROLL)
            dve.wait_ge(sem["loaded"], 32)
            staggered(dve, [(get_own, 0), (take_x, 0), (put_y, 2)], lots, UNROLL)

        @block.gpsimd
        def _(pool):
            pool.sem_inc(sem["y_free"], UNROLL)

            def send(t, j):
                pool.wait_ge(sem["y_ready"], t + 3)
                pool.sem_inc(sem["y_seen"], 1)
                for h in range(HALVES):
                    pool.indirect_dma_start(
                        m["y_dram"][layer], bass.IndirectOffsetOnAxis(ap=where[:, j, h:h + 1], axis=0),
                        y[:, j, h, :], None).then_inc(sem[f"sent{j}"], 16)

            def free(t, j):
                pool.wait_ge(sem[f"sent{j}"], t * (16 * HALVES // UNROLL)
                             + 16 * HALVES // UNROLL * (UNROLL - j))
                pool.sem_inc(sem["y_free"], 1)

            staggered(pool, [(free, 2), (send, 0)], lots, UNROLL)

        @block.tensor
        def _(pe):
            pe.sem_inc(sem["downed"], UNROLL)
            pe.sem_inc(sem["upped"], 4)

            def turn(t, j):
                pe.wait_ge(sem[f"rows{j}"], rows_loaded(t, j))
                pe.wait_ge(sem["x_ready"], t + 1)
                for h in range(HALVES):
                    ins = pe.transpose(ps[:, 4 + j % 2, P * h:P * h + P], rows[:, j, h, 0:D], ident)
                ins.then_inc(sem["turned"], 1)

            def make_hidden(t, j):
                pe.wait_ge(sem["x_ready"], t + 3)
                pe.wait_ge(sem["own_ready"], t + 1)
                pe.wait_ge(sem["hidden_ready"], t + 1)
                for k in range(KI):
                    ins = pe.matmul(ps[:, 2 * (j % 2) + k // 2, (k % 2) * LOT:(k % 2) * LOT + LOT],
                                    own[:, j, P * k:P * k + P], xs[:, j % 2, :], start=True, stop=True)
                    if k % 2 == 1:
                        ins.then_inc(sem["upped"], 1)

            def make_out(t, j):
                pe.wait_ge(sem["hidden_ready"], t + 3)
                pe.wait_ge(sem["y_ready"], t + 1)
                for h in range(HALVES):
                    for k in range(KI):
                        n = INTER + D * k
                        ins = pe.matmul(ps[:, 6 + j % 2, P * h:P * h + P], hidden[:, j % 2, k, P * h:P * h + P],
                                        own[:, j, n:n + D], start=(k == 0), stop=(k == KI - 1))
                ins.then_inc(sem["downed"], 1)

            staggered(pe, [(turn, 0), (make_hidden, 1), (make_out, 2)], lots, UNROLL)

        @block.scalar
        def _(act):
            act.sem_inc(sem["hidden_ready"], 2)
            act.wait_ge(sem["loaded"], 32)

            def activate(t, j):
                act.wait_ge(sem["downed"], t + UNROLL - 1)
                for k in range(KI):
                    if k % 2 == 0:
                        act.wait_ge(sem["upped"], t * 2 + (k // 2 + 5))
                    ins = act.activation(hidden[:, j % 2, k, :],
                                         ps[:, 2 * (j % 2) + k // 2, (k % 2) * LOT:(k % 2) * LOT + LOT],
                                         act_func, bias=own[:, j, PACK - KI + k:PACK - KI + k + 1])
                ins.then_inc(sem["hidden_ready"], 1)

            staggered(act, [(activate, 0)], lots, UNROLL)


def shared(nc, a, m, layer, out=None):
    ps, stream, xT, weights, ident = m["ps"], m["stream"], m["xT"], m["weights"], m["ident"]
    act_func = (ACT.Silu, ACT.Gelu_apprx_tanh)[layer]
    choices = 2 - layer
    with ExitStack() as ctx:
        def sb(name, shape, dt=F32):
            return ctx.enter_context(nc.sbuf_tensor(f"{name}_{layer}", shape, dt))

        pack = sb("pack", [P, PACK])
        out_bias = sb("out_bias", [P, GN])
        hidden = sb("h", [P, 2, KI, GN])
        ws = sb("ws", [P, 2, P])
        wsT = sb("wsT", [P, 2, P])
        routed = sb("routed", [P, 2, choices, GROUP, D])
        stats, mv, rstd = sb("stats_n", [P, 2, GROUP, 6]), sb("mv_n", [P, 2, GROUP, 2]), sb("rstd_n", [P, 2, GROUP])
        sem, block = ctx.enter_context(stage(nc, f"e{layer}_",
            ("loaded", "upped", "hidden_ready", "downed", "ws_ready", "ws_turned", "wsT_ready", "summed",
                "added", "chain", "routed0", "routed1", "stats", "moments", "raised", "rstd", "added_seen", "stored")))
        y = m["y_dram"][layer][0:choices * TOKENS, :].rearrange("(c t p) d -> c p t d", c=choices, p=P)

        @block.sync
        def _(sp):
            sp.dma_start(pack[:, :], a[f"experts{layer}"][:, E, :]).then_inc(sem["loaded"], 16)
            sp.dma_start(out_bias[:, :], a[f"out_bias{layer}"]).then_inc(sem["loaded"], 16)

            def load_routed(g, u):
                sp.wait_ge(sem["summed"], g + 1)
                for c in range(choices):
                    sp.dma_start(routed[:, u, c, :, :], y[c][:, bass.ds(g * GROUP, GROUP), :])\
                      .then_inc(sem[f"routed{u}"], 16)

            def store(g, u):
                sp.wait_ge(sem["added"], g + 2)
                sp.dma_start(out[:, bass.ds(g * GROUP, GROUP), :], stream[:, bass.ds(g * GROUP, GROUP), :])\
                  .then_inc(sem["stored"], 16)

            if layer == 0:
                staggered(sp, [(load_routed, 0)])
            else:
                staggered(sp, [(load_routed, 0), (store, 2)])
                sp.wait_ge(sem["stored"], 16 * GROUPS)

        @block.gpsimd
        def _(pool):
            def gather_weights(g, u):
                pool.wait_ge(sem["ws_turned"], g + 1)
                pool.tensor_copy(ws[:, u, :], weights[:, bass.ds(g * GROUP, GROUP), :].rearrange(
                    "p k e -> p (k e)")).then_inc(sem["ws_ready"], 1)

            def root(g, u):
                inverse_root(pool, sem, g, rstd[:, u], m["power"])

            staggered(pool, [(gather_weights, 0)] if layer else [(gather_weights, 0), (root, 1)])

        @block.tensor
        def _(pe):
            pe.wait_ge(sem["loaded"], 32)
            pe.sem_inc(sem["ws_turned"], 2)
            pe.sem_inc(sem["downed"], 2)

            def make_hidden(g, half):
                for k in range(KI):
                    pe.wait_ge(sem["hidden_ready"], g * KI + k + 1)
                    pe.matmul(ps[:, k, :], pack[:, P * k:P * k + P], xT[:, bass.ds(g * GN, GN)],
                              start=True, stop=True).then_inc(sem["upped"], 1)

            def turn_weights(g, u):
                pe.wait_ge(sem["ws_ready"], g + 1)
                pe.wait_ge(sem["wsT_ready"], g + 1)
                pe.transpose(ps[:, 7, 0:P], ws[:, u, :], ident).then_inc(sem["ws_turned"], 1)

            def make_out(g, half):
                pe.wait_ge(sem["hidden_ready"], g * KI + 2 * KI)
                pe.wait_ge(sem["summed"], g + 1)
                for t in range(GROUP):
                    for k in range(KI):
                        n = INTER + D * k
                        pe.matmul(ps[:, 4 + half, P * t:P * t + P], hidden[:, half, k, P * t:P * t + P],
                                  pack[:, n:n + D], start=(k == 0), stop=(k == KI - 1))
                pe.wait_ge(sem["wsT_ready"], g + 2)
                pe.wait_ge(sem["added"], g + 1)
                pe.matmul(ps[:, 6, :], wsT[:, half, :], out_bias[:, :], start=True, stop=True)\
                  .then_inc(sem["downed"], 1)

            with pe.Fori(0, GROUPS // 2) as i:
                make_hidden(i * 2, 0)
                turn_weights(i * 2, 0)
                make_hidden(i * 2 + 1, 1)
                make_out(i * 2, 0)
                turn_weights(i * 2 + 1, 1)
                make_out(i * 2 + 1, 1)

        @block.scalar
        def _(act):
            act.wait_ge(sem["loaded"], 32)
            act.sem_inc(sem["hidden_ready"], KI)
            with act.Fori(0, GROUPS // 2) as i:
                for half in range(2):
                    g = i * 2 + half
                    act.wait_ge(sem["downed"], g + 1)
                    for k in range(KI):
                        act.wait_ge(sem["upped"], g * KI + k + 1)
                        act.activation(hidden[:, half, k, :], ps[:, k, :], act_func,
                                       bias=pack[:, PACK - KI + k:PACK - KI + k + 1])\
                           .then_inc(sem["hidden_ready"], 1)

        @block.vector
        def _(dve):
            dve.sem_inc(sem["summed"], 2)
            dve.sem_inc(sem["added"], 1)
            dve.sem_inc(sem["wsT_ready"], 1)

            def add_all(g, u):
                tiles = stream[:, bass.ds(g * GROUP, GROUP), :]
                dve.wait_ge(sem["ws_turned"], g + 3)
                dve.tensor_copy(wsT[:, u, :], ps[:, 7, 0:P]).then_inc(sem["wsT_ready"], 1)
                dve.wait_ge(sem[f"routed{u}"], g * (8 * choices) + (16 - 8 * u) * choices)
                r = routed[:, u]
                c = Chain(dve, sem["chain"], g * choices)
                if choices == 2:
                    c.link(dve.tensor_tensor(r[:, 0], r[:, 0], r[:, 1], ALU.add))
                c.link(dve.tensor_tensor(tiles, tiles, r[:, 0], ALU.add))
                dve.wait_ge(sem["downed"], g + 3)
                for k in range(GROUP):
                    tile = tile_of(stream, g * GROUP + k)
                    ins = dve.scalar_tensor_tensor(
                        tile, ps[:, 4 + u, P * k:P * k + P],
                        weights[:, bass.ds(g * GROUP + k, 1), E:E + 1].rearrange("p k e -> p (k e)"),
                        tile, ALU.mult, ALU.add)
                ins.then_inc(sem["summed"], 1)
                dve.wait_ge(sem["summed"], g + 3)
                dve.tensor_tensor(tiles, tiles, ps[:, 6, :].rearrange("p (k d) -> p k d", d=D),
                                  ALU.add).then_inc(sem["added"], 1)

            def measure(g, u):
                dve.wait_ge(sem["added"], g + 2)
                dve.sem_inc(sem["added_seen"], 1)
                moments(dve, sem, g, stream, g * GROUP, stats[:, u], mv[:, u], rstd[:, u], m["post"], EPS)

            def normalise(g, u):
                dve.wait_ge(sem["rstd"], g + 1)
                for k in range(GROUP):
                    dve.tensor_scalar(tile_of(m["xn"], g * GROUP + k), tile_of(stream, g * GROUP + k),
                                      mv[:, u, k, 0:1], rstd[:, u, k:k + 1], ALU.subtract, ALU.mult)

            staggered(dve, [(add_all, 0)] if layer else [(normalise, 2), (measure, 1), (add_all, 0)])


def tile_of(t, k):
    return t[:, bass.ds(k, 1), :].rearrange("p k d -> p (k d)")


def moments(dve, sem, g, source, first, stats, mv, rstd, post, eps):
    for k in range(GROUP):
        ins = dve.bn_stats(stats[:, k, :], tile_of(source, first + k))
    ins.then_inc(sem["stats"], 1)
    dve.wait_ge(sem["stats"], g + 1)
    dve.memset(post[:, :], 0.0)
    for k in range(GROUP):
        ins = dve.bn_aggr(mv[:, k, :], stats[:, k, :])
    ins.then_inc(sem["moments"], 1)
    dve.wait_ge(sem["moments"], g + 1)
    dve.tensor_scalar(rstd, mv[:, :, 1], eps, None, ALU.add).then_inc(sem["raised"], 1)


def inverse_roots(c, x, guess, root):
    dve, bits = c.engine, mybir.dt.int32
    c.link(dve.tensor_scalar(x[:, :], x[:, :], TINY, None, ALU.max))
    c.link(dve.tensor_scalar(guess[:, :].bitcast(bits), x[:, :].bitcast(bits), 1, None, ALU.logical_shift_right))
    c.did(dve.tensor_scalar(root[:, :].bitcast(bits), guess[:, :].bitcast(bits), -1.0, float(0x5f3759df),
                            ALU.mult, ALU.add))
    c.link(dve.tensor_scalar(x[:, :], x[:, :], -0.5, None, ALU.mult))
    for _ in range(NEWTON):
        c.link(dve.tensor_tensor(guess[:, :], root[:, :], root[:, :], ALU.mult))
        c.link(dve.tensor_tensor(guess[:, :], guess[:, :], x[:, :], ALU.mult))
        c.link(dve.scalar_tensor_tensor(root[:, :], guess[:, :], 1.5, root[:, :], ALU.add, ALU.mult))


def inverse_root(pool, sem, g, rstd, power):
    pool.wait_ge(sem["raised"], g + 1)
    pool.tensor_tensor(rstd, rstd, power[:, 0:GROUP], ALU.pow).then_inc(sem["rstd"], 1)


def convolve(nc, a, m):
    ps, xn, ident = m["ps"], m["xn"], m["ident"]
    y = m["xT"][:, :].rearrange("p (t h) -> p t h", h=D)
    QUADS = CH // 4
    with ExitStack() as ctx:
        toeplitz = ctx.enter_context(nc.sbuf_tensor("toeplitz", [P, 2, CH, T], F32))
        xc = ctx.enter_context(nc.sbuf_tensor("xc", [P, 2, CH, 2, B], F32))
        yb = ctx.enter_context(nc.sbuf_tensor("yb", [P, QUADS, T], F32))
        sem, block = ctx.enter_context(stage(nc, "c_",
            ("loaded0", "loaded1", "xc_ready", "convolved", "yb_ready", "turned", "placed")))

        @block.sync
        def _(sp):
            for q in range(D // CH):
                sp.wait_ge(sem["convolved"], q + 1)
                src = bass.AP(m["kernel_dram"].tensor, q * (CH * KPAD), [[1, P], [KPAD, CH], [1, T]])
                sp.dma_start(toeplitz[:, q % 2, :, :], src).then_inc(sem[f"loaded{q % 2}"], 16)

        @block.gpsimd
        def _(pool):
            with pool.Fori(0, D // CH // 2) as i:
                for u in range(2):
                    q = i * 2 + u
                    pool.wait_ge(sem["convolved"], q + 1)
                    for t in range(2):
                        ins = pool.tensor_copy(
                            xc[:, u, :, t, :],
                            xn[:, t::2, bass.ds(q * CH, CH)].rearrange("p b c -> p c b"))
                    ins.then_inc(sem["xc_ready"], 1)

        @block.tensor
        def _(pe):
            pe.sem_inc(sem["convolved"], 2)
            pe.sem_inc(sem["turned"], 1)
            with pe.Fori(0, D // CH // 2) as i:
                for u in range(2):
                    q = i * 2 + u
                    pe.wait_ge(sem[f"loaded{u}"], i * 16 + 16)
                    pe.wait_ge(sem["xc_ready"], q + 1)
                    pe.wait_ge(sem["yb_ready"], q + 1)
                    for k in range(QUADS):
                        bank = ps[:, 2 * u + k // 2, (k % 2) * T:(k % 2) * T + T]
                        for r in range(4):
                            pe.matmul(bank[32 * r:32 * r + 32, :], xc[:, u, 4 * k + r, 0, :],
                                      toeplitz[:, u, 4 * k + r, :], start=True, stop=False,
                                      tile_position=(0, 32 * r), skip_group_check=True)
                        for r in range(4):
                            ins = pe.matmul(bank[32 * r:32 * r + 32, 0:P], xc[:, u, 4 * k + r, 1, :],
                                            toeplitz[:, u, 4 * k + r, P:T], start=False, stop=True,
                                            tile_position=(0, 32 * r), skip_group_check=True)
                    ins.then_inc(sem["convolved"], 1)
                    pe.wait_ge(sem["yb_ready"], q + 2)
                    pe.wait_ge(sem["placed"], q + 1)
                    for t in range(2):
                        for k in range(QUADS):
                            ins = pe.transpose(ps[:, 4 + t, P * k:P * k + P], yb[:, k, P * t:P * t + P], ident)
                    ins.then_inc(sem["turned"], 1)

        @block.scalar
        def _(act):
            act.sem_inc(sem["yb_ready"], 1)
            with act.Fori(0, D // CH // 2) as i:
                for u in range(2):
                    q = i * 2 + u
                    act.wait_ge(sem["convolved"], q + 3)
                    act.wait_ge(sem["turned"], q + 1)
                    act.copy(yb[:, :, :], ps[:, 2 * u:2 * u + 2, :].rearrange(
                        "p k (j t) -> p (k j) t", t=T)[:, :, ::-1]).then_inc(sem["yb_ready"], 1)

        @block.vector
        def _(dve):
            dve.sem_inc(sem["placed"], 1)
            with dve.Fori(0, D // CH) as q:
                dve.wait_ge(sem["turned"], q + 2)
                for t in range(2):
                    ins = dve.tensor_copy(y[:, t::2, bass.ds(q * CH, CH)].rearrange("p b c -> p c b"),
                                          ps[:, 4 + t, :].rearrange("p (c b) -> p c b", b=B))
                ins.then_inc(sem["placed"], 1)


def glu_and_norm(nc, a, m):
    ps, stream, ident, rows = m["ps"], m["stream"], m["ident"], m["rows"]
    y = m["xT"][:, :].rearrange("p (t h) -> p t h", h=D)
    with ExitStack() as ctx:
        def sb(name, shape, dt=F32):
            return ctx.enter_context(nc.sbuf_tensor(name, shape, dt))

        w_out = sb("w_out", [P, 2 * D])
        ys = sb("ys", [P, 2, GROUP, D])
        yT = sb("yT", [P, 2, GN])
        glu = sb("glu", [P, 2, GROUP, 2 * D])
        stats, mv, rstd = sb("stats2", [P, 2, GROUP, 6]), sb("mv2", [P, 2, GROUP, 2]), sb("rstd2", [P, 2, GROUP])
        z = sb("z2", [P, 2, GROUP, D])
        sem, block = ctx.enter_context(stage(nc, "g_",
            ("loaded", "staged", "turned", "yT_ready", "projected", "biased", "tanh", "gated", "stats", "moments", "raised", "rstd",
                "shifted", "scaled")))
        wide = lambda first, n: rows[:, first:first + n].unsqueeze(1).broadcast_to([P, GROUP, n])

        @block.sync
        def _(sp):
            sp.dma_start(w_out[:, :], a["w_out"]).then_inc(sem["loaded"], 16)

        @block.gpsimd
        def _(pool):
            def shift(g, u):
                tiles = stream[:, bass.ds(g * GROUP, GROUP), :]
                pool.tensor_tensor(tiles, tiles, wide(R_BETA, D), ALU.add).then_inc(sem["shifted"], 1)

            def root(g, u):
                inverse_root(pool, sem, g, rstd[:, u], m["power"])

            staggered(pool, [(shift, 0), (root, 1)])

        @block.tensor
        def _(pe):
            pe.wait_ge(sem["loaded"], 16)

            def turn(g, u):
                pe.wait_ge(sem["staged"], g + 1)
                wait_from(pe, sem["yT_ready"], g - 1)
                for k in range(GROUP):
                    ins = pe.transpose(ps[:, u, P * k:P * k + P], ys[:, u, k, :], ident)
                ins.then_inc(sem["turned"], 1)

            def project(g, u):
                pe.wait_ge(sem["yT_ready"], g + 1)
                wait_from(pe, sem["biased"], g - 1)
                for k in range(GROUP):
                    ins = pe.matmul(ps[:, 2 + 2 * u + k // 2, (k % 2) * 2 * D:(k % 2) * 2 * D + 2 * D],
                                    yT[:, u, P * k:P * k + P], w_out[:, :], start=True, stop=True)
                ins.then_inc(sem["projected"], 1)

            staggered(pe, [(turn, 0), (project, 1)])

        @block.scalar
        def _(act):
            def fix(g, u):
                wait_from(act, sem["turned"], g - 1)
                act.copy(ys[:, u, :, :], y[:, bass.ds(g * GROUP, GROUP), :]).then_inc(sem["staged"], 1)

            def take_yT(g, u):
                act.wait_ge(sem["turned"], g + 1)
                wait_from(act, sem["projected"], g - 1)
                act.activation(yT[:, u, :], ps[:, u, :], ACT.Gelu_apprx_tanh).then_inc(sem["yT_ready"], 1)

            def gate(g, u):
                act.wait_ge(sem["biased"], g + 1)
                act.activation(glu[:, u, :, D:2 * D], glu[:, u, :, D:2 * D], ACT.Tanh, scale=0.5)\
                   .then_inc(sem["tanh"], 1)

            staggered(act, [(fix, 0), (take_yT, 1), (gate, 2)])

        @block.vector
        def _(dve):
            def add_bias(g, u):
                wait_from(dve, sem["scaled"], g - 1)
                dve.wait_ge(sem["projected"], g + 1)
                dve.tensor_tensor(glu[:, u, :, :],
                                  ps[:, 2 + 2 * u:4 + 2 * u, :].rearrange("p k (j d) -> p (k j) d", d=2 * D),
                                  wide(R_BOUT, 2 * D), ALU.add).then_inc(sem["biased"], 1)

            def gate_and_measure(g, u):
                dve.wait_ge(sem["tanh"], g + 1)
                v = glu[:, u, :, 0:D]
                dve.scalar_tensor_tensor(v, glu[:, u, :, D:2 * D], 1.0, v, ALU.add, ALU.mult)\
                    .then_inc(sem["gated"], 1)
                dve.wait_ge(sem["gated"], g + 1)
                moments(dve, sem, g, v, 0, stats[:, u], mv[:, u], rstd[:, u], m["post"], 4 * EPS)

            def normalise(g, u):
                dve.wait_ge(sem["rstd"], g + 1)
                for k in range(GROUP):
                    ins = dve.scalar_tensor_tensor(z[:, u, k, :], glu[:, u, k, 0:D], mv[:, u, k, 0:1],
                                                   rows[:, R_GAMMA:R_GAMMA + D], ALU.subtract, ALU.mult)
                ins.then_inc(sem["scaled"], 1)

            def add(g, u):
                dve.wait_ge(sem["shifted"], g + 1)
                dve.wait_ge(sem["scaled"], g + 1)
                for k in range(GROUP):
                    tile = tile_of(stream, g * GROUP + k)
                    dve.scalar_tensor_tensor(tile, z[:, u, k, :], rstd[:, u, k:k + 1], tile, ALU.mult, ALU.add)

            staggered(dve, [(normalise, 2), (gate_and_measure, 1), (add_bias, 0), (add, 2)])


def norm_and_gate1(nc, a, m):
    ps, stream, xn, xT, ident = m["ps"], m["stream"], m["xn"], m["xT"], m["ident"]
    with ExitStack() as ctx:
        def sb(name, shape, dt=F32):
            return ctx.enter_context(nc.sbuf_tensor(name, shape, dt))

        wg = sb("wg", [P, E + 2])
        nwb = sb("nwb", [P, 2])
        stats, mv, rstd = sb("stats3", [P, 2, GROUP, 6]), sb("mv3", [P, 2, GROUP, 2]), sb("rstd3", [P, 2, GROUP])
        z = sb("z3", [P, 2, GROUP, D])
        aT = sb("aT", [P, 2, GN])
        sem, block = ctx.enter_context(stage(nc, "q_",
            ("loaded", "stats", "moments", "raised", "rstd", "normal", "turned", "aT_ready", "kept", "kept_seen", "logits", "taken")))

        @block.sync
        def _(sp):
            sp.dma_start(wg[:, :], a["wg"]).then_inc(sem["loaded"], 16)
            sp.dma_start(nwb[:, :], a["nwb"]).then_inc(sem["loaded"], 16)

        @block.gpsimd
        def _(pool):
            def root(g, u):
                inverse_root(pool, sem, g, rstd[:, u], m["power"])

            def add_residual(g, u):
                tiles = stream[:, bass.ds(g * GROUP, GROUP), :]
                pool.tensor_tensor(tiles, tiles, xn[:, bass.ds(g * GROUP, GROUP), :], ALU.add)\
                    .then_inc(sem["kept"], 1)

            staggered(pool, [(root, 0), (add_residual, 0)])

        @block.vector
        def _(dve):
            def measure(g, u):
                moments(dve, sem, g, xn, g * GROUP, stats[:, u], mv[:, u], rstd[:, u], m["post"], EPS_NW)

            def normalise(g, u):
                dve.wait_ge(sem["rstd"], g + 1)
                wait_from(dve, sem["turned"], g - 1)
                for k in range(GROUP):
                    ins = dve.tensor_scalar(z[:, u, k, :], tile_of(xn, g * GROUP + k), mv[:, u, k, 0:1],
                                            rstd[:, u, k:k + 1], ALU.subtract, ALU.mult)
                ins.then_inc(sem["normal"], 1)

            def keep(g, u):
                dve.wait_ge(sem["normal"], g + 1)
                dve.wait_ge(sem["kept"], g + 1)
                dve.sem_inc(sem["kept_seen"], 1)
                dve.tensor_copy(xn[:, bass.ds(g * GROUP, GROUP), :], z[:, u, :, :])

            def take_logits(g, u):
                dve.wait_ge(sem["logits"], g + 1)
                dve.tensor_copy(m["weights"][:, bass.ds(g * GROUP, GROUP), 0:E + 2],
                                ps[:, 2 + u, 0:GROUP * (E + 2)].rearrange("p (k e) -> p k e", e=E + 2))\
                   .then_inc(sem["taken"], 1)

            staggered(dve, [(normalise, 1), (measure, 0), (keep, 1), (take_logits, 3)])

        @block.tensor
        def _(pe):
            pe.wait_ge(sem["loaded"], 32)

            def turn(g, u):
                pe.wait_ge(sem["normal"], g + 1)
                wait_from(pe, sem["aT_ready"], g - 1)
                for k in range(GROUP):
                    ins = pe.transpose(ps[:, u, P * k:P * k + P], z[:, u, k, :], ident)
                ins.then_inc(sem["turned"], 1)

            def make_logits(g, u):
                pe.wait_ge(sem["aT_ready"], g + 1)
                wait_from(pe, sem["taken"], g - 1)
                for k in range(GROUP):
                    ins = pe.matmul(ps[:, 2 + u, (E + 2) * k:(E + 2) * (k + 1)], aT[:, u, P * k:P * k + P],
                                    wg[:, :], start=True, stop=True)
                ins.then_inc(sem["logits"], 1)

            staggered(pe, [(turn, 0), (make_logits, 1)])

        @block.scalar
        def _(act):
            act.wait_ge(sem["loaded"], 32)

            def take_aT(g, u):
                act.wait_ge(sem["turned"], g + 1)
                wait_from(act, sem["logits"], g - 1)
                act.activation(xT[:, bass.ds(g * GN, GN)], ps[:, u, :], ACT.Identity, bias=nwb[:, 1:2],
                               scale=nwb[:, 0:1])
                act.activation(aT[:, u, :], ps[:, u, :], ACT.Identity, bias=nwb[:, 1:2],
                               scale=nwb[:, 0:1]).then_inc(sem["aT_ready"], 1)

            staggered(act, [(take_aT, 0)])


def top1(nc, a, m):
    ps, cst, weights = m["ps"], m["cst"], m["weights"]
    with ExitStack() as ctx:
        def sb(name, shape, dt=F32):
            return ctx.enter_context(nc.sbuf_tensor(name, shape, dt))

        z, mask = sb("z4", [P, TILES, E]), sb("mask4", [P, TILES, E])
        place, before = sb("place", [P, TILES, E]), sb("before", [P, E, TILES])
        coef = sb("coef", [P, TILES, 2])
        slot = sb("slot4", [P, TILES, E])
        total = sb("total4", [P, E])
        token = cst[:, C_TOKEN:C_TOKEN + TILES]
        ones = sb("ones", [P, P])
        v = [sb(f"w{i}", [P, TILES]) for i in range(4)]
        sem, block = ctx.enter_context(stage(nc, "o_",
            ("args", "expo", "mask", "counts", "chain")))
        jrev = cst[:, C_JREV:C_JREV + E].unsqueeze(1).broadcast_to([P, TILES, E])
        wide = lambda t: t.unsqueeze(2).broadcast_to([P, TILES, E])

        @block.scalar
        def _(act):
            act.wait_ge(sem["args"], 1)
            act.activation(z[:, :, :], z[:, :, :], ACT.Exp).then_inc(sem["expo"], 1)
            act.wait_ge(sem["args"], 2)
            act.activation(coef[:, :, :], coef[:, :, :], ACT.Exp).then_inc(sem["expo"], 1)

        @block.tensor
        def _(pe):
            count(pe, m, sem, mask, ones)

        @block.vector
        def _(dve):
            c = Chain(dve, sem["chain"])
            tt = dve.tensor_tensor
            c.did(dve.memset(ones[:, :], 1.0))
            softmax_parts(c, dve, (sem["expo"], 1), sem["args"], weights[:, :, 0:E], v[0], z, v[1])
            softmax_parts(c, dve, (sem["expo"], 2), sem["args"], weights[:, :, E:E + 2], v[2], coef, v[3])
            first_of(c, dve, mask, z, v[0], v[1], jrev)
            dve.engine_nop().then_inc(sem["mask"], 1)
            rowbuf, ts = m["rowbuf"], dve.tensor_scalar
            c.did(ts(rowbuf[:, :, ROW_E1], v[1][:, :], -1.0, float(E), ALU.mult, ALU.add))
            c.did(ts(rowbuf[:, :, ROW_ID], token, float(TOKENS), None, ALU.add))
            c.did(dve.memset(rowbuf[:, :, ROW_W2], 0.0))
            dve.wait_ge(sem["counts"], 1)
            places(c, dve, ps, ones, before, place, total[:, :])
            c.link(tt(slot[:, :, :], mask[:, :, :], place[:, :, :], ALU.mult))
            c.link(dve.tensor_reduce(v[2][:, :], slot[:, :, :], AX.X, ALU.add))
            c.link(ts(v[3][:, :], v[2][:, :], float(CAP), None, ALU.is_lt))
            c.link(dve.scalar_tensor_tensor(v[2][:, :], rowbuf[:, :, ROW_E1], float(CAP), v[2][:, :],
                                            ALU.mult, ALU.add))
            c.link(tt(v[2][:, :], v[2][:, :], rowbuf[:, :, ROW_ID], ALU.subtract))
            c.link(tt(v[2][:, :], v[2][:, :], v[3][:, :], ALU.mult))
            c.link(tt(v[2][:, :], v[2][:, :], rowbuf[:, :, ROW_ID], ALU.add))
            c.did(dve.tensor_copy(m["slots"][:, 0, :], v[2][:, :]))
            c.did(dve.tensor_copy(m["table"][:, 0:LOTS[1]], cst[:, C_TABLE1:C_TABLE1 + LOTS[1]]))
            c.did(dve.tensor_copy(m["table_int"][:, 0:LOTS[1]], cst[:, C_TABLE1:C_TABLE1 + LOTS[1]]))
            c.link(dve.tensor_scalar(place[:, :, :], place[:, :, :], float(CAP), None, ALU.is_lt))
            c.did(tt(z[:, :, :], z[:, :, :], mask[:, :, :], ALU.mult))
            c.link(tt(place[:, :, :], place[:, :, :], wide(coef[:, :, 1]), ALU.mult))
            c.link(tt(weights[:, :, 0:E], z[:, :, :], place[:, :, :], ALU.mult))
            dve.tensor_reduce(rowbuf[:, :, ROW_DW], weights[:, :, 0:E], AX.X, ALU.add)
            dve.tensor_copy(weights[:, :, E], coef[:, :, 0])
            dve.memset(weights[:, :, E + 1:WCOLS], 0.0)


def constants():
    c = np.zeros((P, C_END), np.float32)
    c[:, C_ID:C_ID + P] = np.eye(P)
    c[:, C_TRI:C_TRI + P] = np.triu(np.ones((P, P)), 1)
    c[:, C_JREV:C_JREV + E] = E - np.arange(E)
    down = np.arange(LOW)[::-1]
    c[:, C_LAG:C_LAG + 2 * LOW] = np.concatenate([down, LOW * down])
    c[:, C_COUNT:C_COUNT + LOTS[0]] = np.arange(LOTS[0])
    c[:, C_TOKEN:C_TOKEN + TILES] = np.arange(TILES) * P + np.arange(P)[:, None]
    c[:, C_TABLE1:C_TABLE1 + LOTS[1]] = np.arange(LOTS[1]) * LOT // CAP
    c[:, C_MASK:C_MASK + P] = np.kron(np.eye(8), np.ones((LOW, LOW)))
    return c


def arrange(i):
    def f(name):
        return np.asarray(i[name])

    def column(v):
        return v.reshape(-1, 1)

    def pack(up, shared_up, down, shared_down, bias, shared_bias):
        up = np.concatenate([up, shared_up[None]]).transpose(1, 0, 2)
        down = np.concatenate([down, shared_down[None]]).reshape(EA, KI, P, D).transpose(2, 0, 1, 3)
        bias = np.concatenate([bias, shared_bias[None]]).reshape(EA, KI, P).transpose(2, 0, 1)
        return np.concatenate([up, down.reshape(P, EA, KI * D), bias], axis=2)

    def out_bias(rows):
        o = np.zeros((GROUP, WCOLS, GROUP, D), np.float32)
        for k in range(GROUP):
            o[k, 0:len(rows), k] = rows
        return o.reshape(P, GN)

    r = {
        "x": f("L0_attn_x").reshape(TOKENS, D),
        "cst": constants(),
        "rows": np.broadcast_to(np.concatenate([
            f("L0_attn_bq"), f("L0_attn_bk"), f("L0_attn_bv"), f("L1_attn_b_out"), f("L1_attn_gamma"),
            f("L1_attn_beta")]), (P, R_END)),
        "s4": np.concatenate([f("L1_attn_A_re"), f("L1_attn_A_im"), f("L1_attn_C_re"), f("L1_attn_C_im"),
                              column(f("L1_attn_log_dt")), column(f("L1_attn_D"))], axis=1),
        "w_router": np.concatenate([f("L0_ffn_Wr1"), f("L0_attn_Wg1").T], axis=1),
        "wr2": np.concatenate([f("L0_ffn_Wr2"), f("L0_ffn_br2")[None]]),
        "b_router": np.stack([np.pad(f("L0_ffn_br1"), (0, HG - R1)), f("L0_attn_bg1")], axis=1),
        "wg2": np.repeat(f("L0_attn_Wg2").T, DK, axis=1),
        "gate_bias": np.repeat(np.stack([f("L0_attn_bg2"), f("L0_attn_g")], axis=1), DK, axis=0),
        "wqkv": np.concatenate([f("L0_attn_Wq").T, f("L0_attn_Wk").T, f("L0_attn_Wv").T], axis=1),
        "wo": f("L0_attn_Wo").T,
        "experts0": pack(*(f("L0_ffn_" + n) for n in ("We1", "Ws1", "We2", "Ws2", "be1", "bs1"))),
        "out_bias0": out_bias(np.concatenate([f("L0_ffn_be2"), f("L0_ffn_bs2")[None], f("L0_attn_bo")[None]])),
        "w_out": f("L1_attn_W_out"),
        "wg": np.concatenate([f("L1_ffn_wg"), f("L1_ffn_res_coef")], axis=1),
        "nwb": np.stack([f("L1_ffn_attn_nw"), f("L1_ffn_attn_nb")], axis=1),
        "experts1": pack(*(f("L1_ffn_" + n) for n in ("inter_w", "res_inter_w", "output_w", "res_output_w",
                                                       "inter_b", "res_inter_b"))),
        "out_bias1": out_bias(np.concatenate([f("L1_ffn_output_b"), f("L1_ffn_res_output_b")[None]])),
    }
    return {k: np.ascontiguousarray(v) for k, v in r.items()}


def kernel(**inputs):
    import concourse.bacc as bacc
    from concourse.bass_utils import run_bass_kernel_spmd

    arrays = arrange(inputs)
    nc = bacc.Bacc("TRN2", target_bir_lowering=False, num_devices=1)
    a = {k: nc.dram_tensor("in_" + k, v.shape, F32, kind="ExternalInput").ap() for k, v in arrays.items()}
    out = nc.dram_tensor("out", (TOKENS, D), F32, kind="ExternalOutput").ap()
    build(nc, a, out)
    r = run_bass_kernel_spmd(nc, [{"in_" + k: v for k, v in arrays.items()}], core_ids=[0])
    return np.asarray(r.results[0]["out"]).reshape(B, T, D)
```

```python
from contextlib import ExitStack, contextmanager

import numpy as np

import concourse.bass as bass
from concourse import mybir

F32 = mybir.dt.float32
F16 = mybir.dt.float16
ALU = mybir.AluOpType
ACT = mybir.ActivationFunctionType
AX = mybir.AxisListType

P = 128
B, T, D = 32, 256, 128
TOKENS = B * T
TILES = TOKENS // P
H, DK = 16, 8
HG = 64
E = 8
EA = E + 1
INTER = 512
KI = INTER // P
CAP = TOKENS // E
R1 = 32
NS = 64
GROUP = 4
GROUPS = TILES // GROUP
GN = GROUP * P
STACK = 4 * DK
VW = 32
PAIRS = H // 2
LOW = 16
CH = 16
KPAD = P + T
WCOLS = E + 2
LOT = 256
LOTS = (2 * TOKENS // LOT + E, TOKENS // LOT)
UNROLL = 4
BLANK = 8
BLANK_CHUNKS = [(i, k) for i in range(2) for k in range(LOTS[i] * LOT // (BLANK * P))]
P_DOWN = INTER
P_BIAS = P_DOWN + KI * D
P_OUT = P_BIAS + KI
PACK = P_OUT + D
ROW_ID, ROW_DW, ROW_W2, ROW_E1 = D, D + 1, D + 2, D + 3
ROW = D + 4
TINY = 1e-24
NEWTON = 3
ROOT_STEPS = 4 + 3 * NEWTON
EPS = 1e-5
EPS_NW = 1e-12

C_ID, C_TRI, C_JREV, C_LAG, C_MASK = 0, 128, 256, 264, 296
C_COUNT = C_MASK + 128
C_TOKEN = C_COUNT + 72
C_TABLE1 = C_TOKEN + 64
C_END = C_TABLE1 + 32
R_BQKV, R_BOUT, R_GAMMA, R_BETA = 0, 384, 640, 768
R_BO = 896
R_END = R_BO + D


class Chain:

    def __init__(self, engine, sem, first=0):
        self.engine, self.sem, self.first, self.n = engine, sem, first, 0

    def did(self, instruction):
        instruction.then_inc(self.sem, 1)
        self.n += 1

    def settle(self):
        self.engine.wait_ge(self.sem, self.first + self.n)

    def link(self, instruction):
        self.did(instruction)
        self.settle()


@contextmanager
def stage(nc, prefix, names):
    sems = {n: nc.alloc_semaphore(prefix + n) for n in names}
    with nc.Block() as block:
        yield sems, block
    nc.clear_and_free_semaphores(list(sems.values()))
    nc.all_engine_barrier()




def wait_from(engine, sem, value):
    if isinstance(value, int) and value <= 0:
        return
    engine.wait_ge(sem, value)


def staggered(engine, steps, count=GROUPS, buffers=2):
    peeled = 4
    for i in range(peeled):
        for step, lag in steps:
            if i >= lag:
                step(i - lag, (i - lag) % buffers)
    with engine.Fori(0, (count - peeled) // buffers) as r:
        for u in range(buffers):
            for step, lag in steps:
                step(r * buffers + (u + peeled - lag), (u - lag) % buffers)
    for i in range(count, count + max(lag for _, lag in steps)):
        for step, lag in steps:
            if i - lag < count:
                step(i - lag, (i - lag) % buffers)


def build(nc, a, out):
    with ExitStack() as ctx:
        def sb(name, shape, dt=F32):
            return ctx.enter_context(nc.sbuf_tensor(name, shape, dt))

        ps = ctx.enter_context(nc.psum_tensor("ps", [P, 8, 512], F32))
        stream = sb("stream", [P, TILES, D])
        xT = sb("xT", [P, TOKENS])
        cst = sb("cst", [P, C_END])
        rows = sb("rows", [P, R_END])
        ident16 = sb("ident16", [P, P], F16)
        weights = sb("weights", [P, TILES, WCOLS])
        power = sb("power", [P, GROUP])
        post = sb("post", [P, 1])
        rowbuf = sb("rowbuf", [P, TILES, ROW])
        slots = sb("slots", [P, 2, TILES], mybir.dt.int32)
        table = sb("table", [P, LOTS[0]])
        table_int = sb("table_int", [P, LOTS[0]], mybir.dt.int32)
        slot_dram = [nc.dram_tensor(f"slots{i}", [(LOTS[i] * LOT + i * TOKENS), ROW], F32).ap() for i in range(2)]
        y_dram = [nc.dram_tensor(f"y{i}", [3 * TOKENS + LOTS[i] * LOT, D], F32).ap() for i in range(2)]
        kernel_dram = nc.dram_tensor("conv_kernel", [P, KPAD], F32).ap()
        ident = cst[:, C_ID:C_ID + P]
        m = dict(ps=ps, stream=stream, xT=xT, cst=cst, rows=rows, ident=ident, ident16=ident16,
                 weights=weights, power=power, post=post, kernel_dram=kernel_dram, rowbuf=rowbuf,
                 slots=slots, table=table, table_int=table_int, slot_dram=slot_dram, y_dram=y_dram,
                 xn=rowbuf[:, :, 0:D])

        m["blank"] = sb("blank", [P, 2, BLANK, ROW])
        m["taps"] = sb("taps", [P, LOW, LOW])
        m["zero"] = sb("zero", [P, P])
        for name in ("cleared", "blanked0", "blanked1", "kernel_stored"):
            m[name] = ctx.enter_context(nc.semaphore(name))
        m["x_loaded"] = ctx.enter_context(nc.semaphore("x_loaded"))
        m["packs_loaded"] = ctx.enter_context(nc.semaphore("packs_loaded"))

        load_all(nc, a, m)
        conv_kernel(nc, a, m)
        m["packs"] = sb("packs", [P, E, PACK])
        with ExitStack() as layer:
            m["hsum"] = layer.enter_context(nc.sbuf_tensor("hsum", [HG, B], F32))
            m["gate"] = layer.enter_context(nc.sbuf_tensor("gate", [P, B], F32))
            norm_and_router(nc, a, m)
            top2(nc, a, m)
            attention(nc, a, m)
        grouped(nc, a, m, 0)
        shared(nc, a, m, 0)
        convolve(nc, a, m)
        glu_and_norm(nc, a, m)
        norm_and_gate1(nc, a, m)
        top1(nc, a, m)
        shared(nc, a, m, 1)
        grouped(nc, a, m, 1)
        add_routed(nc, m, out.rearrange("(t p) d -> p t d", p=P))


def load_all(nc, a, m):
    with nc.semaphore("loaded") as loaded, nc.Block() as block:
        @block.sync
        def _(sp):
            sp.dma_start(m["cst"][:, :], a["cst"]).then_inc(loaded, 16)
            sp.dma_start(m["rows"][:, :], a["rows"]).then_inc(loaded, 16)
            sp.wait_ge(loaded, 32)

        @block.vector
        def _(dve):
            dve.wait_ge(loaded, 32)
            dve.tensor_copy(m["ident16"][:, :], m["ident"])
            dve.memset(m["power"][:, :], -0.5)


def conv_kernel(nc, a, m):
    ps, cst, ident = m["ps"], m["cst"], m["ident"]
    MAGIC = 1.5 * 2.0 ** 23
    TWO_PI = 2 * np.pi
    C1 = 6.28125
    C2 = float(np.float32(np.round((TWO_PI - C1) * 2 ** 20) / 2 ** 20))
    C3 = float(np.float32(TWO_PI - C1 - C2))
    L2 = 2 * LOW
    with ExitStack() as ctx:
        def sb(name, shape, dt=F32):
            return ctx.enter_context(nc.sbuf_tensor(name, shape, dt))

        s4 = sb("s4", [P, 4 * NS + 2])
        small = sb("small", [P, 16, NS])
        big = [sb(f"big{i}", [P, L2, NS]) for i in range(5)]
        pair = sb("pair", [P, L2, 2, NS])
        pairT = sb("pairT", [P, 2, D, LOW])
        dcol = sb("dcol", [P, 8, LOW])
        pick = sb("pick", [P, LOW, 8, LOW])
        taps, zero, blank = m["taps"], m["zero"], m["blank"]
        dt1 = sb("dt1", [P, 1])
        sem, block = ctx.enter_context(stage(nc, "k_",
            ("loaded", "dt", "args", "expo", "sine", "pair", "turned", "copied", "product", "taps",
                "zeroed", "cleaned", "blank", "numbered", "chain")))
        are, aim, cre, cim = (s4[:, NS * i:NS * (i + 1)] for i in range(4))
        log_dt, skip = s4[:, 4 * NS:4 * NS + 1], s4[:, 4 * NS + 1:4 * NS + 2]
        phase, decay, turns, cosine, scratch = big
        masked = scratch[:, :, :].rearrange("p l n -> p (l n)").rearrange("p (g c) -> p g c", g=LOW)
        lag = cst[:, C_LAG:C_LAG + L2].unsqueeze(2).broadcast_to([P, L2, NS])

        def store_kernel(engine, channels):
            for h in channels:
                engine.dma_start(m["kernel_dram"][h::8, 0:T].rearrange("g (i j) -> i g j", j=LOW),
                                 taps[LOW * h:LOW * h + LOW, :, :]).then_inc(m["kernel_stored"], 16)

        @block.sync
        def _(sp):
            sp.dma_start(s4[:, :], a["s4"]).then_inc(sem["loaded"], 16)
            sp.dma_start(m["stream"][:, :, :], a["x"].rearrange("(t p) d -> p t d", p=P))\
              .then_inc(m["x_loaded"], 16)
            sp.wait_ge(sem["blank"], 1)
            rows = BLANK * P
            for n, (i, k) in enumerate(BLANK_CHUNKS):
                sp.wait_ge(sem["numbered"], n + 1)
                sp.dma_start(m["slot_dram"][i][rows * k:rows * (k + 1), :].rearrange("(p j) d -> p j d", p=P),
                             blank[:, n % 2, :, :]).then_inc(m[f"blanked{n % 2}"], 16)
            for k in range(TOKENS // rows):
                sp.dma_start(m["y_dram"][1][rows * k:rows * (k + 1), :].rearrange("(p j) d -> p j d", p=P),
                             blank[:, 0, :, 0:D]).then_inc(m["cleared"], 16)
            sp.wait_ge(sem["taps"], 1)
            store_kernel(sp, range(4, 8))

        @block.gpsimd
        def _(pool):
            pool.memset(blank[:, :, :, :], 0.0).then_inc(sem["cleaned"], 1)
            pool.wait_ge(sem["cleaned"], 1)
            pool.memset(blank[:, :, :, ROW_E1:ROW], -1.0).then_inc(sem["blank"], 1)
            pool.wait_ge(sem["blank"], 1)
            for n, (i, k) in enumerate(BLANK_CHUNKS):
                if n >= 2:
                    pool.wait_ge(m[f"blanked{n % 2}"], 16 * (n // 2))
                pool.iota(blank[:, n % 2, :, ROW_ID], pattern=[[1, BLANK]], base=2 * TOKENS + BLANK * P * k,
                          channel_multiplier=BLANK, allow_small_or_imprecise_dtypes=True)\
                    .then_inc(sem["numbered"], 1)

        @block.scalar
        def _(act):
            act.wait_ge(sem["loaded"], 16)
            act.activation(dt1[:, :], log_dt, ACT.Exp).then_inc(sem["dt"], 1)
            act.wait_ge(sem["args"], 1)
            act.activation(decay[:, :, :], decay[:, :, :], ACT.Exp).then_inc(sem["expo"], 1)
            act.wait_ge(sem["args"], 2)
            act.activation(phase[:, :, :], phase[:, :, :], ACT.Sin)
            act.activation(cosine[:, :, :], cosine[:, :, :], ACT.Sin).then_inc(sem["sine"], 1)
            for q in range(L2 // 4):
                act.wait_ge(sem["turned"], q + 1)
                k = 4 * q % LOW
                act.copy(pairT[:, 4 * q // LOW, :, k:k + 4].rearrange("p h l -> p l h"),
                         ps[:, q % 2, :].rearrange("p (l h) -> p l h", l=4)).then_inc(sem["copied"], 1)
            act.wait_ge(sem["zeroed"], 1)
            act.dma_start(m["kernel_dram"][:, T:KPAD], zero[:, :]).then_inc(m["kernel_stored"], 16)
            act.wait_ge(sem["taps"], 1)
            store_kernel(act, range(0, 4))

        @block.vector
        def _(dve):
            c = Chain(dve, sem["chain"])
            tt, ts = dve.tensor_tensor, dve.tensor_scalar
            dve.memset(zero[:, :], 0.0).then_inc(sem["zeroed"], 1)
            c.did(dve.memset(pick[:, :, :, :], 0.0))
            c.link(dve.memset(dcol[:, :, :], 0.0))
            c.did(dve.tensor_copy(pick[:, :, :, LOW - 1], ident.rearrange("p (g h) -> p g h", g=LOW)))
            dve.wait_ge(sem["dt"], 1)
            c.did(dve.tensor_copy(dcol[:, :, LOW - 1], skip.broadcast_to([P, 8])))
            dre, dim = small[:, 0, :], small[:, 1, :]
            c.did(ts(dre, are, dt1[:, :], None, ALU.mult))
            c.link(ts(dim, aim, dt1[:, :], None, ALU.mult))
            tt(decay[:, :, :], dre.unsqueeze(1).broadcast_to([P, L2, NS]), lag, ALU.mult).then_inc(sem["args"], 1)
            c.link(tt(phase[:, :, :], dim.unsqueeze(1).broadcast_to([P, L2, NS]), lag, ALU.mult))
            c.link(ts(turns[:, :, :], phase[:, :, :], 1 / TWO_PI, MAGIC, ALU.mult, ALU.add))
            c.link(ts(turns[:, :, :], turns[:, :, :], -MAGIC, None, ALU.add))
            for part in (C1, C2, C3):
                c.link(dve.scalar_tensor_tensor(phase[:, :, :], turns[:, :, :], -part, phase[:, :, :],
                                                ALU.mult, ALU.add))
            c.link(ts(scratch[:, :, :], phase[:, :, :], np.pi / 2, -TWO_PI, ALU.is_gt, ALU.mult))
            c.link(dve.scalar_tensor_tensor(cosine[:, :, :], phase[:, :, :], np.pi / 2, scratch[:, :, :],
                                            ALU.add, ALU.add))
            edge = float(np.nextafter(np.float32(np.pi), np.float32(0)))
            c.did(ts(cosine[:, :, :], cosine[:, :, :], edge, -edge, ALU.min, ALU.max))
            ts(phase[:, :, :], phase[:, :, :], edge, -edge, ALU.min, ALU.max).then_inc(sem["args"], 1)
            dve.wait_ge(sem["expo"], 1)
            dve.wait_ge(sem["sine"], 1)
            er, ei = cosine, phase
            c.did(tt(er[:, :, :], cosine[:, :, :], decay[:, :, :], ALU.mult))
            c.link(tt(ei[:, :, :], phase[:, :, :], decay[:, :, :], ALU.mult))
            s = lambda i: small[:, i, :]
            c.did(ts(s(2), er[:, LOW - 2, :], -1.0, None, ALU.add))
            c.did(tt(s(3), are, are, ALU.mult))
            c.did(tt(s(4), aim, aim, ALU.mult))
            c.link(dve.tensor_copy(s(5), ei[:, LOW - 2, :]))
            c.did(tt(s(3), s(3), s(4), ALU.add))
            c.did(tt(s(6), s(2), are, ALU.mult))
            c.did(tt(s(7), s(5), aim, ALU.mult))
            c.did(tt(s(8), s(5), are, ALU.mult))
            c.link(tt(s(9), s(2), aim, ALU.mult))
            c.did(dve.reciprocal(s(3), s(3)))
            c.did(tt(s(6), s(6), s(7), ALU.add))
            c.link(tt(s(8), s(8), s(9), ALU.subtract))
            c.did(tt(s(6), s(6), s(3), ALU.mult))
            c.link(tt(s(8), s(8), s(3), ALU.mult))
            c.did(tt(s(9), cre, s(6), ALU.mult))
            c.did(tt(s(10), cim, s(8), ALU.mult))
            c.did(tt(s(11), cre, s(8), ALU.mult))
            c.link(tt(s(12), cim, s(6), ALU.mult))
            c.did(tt(s(9), s(9), s(10), ALU.subtract))
            c.link(tt(s(11), s(11), s(12), ALU.add))
            ctr = s(9).unsqueeze(1).broadcast_to([P, LOW, NS])
            cti = s(11).unsqueeze(1).broadcast_to([P, LOW, NS])
            lo, hi = slice(0, LOW), slice(LOW, L2)
            c.did(dve.tensor_copy(pair[:, lo, 0, :], er[:, lo, :]))
            c.did(dve.tensor_copy(pair[:, lo, 1, :], ei[:, lo, :]))
            c.did(tt(decay[:, lo, :], er[:, hi, :], ctr, ALU.mult))
            c.did(tt(decay[:, hi, :], ei[:, hi, :], cti, ALU.mult))
            c.did(tt(turns[:, lo, :], er[:, hi, :], cti, ALU.mult))
            c.link(tt(turns[:, hi, :], ei[:, hi, :], ctr, ALU.mult))
            c.did(tt(decay[:, lo, :], decay[:, lo, :], decay[:, hi, :], ALU.subtract))
            c.link(tt(turns[:, lo, :], turns[:, lo, :], turns[:, hi, :], ALU.add))
            c.did(ts(pair[:, hi, 0, :], decay[:, lo, :], 2.0, None, ALU.mult))
            c.link(ts(pair[:, hi, 1, :], turns[:, lo, :], -2.0, None, ALU.mult))
            dve.engine_nop().then_inc(sem["pair"], 1)
            dve.wait_ge(sem["product"], 1)
            mask = cst[:, C_MASK:C_MASK + P].unsqueeze(1).broadcast_to([P, LOW, P])
            c.link(tt(masked, ps[:, 4:8, :].rearrange("p k (g c) -> p (k g) c", c=P), mask, ALU.mult))
            dve.tensor_reduce(taps[:, :, :], masked.rearrange("p g (h j) -> p g j h", j=LOW),
                              AX.X, ALU.add).then_inc(sem["taps"], 1)

        @block.tensor
        def _(pe):
            pe.wait_ge(sem["pair"], 1)
            for q in range(L2 // 4):
                if q >= 2:
                    pe.wait_ge(sem["copied"], q - 1)
                for k in range(4):
                    ins = pe.transpose(ps[:, q % 2, P * k:P * k + P],
                                       pair[:, 4 * q + k, :, :].rearrange("p c n -> p (c n)"), ident)
                ins.then_inc(sem["turned"], 1)
            pe.wait_ge(sem["copied"], L2 // 4)
            for g in range(LOW):
                bank = ps[:, 4 + g // 4, P * (g % 4):P * (g % 4) + P]
                lo, hi = (pairT[:, part, 8 * g:8 * g + 8, :].rearrange("p h i -> p (h i)") for part in range(2))
                pe.matmul(bank, hi, lo, start=True, stop=False)
                ins = pe.matmul(bank, pick[:, g, :, :].rearrange("p h i -> p (h i)"),
                                dcol[:, :, :].rearrange("p h j -> p (h j)"), start=False, stop=True)
            ins.then_inc(sem["product"], 1)


def norm_and_router(nc, a, m):
    ps, stream, xT, ident = m["ps"], m["stream"], m["xT"], m["ident"]
    with ExitStack() as ctx:
        def sb(name, shape, dt=F32):
            return ctx.enter_context(nc.sbuf_tensor(name, shape, dt))

        w = sb("w_router", [P, R1 + HG])
        wr2 = sb("wr2", [R1 + 1, E])
        bias = sb("b_router", [HG, 2])
        stats = sb("stats", [P, 2, GROUP, 6])
        mv = sb("mv", [P, 2, GROUP, 2])
        rstd = sb("rstd", [P, 2, GROUP])
        xn = sb("xn", [P, 2, GROUP, D])
        hidden = sb("hidden", [R1 + 1, 2, GN])
        junk = sb("junk", [HG, 4, T])
        sem, block = ctx.enter_context(stage(nc, "n_",
            ("loaded", "ones", "kept", "xn_ready", "turned", "xT_ready", "hidden_ready", "relu_ready", "gelu_done",
                "logits_ready", "logits_copied", "stats", "moments", "raised", "rstd")))

        @block.sync
        def _(sp):
            sp.dma_start(w[:, :], a["w_router"]).then_inc(sem["loaded"], 16)
            sp.dma_start(wr2[:, :], a["wr2"]).then_inc(sem["loaded"], 16)
            sp.dma_start(bias[:, :], a["b_router"]).then_inc(sem["loaded"], 16)
            sp.wait_ge(m["cleared"], 16 * (TOKENS // (BLANK * P)))
            for u in range(2):
                sp.wait_ge(m[f"blanked{u}"], 16 * len(BLANK_CHUNKS[u::2]))

        @block.gpsimd
        def _(pool):
            def root(g, u):
                inverse_root(pool, sem, g, rstd[:, u], m["power"])

            def keep(g, u):
                pool.wait_ge(sem["xn_ready"], g + 1)
                pool.tensor_copy(m["xn"][:, bass.ds(g * GROUP, GROUP), :], xn[:, u, :, :])\
                    .then_inc(sem["kept"], 1)

            staggered(pool, [(root, 0), (keep, 1)])

        @block.vector
        def _(dve):
            dve.memset(hidden[R1:R1 + 1, :, :], 1.0).then_inc(sem["ones"], 1)

            def measure(g, u):
                moments(dve, sem, g, stream, g * GROUP, stats[:, u], mv[:, u], rstd[:, u], m["post"], EPS)

            def normalise(g, u):
                dve.wait_ge(sem["rstd"], g + 1)
                wait_from(dve, sem["turned"], g - 1)
                wait_from(dve, sem["kept"], g - 1)
                for k in range(GROUP):
                    ins = dve.tensor_scalar(xn[:, u, k, :], tile_of(stream, g * GROUP + k),
                                            mv[:, u, k, 0:1], rstd[:, u, k:k + 1], ALU.subtract, ALU.mult)
                ins.then_inc(sem["xn_ready"], 1)

            def take_logits(g, u):
                dve.wait_ge(sem["logits_ready"], g + 1)
                dve.tensor_copy(m["weights"][:, bass.ds(g * GROUP, GROUP), 0:E],
                                ps[:, 6 + u, 0:GROUP * E].rearrange("p (k e) -> p k e", e=E))\
                   .then_inc(sem["logits_copied"], 1)

            dve.wait_ge(m["x_loaded"], 16)
            staggered(dve, [(measure, 0), (normalise, 1), (take_logits, 4)])

        @block.tensor
        def _(pe):
            pe.wait_ge(sem["loaded"], 48)
            pe.wait_ge(sem["ones"], 1)

            def turn(g, u):
                pe.wait_ge(sem["xn_ready"], g + 1)
                wait_from(pe, sem["xT_ready"], g - 1)
                for k in range(GROUP):
                    ins = pe.transpose(ps[:, u, P * k:P * k + P], xn[:, u, k, :], ident)
                ins.then_inc(sem["turned"], 1)

            def make_hidden(g, u):
                pe.wait_ge(sem["xT_ready"], g + 1)
                wait_from(pe, sem["gelu_done"], g - 1)
                xg = xT[:, bass.ds(g * GN, GN)]
                pe.matmul(ps[0:R1, 2 + u, :], w[:, 0:R1], xg, start=True, stop=True)
                pe.matmul(ps[0:HG, 4 + u, :], w[:, R1:R1 + HG], xg, start=True, stop=True)\
                  .then_inc(sem["hidden_ready"], 1)

            def make_logits(g, u):
                pe.wait_ge(sem["relu_ready"], g + 1)
                wait_from(pe, sem["logits_copied"], g - 1)
                for k in range(GROUP):
                    ins = pe.matmul(ps[:, 6 + u, E * k:E * k + E], hidden[:, u, P * k:P * k + P], wr2[:, :],
                                    start=True, stop=True)
                ins.then_inc(sem["logits_ready"], 1)

            staggered(pe, [(turn, 0), (make_hidden, 1), (make_logits, 2)])

        @block.scalar
        def _(act):
            act.wait_ge(sem["loaded"], 48)

            def take_xT(g, u):
                act.wait_ge(sem["turned"], g + 1)
                act.copy(xT[:, bass.ds(g * GN, GN)], ps[:, u, :]).then_inc(sem["xT_ready"], 1)

            def activate(g, u):
                act.wait_ge(sem["hidden_ready"], g + 1)
                wait_from(act, sem["logits_ready"], g - 1)
                act.activation(hidden[0:R1, u, :], ps[0:R1, 2 + u, :], ACT.Relu, bias=bias[0:R1, 0:1])\
                   .then_inc(sem["relu_ready"], 1)
                for j in range(2):
                    ins = act.activation(junk[:, 2 * u + j, :], ps[0:HG, 4 + u, T * j:T * j + T], ACT.Gelu,
                                         bias=bias[:, 1:2],
                                         accum_out=m["hsum"][:, bass.ds(g * 2 + j, 1)])
                ins.then_inc(sem["gelu_done"], 1)

            staggered(act, [(take_xT, 0), (activate, 1)])


def first_of(c, dve, mask, value, best, tmp, jrev):
    wide = lambda t: t.unsqueeze(2).broadcast_to([P, TILES, E])
    c.link(dve.tensor_reduce(best[:, :], value[:, :, :], AX.X, ALU.max))
    c.link(dve.tensor_tensor(mask[:, :, :], value[:, :, :], wide(best[:, :]), ALU.is_equal))
    c.link(dve.tensor_tensor(mask[:, :, :], mask[:, :, :], jrev, ALU.mult))
    c.link(dve.tensor_reduce(tmp[:, :], mask[:, :, :], AX.X, ALU.max))
    c.link(dve.tensor_tensor(mask[:, :, :], jrev, wide(tmp[:, :]), ALU.is_equal))


def softmax_parts(c, dve, act_done, args_ready, logits, top, z, total):
    wide = lambda t: t.unsqueeze(2).broadcast_to(list(z.shape))
    c.link(dve.tensor_reduce(top[:, :], logits, AX.X, ALU.max))
    dve.tensor_tensor(z[:, :, :], logits, wide(top[:, :]), ALU.subtract).then_inc(args_ready, 1)
    dve.wait_ge(act_done[0], act_done[1])
    c.link(dve.tensor_reduce(total[:, :], z[:, :, :], AX.X, ALU.add))
    c.link(dve.reciprocal(total[:, :], total[:, :]))
    c.link(dve.tensor_tensor(z[:, :, :], z[:, :, :], wide(total[:, :]), ALU.mult))


def top2(nc, a, m):
    ps, cst, weights = m["ps"], m["cst"], m["weights"]
    with ExitStack() as ctx:
        def sb(name, shape, dt=F32):
            return ctx.enter_context(nc.sbuf_tensor(name, shape, dt))

        z = sb("z", [P, TILES, E])
        mask1, mask2 = sb("mask1", [P, TILES, E]), sb("mask2", [P, TILES, E])
        v = [sb(f"v{i}", [P, TILES]) for i in range(5)]
        wg2 = sb("wg2", [HG, P])
        gb = sb("gb", [P, 2])
        gs = sb("gs", [P, 1])
        ones = sb("ones2", [P, P])
        chosen, place = sb("chosen", [P, TILES, E]), sb("place2", [P, TILES, E])
        before = sb("before2", [P, E, TILES])
        lots = sb("lots", [P, 4, E])
        reached = sb("reached", [P, LOTS[0], E])
        sem, block = ctx.enter_context(stage(nc, "t_",
            ("loaded", "args", "expo", "gate", "gated", "mask", "counts", "chain")))
        jrev = cst[:, C_JREV:C_JREV + E].unsqueeze(1).broadcast_to([P, TILES, E])

        @block.sync
        def _(sp):
            sp.dma_start(wg2[:, :], a["wg2"]).then_inc(sem["loaded"], 16)
            sp.dma_start(gb[:, :], a["gate_bias"]).then_inc(sem["loaded"], 16)

        @block.tensor
        def _(pe):
            pe.wait_ge(sem["loaded"], 32)
            pe.matmul(ps[:, 0, 0:B], wg2[:, :], m["hsum"][:, :], start=True, stop=True).then_inc(sem["gate"], 1)
            count(pe, m, sem, chosen, ones)

        @block.scalar
        def _(act):
            act.wait_ge(sem["loaded"], 32)
            act.wait_ge(sem["gate"], 1)
            act.activation(m["gate"][:, :], ps[:, 0, 0:B], ACT.Sigmoid, bias=gb[:, 0:1], scale=1.0 / T)
            act.activation(gs[:, :], gb[:, 1:2], ACT.Sigmoid).then_inc(sem["gated"], 1)
            act.wait_ge(sem["args"], 1)
            act.activation(z[:, :, :], z[:, :, :], ACT.Exp).then_inc(sem["expo"], 1)
            act.wait_ge(sem["args"], 2)
            act.activation(v[2][:, :], v[2][:, :], ACT.Exp, scale=0.5).then_inc(sem["expo"], 1)

        @block.vector
        def _(dve):
            c = Chain(dve, sem["chain"])
            tt, ts = dve.tensor_tensor, dve.tensor_scalar
            dve.wait_ge(sem["gated"], 1)
            c.did(ts(m["gate"][:, :], m["gate"][:, :], gs[:, :], None, ALU.mult))
            softmax_parts(c, dve, (sem["expo"], 1), sem["args"], weights[:, :, 0:E], v[0], z, v[1])
            c.did(dve.memset(ones[:, :], 1.0))
            first_of(c, dve, mask1, z, v[0], v[4], jrev)
            c.did(ts(m["rowbuf"][:, :, ROW_E1], v[4][:, :], -1.0, float(E), ALU.mult, ALU.add))
            c.link(dve.scalar_tensor_tensor(z[:, :, :], mask1[:, :, :], -2.0, z[:, :, :], ALU.mult, ALU.add))
            first_of(c, dve, mask2, z, v[1], v[4], jrev)
            tt(chosen[:, :, :], mask1[:, :, :], mask2[:, :, :], ALU.add).then_inc(sem["mask"], 1)
            tt(v[2][:, :], v[1][:, :], v[0][:, :], ALU.subtract).then_inc(sem["args"], 1)
            dve.wait_ge(sem["expo"], 2)
            c.link(ts(v[3][:, :], v[2][:, :], 1.0, None, ALU.add))
            c.link(dve.reciprocal(v[3][:, :], v[3][:, :]))
            c.link(tt(v[2][:, :], v[2][:, :], v[3][:, :], ALU.mult))
            c.did(tt(m["rowbuf"][:, :, ROW_DW], v[3][:, :], v[2][:, :], ALU.subtract))
            c.did(dve.tensor_copy(m["rowbuf"][:, :, ROW_W2], v[2][:, :]))
            token = cst[:, C_TOKEN:C_TOKEN + TILES]
            c.did(ts(m["rowbuf"][:, :, ROW_ID], token, float(TOKENS), None, ALU.add))
            dve.wait_ge(sem["counts"], 1)
            places(c, dve, ps, ones, before, place, lots[:, 0, :])
            size, end, start, tmp = (lots[:, k, :] for k in range(4))
            c.link(ts(tmp, size, 1.0 / LOT, 0.5 - 0.5 / LOT, ALU.mult, ALU.add))
            c.link(ts(tmp, tmp, 1.5 * 2.0 ** 23, None, ALU.add))
            c.link(ts(tmp, tmp, -1.5 * 2.0 ** 23, None, ALU.add))
            c.link(dve.tensor_tensor_scan(end, ones[:, 0:E], tmp, 0.0, ALU.mult, ALU.add))
            c.link(tt(start, end, tmp, ALU.subtract))
            c.link(dve.scalar_tensor_tensor(place[:, :, :], start.unsqueeze(1).broadcast_to([P, TILES, E]),
                                            float(LOT), place[:, :, :], ALU.mult, ALU.add))
            for choice, mask in enumerate((mask1, mask2)):
                c.link(tt(z[:, :, :], mask[:, :, :], place[:, :, :], ALU.mult))
                c.link(dve.tensor_reduce(v[4][:, :], z[:, :, :], AX.X, ALU.add))
                c.link(dve.tensor_copy(m["slots"][:, choice, :], v[4][:, :]))
            n = LOTS[0]
            c.link(tt(reached[:, :, :], cst[:, C_COUNT:C_COUNT + n].unsqueeze(2).broadcast_to([P, n, E]),
                      end.unsqueeze(1).broadcast_to([P, n, E]), ALU.is_ge))
            c.link(dve.tensor_reduce(m["table"][:, :], reached[:, :, :], AX.X, ALU.add))
            c.link(ts(m["table"][:, :], m["table"][:, :], float(E - 1), None, ALU.min))
            c.did(dve.tensor_copy(m["table_int"][:, :], m["table"][:, :]))


def attention(nc, a, m):
    ps, stream, xT, ident, ident16 = m["ps"], m["stream"], m["xT"], m["ident"], m["ident16"]
    with ExitStack() as ctx:
        def sb(name, shape, dt=F32):
            return ctx.enter_context(nc.sbuf_tensor(name, shape, dt))

        wqkv = sb("wqkv", [P, 3 * D])
        wo = sb("wo", [D, D])
        xs = sb("xs", [P, 2, T])
        qk = sb("qk", [P, 2, 2 * D])
        sq = sb("sq", [P, 2, 2 * D])
        rn, guess, root = sb("rn", [P, 4 * H]), sb("guess", [P, 4 * H]), sb("root", [P, 4 * H])
        stack = [sb("q_stack", [P, 2 * H, 4, DK], F16), sb("k_stack", [P, 2 * H, 4, DK], F16)]
        stackT = [sb("q_stackT", [P, 2, 4, T], F16), sb("k_stackT", [P, 2, 4, T], F16)]
        vext = sb("vext", [P, 2, 2, H, VW])
        probs = sb("probs", [P, 2, 2, 2, T])
        oT = sb("oT", [P, 4, T])
        rsum = sb("rsum", [P, 2, H])
        on = sb("on", [P, 2, D])
        onT = sb("onT", [P, T])
        sem, block = ctx.enter_context(stage(nc, "a_",
            ("loaded", "v_zero", "v_ready", "xs_ready", "projected", "qkv_ready", "squared", "summed",
                "norms", "highs", "normal", "turned", "stacked", "rsum", "stackT_ready", "scores", "probs", "pv", "oT_ready", "out_turned", "on_ready",
                "on_turned", "onT_ready", "mixed", "added", "scattered")))
        xb = ps[:, 4:6, :]

        def take_stack(copy, which, par):
            copy(stackT[which][:, par, :, :], xb[:, which, :].bitcast(F16).rearrange("p (g t) -> p g t", t=T))\
                .then_inc(sem["stackT_ready"], 1)

        def over_batches(engine, body):
            body(0, 0)
            with engine.Fori(0, B // 2 - 2) as i:
                body(i * 2 + 1, 1)
                body(i * 2 + 2, 0)
            for b in range(B - 3, B):
                body(b, b % 2)

        def lacks(b, n):
            return isinstance(b, int) and not 0 <= b + n < B

        @block.sync
        def _(sp):
            sp.dma_start(wqkv[:, :], a["wqkv"]).then_inc(sem["loaded"], 16)
            sp.dma_start(wo[:, :], a["wo"]).then_inc(sem["loaded"], 16)
            sp.dma_start(m["packs"][:, :, :], a["experts0"][:, 0:E, :]).then_inc(m["packs_loaded"], 16)

        @block.tensor
        def _(pe):
            def project(b, par):
                wait_from(pe, sem["stackT_ready"], 2 * b)
                pe.wait_ge(sem["xs_ready"], b + 1)
                for t in range(2):
                    ins = pe.matmul(xb[:, t, 0:3 * D], xs[:, par, P * t:P * t + P], wqkv[:, :], start=True, stop=True)
                ins.then_inc(sem["projected"], 1)

            def turn_stacks(b):
                pe.wait_ge(sem["stacked"], b + 1)
                wait_from(pe, sem["added"], b - 1)
                for which in range(2):
                    bank = xb[:, which, :].bitcast(F16)
                    for g in range(4):
                        for t in range(2):
                            ins = pe.transpose(bank[:, g * T + t * P:g * T + t * P + P],
                                               stack[which][:, t * H + 4 * g:t * H + 4 * g + 4, :, :]
                                               .rearrange("p h s d -> p (h s d)"), ident16[:, :])
                ins.then_inc(sem["turned"], 1)

            def score(b, par, p):
                if p == 0:
                    pe.wait_ge(sem["stackT_ready"], 2 * b + 2)
                wait_from(pe, sem["probs"], b * PAIRS + p - 1)
                for kt in range(2):
                    for j in range(2):
                        g, r = divmod(2 * p + j, 4)
                        rows = slice(32 * r, 32 * r + 32)
                        ins = pe.matmul(ps[:, 2 * (p % 2) + j, kt * T:kt * T + T],
                                        stackT[1][rows, par, g, kt * P:kt * P + P],
                                        stackT[0][rows, par, g, :], start=True, stop=True,
                                        tile_position=(32 * r, 0))
                ins.then_inc(sem["scores"], 1)

            def weigh(b, par, p):
                pe.wait_ge(sem["probs"], b * PAIRS + p + 1)
                if p % 4 == 0:
                    wait_from(pe, sem["oT_ready"], 2 * b - 1 + p // 4)
                for kt in range(2):
                    for j in range(2):
                        g, r = divmod(2 * p + j, 4)
                        ins = pe.matmul(ps[32 * r:32 * r + 32, 6 + g // 2, (g % 2) * T:(g % 2) * T + T],
                                        vext[:, par, kt, 2 * p + j, :], probs[:, p % 2, j, kt, :],
                                        start=(kt == 0), stop=(kt == 1), tile_position=(0, 32 * r),
                                        skip_group_check=True)
                ins.then_inc(sem["pv"], 1)

            def turn_out(b):
                pe.wait_ge(sem["oT_ready"], 2 * b + 2)
                if not lacks(b, 2):
                    pe.wait_ge(sem["qkv_ready"], b + 3)
                elif lacks(b, 1):
                    pe.wait_ge(sem["added"], B - 1)
                for t in range(2):
                    for g in range(4):
                        ins = pe.transpose(xb[:, t, P * g:P * g + P], oT[:, g, P * t:P * t + P], ident)
                ins.then_inc(sem["out_turned"], 1)

            def turn_normal(b):
                pe.wait_ge(sem["on_ready"], b + 1)
                for t in range(2):
                    ins = pe.transpose(xb[:, 0, P * t:P * t + P], on[:, t, :], ident)
                ins.then_inc(sem["on_turned"], 1)

            def mix(b):
                pe.wait_ge(sem["onT_ready"], b + 1)
                for t in range(2):
                    ins = pe.matmul(xb[:, 1, P * t:P * t + P], onT[:, P * t:P * t + P], wo[:, :],
                                    start=True, stop=True)
                ins.then_inc(sem["mixed"], 1)

            def body(b, par):
                for p in range(PAIRS):
                    if p + 1 < PAIRS:
                        score(b, par, p + 1)
                    if p == 0 and not lacks(b, -1):
                        turn_out(b - 1)
                    if p == 3 and not lacks(b, -1):
                        turn_normal(b - 1)
                    if p == 5 and not lacks(b, -1):
                        mix(b - 1)
                    if p == 7 and not lacks(b, 1):
                        turn_stacks(b + 1)
                    weigh(b, par, p)
                if not lacks(b, 2):
                    project(b + 2, par)
                if not lacks(b, 1):
                    score(b + 1, 1 - par, 0)

            pe.wait_ge(sem["loaded"], 32)
            pe.wait_ge(sem["v_ready"], 1)
            project(0, 0)
            turn_stacks(0)
            score(0, 0, 0)
            project(1, 1)
            over_batches(pe, body)
            turn_out(B - 1)
            turn_normal(B - 1)
            mix(B - 1)

        @block.scalar
        def _(act):
            def slice_x(b, par):
                wait_from(act, sem["projected"], b - 1)
                act.copy(xs[:, par, :], xT[:, bass.ds(b * T, T)]).then_inc(sem["xs_ready"], 1)

            def take_k(b, par):
                act.wait_ge(sem["turned"], b + 1)
                take_stack(act.copy, 1, par)

            def body(b, par):
                for p in range(PAIRS):
                    if p == 4 and not lacks(b, 2):
                        slice_x(b + 2, par)
                    act.wait_ge(sem["scores"], b * PAIRS + p + 1)
                    wait_from(act, sem["pv"], b * PAIRS + p - 1)
                    act.activation(probs[:, p % 2, :, :, :].rearrange("p j k t -> p j (k t)"),
                                   ps[:, 2 * (p % 2):2 * (p % 2) + 2, :], ACT.Exp,
                                   scale=DK ** -0.5).then_inc(sem["probs"], 1)
                if not lacks(b, 1):
                    take_k(b + 1, 1 - par)

            slice_x(0, 0)
            slice_x(1, 1)
            take_k(0, 0)
            over_batches(act, body)

        @block.gpsimd
        def _(pool):
            def scatter(b):
                for t in range(2):
                    for choice in range(2):
                        scatter_tile(pool, m, 0, 2 * b + t, choice).then_inc(sem["scattered"], 16)

            for b in range(B):
                scatter(b)
            pool.wait_ge(sem["scattered"], 16 * 2 * TILES)

        @block.vector
        def _(dve):
            def take_qkv(b, par):
                dve.wait_ge(sem["projected"], b + 1)
                wait_from(dve, sem["pv"], (b - 1) * PAIRS)
                rows = m["rows"]
                wide = rows[:, R_BQKV:R_BQKV + 2 * D].unsqueeze(1).broadcast_to([P, 2, 2 * D])
                dve.tensor_tensor(qk[:, :, :], xb[:, :, 0:2 * D], wide, ALU.add)
                for t in range(2):
                    ins = dve.tensor_tensor(
                        vext[:, par, t, :, 0:DK],
                        xb[:, t, 2 * D:3 * D].rearrange("p (h d) -> p h d", d=DK),
                        rows[:, R_BQKV + 2 * D:R_BQKV + 3 * D].rearrange("p (h d) -> p h d", d=DK), ALU.add)
                ins.then_inc(sem["qkv_ready"], 1)

            def norms(b):
                dve.wait_ge(sem["qkv_ready"], b + 1)
                dve.tensor_tensor(sq[:, :, :], qk[:, :, :], qk[:, :, :], ALU.mult).then_inc(sem["squared"], 1)
                dve.wait_ge(sem["squared"], b + 1)
                dve.tensor_reduce(rn[:, :], sq[:, :, :].rearrange("p t (h d) -> p (t h) d", d=DK),
                                  AX.X, ALU.add).then_inc(sem["summed"], 1)

            def roots(b):
                dve.wait_ge(sem["summed"], b + 1)
                inverse_roots(Chain(dve, sem["norms"], b * ROOT_STEPS), rn, guess, root)

            def unit(b):
                dve.tensor_tensor(sq[:, :, :].rearrange("p t (h d) -> p (t h) d", d=DK),
                                  qk[:, :, :].rearrange("p t (h d) -> p (t h) d", d=DK),
                                  root[:, :].unsqueeze(2).broadcast_to([P, 4 * H, DK]),
                                  ALU.mult).then_inc(sem["normal"], 1)

            def split(b):
                dve.wait_ge(sem["normal"], b + 1)
                wait_from(dve, sem["turned"], b)
                highs = []
                for which, high in ((0, slice(0, 4, 2)), (1, slice(0, 4, 3))):
                    x3 = sq[:, :, :].rearrange("p t (w h d) -> p t w h d", w=2, d=DK)[:, :, which, :, :]
                    for t in range(2):
                        wide = x3[:, t].unsqueeze(2).broadcast_to([P, H, 2, DK])
                        highs.append((which, high, t, wide))
                for which, high, t, wide in highs:
                    ins = dve.tensor_copy(stack[which][:, t * H:t * H + H, high, :], wide)
                ins.then_inc(sem["highs"], 1)
                dve.wait_ge(sem["highs"], b + 1)
                for which, high, t, wide in highs:
                    low = slice(1, 4, 2) if which == 0 else slice(1, 3)
                    s = stack[which][:, t * H:t * H + H, :, :]
                    ins = dve.tensor_tensor(s[:, :, low, :], wide,
                                            s[:, :, 0:1, :].broadcast_to([P, H, 2, DK]), ALU.subtract)
                ins.then_inc(sem["stacked"], 1)

            def take_q(b, par):
                dve.wait_ge(sem["turned"], b + 1)
                take_stack(dve.tensor_copy, 0, par)


            def take_out(b, half):
                dve.wait_ge(sem["pv"], b * PAIRS + 4 * half + 4)
                wait_from(dve, sem["out_turned"], b)
                dve.tensor_copy(oT[:, 2 * half:2 * half + 2, :], ps[:, 6 + half, :].rearrange(
                    "p (g t) -> p g t", t=T)).then_inc(sem["oT_ready"], 1)

            def normalise(b):
                dve.wait_ge(sem["out_turned"], b + 1)
                o = xb[:, :, :].rearrange("p t (h e) -> p t h e", e=VW)
                dve.reciprocal(rsum[:, :, :], o[:, :, :, DK]).then_inc(sem["rsum"], 1)
                dve.wait_ge(sem["rsum"], b + 1)
                for t in range(2):
                    ins = dve.tensor_tensor(on[:, t, :].rearrange("p (h d) -> p h d", d=DK), o[:, t, :, 0:DK],
                                            rsum[:, t, :].unsqueeze(2).broadcast_to([P, H, DK]), ALU.mult)
                ins.then_inc(sem["on_ready"], 1)

            def gate(b):
                dve.wait_ge(sem["on_turned"], b + 1)
                dve.tensor_scalar(onT[:, :], xb[:, 0, 0:T], m["gate"][:, bass.ds(b, 1)], None, ALU.mult)\
                   .then_inc(sem["onT_ready"], 1)

            def add(b):
                dve.wait_ge(sem["mixed"], b + 1)
                s = stream[:, bass.ds(2 * b, 2), :]
                dve.tensor_tensor(s, s, xb[:, 1, 0:T].rearrange("p (t d) -> p t d", d=D), ALU.add)\
                   .then_inc(sem["added"], 1)

            def body(b, par):
                if not lacks(b, 1):
                    take_qkv(b + 1, 1 - par)
                    norms(b + 1)
                if not lacks(b, -1):
                    normalise(b - 1)
                if not lacks(b, 1):
                    roots(b + 1)
                if not lacks(b, -1):
                    gate(b - 1)
                if not lacks(b, 1):
                    unit(b + 1)
                    split(b + 1)
                if not lacks(b, -1):
                    add(b - 1)
                take_out(b, 0)
                if not lacks(b, 1):
                    take_q(b + 1, 1 - par)
                take_out(b, 1)

            dve.memset(vext[:, :, :, :, :], 0.0).then_inc(sem["v_zero"], 1)
            dve.wait_ge(sem["v_zero"], 1)
            dve.memset(vext[:, :, :, :, DK:DK + 1], 1.0).then_inc(sem["v_ready"], 1)
            dve.wait_ge(sem["v_ready"], 1)
            take_qkv(0, 0)
            norms(0)
            roots(0)
            unit(0)
            split(0)
            take_q(0, 0)
            over_batches(dve, body)
            normalise(B - 1)
            gate(B - 1)
            add(B - 1)


def count(pe, m, sem, chosen, ones):
    pe.wait_ge(sem["mask"], 1)
    flat = chosen[:, :, :].rearrange("p t e -> p (t e)")
    pe.matmul(m["ps"][:, 1, :], m["cst"][:, C_TRI:C_TRI + P], flat, start=True, stop=True)
    pe.matmul(m["ps"][:, 2, :], ones[:, :], flat, start=True, stop=True).then_inc(sem["counts"], 1)


def places(c, dve, ps, ones, before, place, total):
    totals = ps[:, 2, :].rearrange("p (t e) -> p e t", e=E)
    for e in range(E):
        ins = dve.tensor_tensor_scan(before[:, e, :], ones[:, 0:TILES], totals[:, e, :], 0.0, ALU.mult, ALU.add)
    c.link(ins)
    c.link(dve.tensor_copy(total, before[:, :, TILES - 1]))
    c.link(dve.tensor_tensor(before[:, :, :], before[:, :, :], totals, ALU.subtract))
    c.link(dve.tensor_tensor(place[:, :, :], ps[:, 1, :].rearrange("p (t e) -> p t e", e=E),
                             before[:, :, :].rearrange("p e t -> p t e"), ALU.add))


def scatter_tile(pool, m, layer, tile, choice):
    where = m["slots"][:, choice, tile:tile + 1]
    return pool.indirect_dma_start(m["slot_dram"][layer], bass.IndirectOffsetOnAxis(ap=where, axis=0),
                                   m["rowbuf"][:, tile, :], None)


def grouped(nc, a, m, layer):
    ps, ident = m["ps"], m["ident"]
    lots = LOTS[layer]
    act_func = (ACT.Silu, ACT.Gelu_apprx_tanh)[layer]
    HALVES = LOT // P
    with ExitStack() as ctx:
        def sb(name, shape, dt=F32):
            return ctx.enter_context(nc.sbuf_tensor(f"{name}_{layer}", shape, dt))

        packs = m["packs"]
        own = sb("own", [P, UNROLL, PACK])
        nwb = sb("nwb_g", [P, 2])
        rows = sb("slot_rows", [P, UNROLL, HALVES, ROW])
        xs = sb("slot_x", [P, 2, LOT])
        hidden = sb("slot_h", [P, 2, KI, LOT])
        first = sb("first", [P, UNROLL, HALVES])
        weight = sb("weight", [P, UNROLL, HALVES])
        where = sb("where", [P, UNROLL, HALVES], mybir.dt.int32)
        y = sb("slot_y", [P, UNROLL, HALVES, D])
        sem, block = ctx.enter_context(stage(nc, f"r{layer}_",
            ["loaded", "own_ready", "turned", "x_ready", "upped", "hidden_ready", "downed",
                "first_ready", "picked", "weight_ready", "biased", "y_ready", "y_seen", "y_free"]
               + [f"rows{j}" for j in range(UNROLL)] + [f"sent{j}" for j in range(UNROLL)]))
        slots = m["slot_dram"][layer][0:lots * LOT, :].rearrange("(t p j) d -> p t (j d)", p=P, j=HALVES)

        @block.sync
        def _(sp):
            sp.dma_start(nwb[:, :], a["nwb"]).then_inc(sem["loaded"], 16)
            with sp.Fori(0, lots // UNROLL) as i:
                for j in range(UNROLL):
                    sp.wait_ge(sem["downed"], i * UNROLL + j + 1)
                    sp.wait_ge(sem["weight_ready"], i * UNROLL + j + 1)
                    sp.dma_start(rows[:, j, :, :].rearrange("p h d -> p (h d)"),
                                 slots[:, bass.ds(i * UNROLL + j, 1), :].rearrange("p t d -> p (t d)"))\
                      .then_inc(sem[f"rows{j}"], 16)

        def rows_loaded(t, j):
            return t * (16 // UNROLL) + (16 - 16 // UNROLL * j)

        @block.vector
        def _(dve):
            def get_own(t, j):
                dve.wait_ge(sem["downed"], t + 1)
                e = dve.value_load(m["table_int"][0:1, bass.ds(t, 1)], min_val=0, max_val=E - 1)
                dve.tensor_copy(own[:, j, :], packs[:, bass.ds(e, 1), :].rearrange("p e n -> p (e n)"))\
                    .then_inc(sem["own_ready"], 1)
                dve.wait_ge(sem[f"rows{j}"], rows_loaded(t, j))
                dve.wait_ge(sem["y_free"], t + 1)
                dve.tensor_scalar(first[:, j, :], rows[:, j, :, ROW_E1], m["table"][:, bass.ds(t, 1)], None,
                                  ALU.is_equal).then_inc(sem["first_ready"], 1)
                dve.wait_ge(sem["first_ready"], t + 1)
                dve.scalar_tensor_tensor(where[:, j, :], first[:, j, :], -float(TOKENS), rows[:, j, :, ROW_ID],
                                         ALU.mult, ALU.add)
                dve.tensor_tensor(weight[:, j, :], first[:, j, :], rows[:, j, :, ROW_DW], ALU.mult)\
                    .then_inc(sem["picked"], 1)
                dve.wait_ge(sem["picked"], t + 1)
                dve.tensor_tensor(weight[:, j, :], weight[:, j, :], rows[:, j, :, ROW_W2], ALU.add)\
                    .then_inc(sem["weight_ready"], 1)

            def take_x(t, j):
                dve.wait_ge(sem["turned"], t + 1)
                dve.wait_ge(sem["upped"], (t + 1) * 2)
                x, xT = xs[:, j % 2, :], ps[:, 4 + j % 2, 0:LOT]
                if layer:
                    ins = dve.tensor_scalar(x, xT, nwb[:, 0:1], nwb[:, 1:2], ALU.mult, ALU.add)
                else:
                    ins = dve.tensor_copy(x, xT)
                ins.then_inc(sem["x_ready"], 1)

            def put_y(t, j):
                dve.wait_ge(sem["weight_ready"], t + UNROLL + 1)
                dve.wait_ge(sem["downed"], t + UNROLL + 1)
                dve.tensor_tensor(y[:, j, :, :], ps[:, 6 + j % 2, 0:HALVES * D].rearrange("p (h d) -> p h d", d=D),
                                  own[:, j, P_OUT:PACK].unsqueeze(1).broadcast_to([P, HALVES, D]),
                                  ALU.add).then_inc(sem["biased"], 1)
                dve.wait_ge(sem["biased"], t + 1)
                for h in range(HALVES):
                    ins = dve.tensor_scalar(y[:, j, h, :], y[:, j, h, :], weight[:, j, h:h + 1], None, ALU.mult)
                ins.then_inc(sem["y_ready"], 1)

            dve.sem_inc(sem["x_ready"], 2)
            dve.sem_inc(sem["y_ready"], 2)
            dve.sem_inc(sem["weight_ready"], UNROLL)
            dve.wait_ge(sem["loaded"], 16)
            dve.wait_ge(m["packs_loaded"], 16 * (layer + 1))
            staggered(dve, [(get_own, 0), (take_x, 0), (put_y, 2)], lots, UNROLL)

        @block.gpsimd
        def _(pool):
            pool.sem_inc(sem["y_free"], UNROLL)

            def send(t, j):
                pool.wait_ge(sem["y_ready"], t + 3)
                pool.sem_inc(sem["y_seen"], 1)
                for h in range(HALVES):
                    pool.indirect_dma_start(
                        m["y_dram"][layer], bass.IndirectOffsetOnAxis(ap=where[:, j, h:h + 1], axis=0),
                        y[:, j, h, :], None).then_inc(sem[f"sent{j}"], 16)

            def free(t, j):
                pool.wait_ge(sem[f"sent{j}"], t * (16 * HALVES // UNROLL)
                             + 16 * HALVES // UNROLL * (UNROLL - j))
                pool.sem_inc(sem["y_free"], 1)

            staggered(pool, [(free, 2), (send, 0)], lots, UNROLL)

        @block.tensor
        def _(pe):
            pe.sem_inc(sem["downed"], UNROLL)
            pe.sem_inc(sem["upped"], 4)

            def turn(t, j):
                pe.wait_ge(sem[f"rows{j}"], rows_loaded(t, j))
                pe.wait_ge(sem["x_ready"], t + 1)
                for h in range(HALVES):
                    ins = pe.transpose(ps[:, 4 + j % 2, P * h:P * h + P], rows[:, j, h, 0:D], ident)
                ins.then_inc(sem["turned"], 1)

            def make_hidden(t, j):
                pe.wait_ge(sem["x_ready"], t + 3)
                pe.wait_ge(sem["own_ready"], t + 1)
                pe.wait_ge(sem["hidden_ready"], t + 1)
                for k in range(KI):
                    ins = pe.matmul(ps[:, 2 * (j % 2) + k // 2, (k % 2) * LOT:(k % 2) * LOT + LOT],
                                    own[:, j, P * k:P * k + P], xs[:, j % 2, :], start=True, stop=True)
                    if k % 2 == 1:
                        ins.then_inc(sem["upped"], 1)

            def make_out(t, j):
                pe.wait_ge(sem["hidden_ready"], t + 3)
                pe.wait_ge(sem["y_ready"], t + 1)
                for h in range(HALVES):
                    for k in range(KI):
                        n = INTER + D * k
                        ins = pe.matmul(ps[:, 6 + j % 2, P * h:P * h + P], hidden[:, j % 2, k, P * h:P * h + P],
                                        own[:, j, n:n + D], start=(k == 0), stop=(k == KI - 1))
                ins.then_inc(sem["downed"], 1)

            staggered(pe, [(turn, 0), (make_hidden, 1), (make_out, 2)], lots, UNROLL)

        @block.scalar
        def _(act):
            act.sem_inc(sem["hidden_ready"], 2)

            def activate(t, j):
                act.wait_ge(sem["downed"], t + UNROLL - 1)
                for k in range(KI):
                    if k % 2 == 0:
                        act.wait_ge(sem["upped"], t * 2 + (k // 2 + 5))
                    ins = act.activation(hidden[:, j % 2, k, :],
                                         ps[:, 2 * (j % 2) + k // 2, (k % 2) * LOT:(k % 2) * LOT + LOT],
                                         act_func, bias=own[:, j, P_BIAS + k:P_BIAS + k + 1])
                ins.then_inc(sem["hidden_ready"], 1)

            staggered(act, [(activate, 0)], lots, UNROLL)


def shared(nc, a, m, layer):
    ps, stream, xT, weights = m["ps"], m["stream"], m["xT"], m["weights"]
    act_func = (ACT.Silu, ACT.Gelu_apprx_tanh)[layer]
    with ExitStack() as ctx:
        def sb(name, shape, dt=F32):
            return ctx.enter_context(nc.sbuf_tensor(f"{name}_{layer}", shape, dt))

        pack = sb("pack", [P, PACK])
        out_bias = sb("out_bias", [P, D])
        hidden = sb("h", [P, 2, KI, GN])
        result = sb("result", [P, 2, GROUP, D])
        routed = None if layer else sb("routed", [P, 2, 2, GROUP, D])
        stats, mv, rstd = sb("stats_n", [P, 2, GROUP, 6]), sb("mv_n", [P, 2, GROUP, 2]), sb("rstd_n", [P, 2, GROUP])
        sem, block = ctx.enter_context(stage(nc, f"e{layer}_",
            ("loaded", "upped", "hidden_ready", "downed", "bias_ready", "summed",
                "added", "chain", "routed0", "routed1", "stats", "moments", "raised", "rstd",
                "added_seen", "scattered")))
        y = m["y_dram"][0][0:2 * TOKENS, :].rearrange("(c t p) d -> c p t d", c=2, p=P)

        @block.sync
        def _(sp):
            sp.dma_start(pack[:, :], a[f"experts{layer}"][:, E, :]).then_inc(sem["loaded"], 16)
            if layer == 0:
                sp.dma_start(m["packs"][:, :, :], a["experts1"][:, 0:E, :]).then_inc(m["packs_loaded"], 16)

            def load_routed(g, u):
                sp.wait_ge(sem["summed"], g + 1)
                for c in range(2):
                    sp.dma_start(routed[:, u, c, :, :], y[c][:, bass.ds(g * GROUP, GROUP), :])\
                      .then_inc(sem[f"routed{u}"], 16)

            if layer == 0:
                staggered(sp, [(load_routed, 0)])

        @block.gpsimd
        def _(pool):
            def root(g, u):
                inverse_root(pool, sem, g, rstd[:, u], m["power"])

            if layer == 0:
                staggered(pool, [(root, 0)])
            else:
                for t in range(TILES):
                    scatter_tile(pool, m, 1, t, 0).then_inc(sem["scattered"], 16)
                pool.wait_ge(sem["scattered"], 16 * TILES)

        @block.tensor
        def _(pe):
            pe.wait_ge(sem["loaded"], 16)
            pe.sem_inc(sem["downed"], 2)

            def make_hidden(g, half):
                for k in range(KI):
                    pe.wait_ge(sem["hidden_ready"], g * KI + k + 1)
                    pe.matmul(ps[:, k, :], pack[:, P * k:P * k + P], xT[:, bass.ds(g * GN, GN)],
                              start=True, stop=True).then_inc(sem["upped"], 1)

            def make_out(g, half):
                pe.wait_ge(sem["hidden_ready"], g * KI + 2 * KI)
                pe.wait_ge(sem["summed"], g + 1)
                for t in range(GROUP):
                    for k in range(KI):
                        n = P_DOWN + D * k
                        ins = pe.matmul(ps[:, 4 + half, P * t:P * t + P], hidden[:, half, k, P * t:P * t + P],
                                        pack[:, n:n + D], start=(k == 0), stop=(k == KI - 1))
                ins.then_inc(sem["downed"], 1)

            with pe.Fori(0, GROUPS // 2) as i:
                make_hidden(i * 2, 0)
                make_hidden(i * 2 + 1, 1)
                make_out(i * 2, 0)
                make_out(i * 2 + 1, 1)

        @block.scalar
        def _(act):
            act.wait_ge(sem["loaded"], 16)
            act.sem_inc(sem["hidden_ready"], KI)
            with act.Fori(0, GROUPS // 2) as i:
                for half in range(2):
                    g = i * 2 + half
                    act.wait_ge(sem["downed"], g + 1)
                    for k in range(KI):
                        act.wait_ge(sem["upped"], g * KI + k + 1)
                        act.activation(hidden[:, half, k, :], ps[:, k, :], act_func,
                                       bias=pack[:, P_BIAS + k:P_BIAS + k + 1])\
                           .then_inc(sem["hidden_ready"], 1)

        @block.vector
        def _(dve):
            dve.wait_ge(sem["loaded"], 16)
            if layer == 0:
                ins = dve.tensor_tensor(out_bias[:, :], pack[:, P_OUT:PACK], m["rows"][:, R_BO:R_BO + D], ALU.add)
            else:
                ins = dve.tensor_copy(out_bias[:, :], pack[:, P_OUT:PACK])
            ins.then_inc(sem["bias_ready"], 1)
            dve.wait_ge(sem["bias_ready"], 1)
            dve.sem_inc(sem["summed"], 2)

            def add_all(g, u):
                tiles = stream[:, bass.ds(g * GROUP, GROUP), :]
                if layer == 0:
                    dve.wait_ge(sem[f"routed{u}"], g * 16 + (32 - 16 * u))
                    r = routed[:, u]
                    c = Chain(dve, sem["chain"], g * 2)
                    c.link(dve.tensor_tensor(r[:, 0], r[:, 0], r[:, 1], ALU.add))
                    c.link(dve.tensor_tensor(tiles, tiles, r[:, 0], ALU.add))
                dve.wait_ge(sem["downed"], g + 3)
                dve.tensor_tensor(result[:, u, :, :], ps[:, 4 + u, :].rearrange("p (k d) -> p k d", d=D),
                                  out_bias[:, :].unsqueeze(1).broadcast_to([P, GROUP, D]),
                                  ALU.add).then_inc(sem["summed"], 1)
                dve.wait_ge(sem["summed"], g + 3)
                if layer == 0:
                    ins = dve.tensor_tensor(tiles, tiles, result[:, u, :, :], ALU.add)
                else:
                    for k in range(GROUP):
                        tile = tile_of(stream, g * GROUP + k)
                        ins = dve.scalar_tensor_tensor(
                            tile, result[:, u, k, :],
                            weights[:, bass.ds(g * GROUP + k, 1), E:E + 1].rearrange("p k e -> p (k e)"),
                            tile, ALU.mult, ALU.add)
                ins.then_inc(sem["added"], 1)

            def measure(g, u):
                dve.wait_ge(sem["added"], g + 1)
                dve.sem_inc(sem["added_seen"], 1)
                moments(dve, sem, g, stream, g * GROUP, stats[:, u], mv[:, u], rstd[:, u], m["post"], EPS)

            def normalise(g, u):
                dve.wait_ge(sem["rstd"], g + 1)
                for k in range(GROUP):
                    dve.tensor_scalar(tile_of(m["xn"], g * GROUP + k), tile_of(stream, g * GROUP + k),
                                      mv[:, u, k, 0:1], rstd[:, u, k:k + 1], ALU.subtract, ALU.mult)

            staggered(dve, [(add_all, 0)] if layer else [(normalise, 2), (measure, 1), (add_all, 0)])


def add_routed(nc, m, out):
    stream = m["stream"]
    buffers = 4
    with ExitStack() as ctx:
        routed = ctx.enter_context(nc.sbuf_tensor("routed1", [P, buffers, GROUP, D], F32))
        sem, block = ctx.enter_context(stage(nc, "z_", ["added", "stored"] + [f"routed{u}" for u in range(buffers)]))
        y = m["y_dram"][1][0:TOKENS, :].rearrange("(t p) d -> p t d", p=P)

        @block.sync
        def _(sp):
            def load(g, u):
                wait_from(sp, sem["added"], g - buffers + 1)
                sp.dma_start(routed[:, u, :, :], y[:, bass.ds(g * GROUP, GROUP), :]).then_inc(sem[f"routed{u}"], 16)

            staggered(sp, [(load, 0)], GROUPS, buffers)

        @block.vector
        def _(dve):
            def add(g, u):
                dve.wait_ge(sem[f"routed{u}"], g * (16 // buffers) + (16 - 16 // buffers * u))
                tiles = stream[:, bass.ds(g * GROUP, GROUP), :]
                dve.tensor_tensor(tiles, tiles, routed[:, u, :, :], ALU.add).then_inc(sem["added"], 1)

            staggered(dve, [(add, 0)], GROUPS, buffers)

        @block.scalar
        def _(act):
            def store(g, u):
                act.wait_ge(sem["added"], g + 1)
                tiles = bass.ds(g * GROUP, GROUP)
                act.dma_start(out[:, tiles, :], stream[:, tiles, :]).then_inc(sem["stored"], 16)

            staggered(act, [(store, 0)], GROUPS, buffers)
            act.wait_ge(sem["stored"], 16 * GROUPS)


def tile_of(t, k):
    return t[:, bass.ds(k, 1), :].rearrange("p k d -> p (k d)")


def moments(dve, sem, g, source, first, stats, mv, rstd, post, eps):
    for k in range(GROUP):
        ins = dve.bn_stats(stats[:, k, :], tile_of(source, first + k))
    ins.then_inc(sem["stats"], 1)
    dve.wait_ge(sem["stats"], g + 1)
    dve.memset(post[:, :], 0.0)
    for k in range(GROUP):
        ins = dve.bn_aggr(mv[:, k, :], stats[:, k, :])
    ins.then_inc(sem["moments"], 1)
    dve.wait_ge(sem["moments"], g + 1)
    dve.tensor_scalar(rstd, mv[:, :, 1], eps, None, ALU.add).then_inc(sem["raised"], 1)


def inverse_roots(c, x, guess, root):
    dve, bits = c.engine, mybir.dt.int32
    c.link(dve.tensor_scalar(x[:, :], x[:, :], TINY, None, ALU.max))
    c.link(dve.tensor_scalar(guess[:, :].bitcast(bits), x[:, :].bitcast(bits), 1, None, ALU.logical_shift_right))
    c.did(dve.tensor_scalar(root[:, :].bitcast(bits), guess[:, :].bitcast(bits), -1.0, float(0x5f3759df),
                            ALU.mult, ALU.add))
    c.link(dve.tensor_scalar(x[:, :], x[:, :], -0.5, None, ALU.mult))
    for _ in range(NEWTON):
        c.link(dve.tensor_tensor(guess[:, :], root[:, :], root[:, :], ALU.mult))
        c.link(dve.tensor_tensor(guess[:, :], guess[:, :], x[:, :], ALU.mult))
        c.link(dve.scalar_tensor_tensor(root[:, :], guess[:, :], 1.5, root[:, :], ALU.add, ALU.mult))


def inverse_root(pool, sem, g, rstd, power):
    pool.wait_ge(sem["raised"], g + 1)
    pool.tensor_tensor(rstd, rstd, power[:, 0:GROUP], ALU.pow).then_inc(sem["rstd"], 1)


def convolve(nc, a, m):
    ps, xn, ident = m["ps"], m["xn"], m["ident"]
    y = m["xT"][:, :].rearrange("p (t h) -> p t h", h=D)
    QUADS = CH // 4
    with ExitStack() as ctx:
        toeplitz = ctx.enter_context(nc.sbuf_tensor("toeplitz", [P, 2, CH, T], F32))
        xc = ctx.enter_context(nc.sbuf_tensor("xc", [P, 2, CH, 2, B], F32))
        yb = ctx.enter_context(nc.sbuf_tensor("yb", [P, QUADS, T], F32))
        sem, block = ctx.enter_context(stage(nc, "c_",
            ("loaded0", "loaded1", "xc_ready", "convolved", "yb_ready", "turned", "placed")))

        @block.sync
        def _(sp):
            sp.wait_ge(m["kernel_stored"], 16 * (1 + 8))
            for q in range(D // CH):
                sp.wait_ge(sem["convolved"], q + 1)
                src = bass.AP(m["kernel_dram"].tensor, q * (CH * KPAD), [[1, P], [KPAD, CH], [1, T]])
                sp.dma_start(toeplitz[:, q % 2, :, :], src).then_inc(sem[f"loaded{q % 2}"], 16)

        @block.gpsimd
        def _(pool):
            with pool.Fori(0, D // CH // 2) as i:
                for u in range(2):
                    q = i * 2 + u
                    pool.wait_ge(sem["convolved"], q + 1)
                    for t in range(2):
                        ins = pool.tensor_copy(
                            xc[:, u, :, t, :],
                            xn[:, t::2, bass.ds(q * CH, CH)].rearrange("p b c -> p c b"))
                    ins.then_inc(sem["xc_ready"], 1)

        @block.tensor
        def _(pe):
            pe.sem_inc(sem["convolved"], 2)
            pe.sem_inc(sem["turned"], 1)
            with pe.Fori(0, D // CH // 2) as i:
                for u in range(2):
                    q = i * 2 + u
                    pe.wait_ge(sem[f"loaded{u}"], i * 16 + 16)
                    pe.wait_ge(sem["xc_ready"], q + 1)
                    pe.wait_ge(sem["yb_ready"], q + 1)
                    for k in range(QUADS):
                        bank = ps[:, 2 * u + k // 2, (k % 2) * T:(k % 2) * T + T]
                        for r in range(4):
                            pe.matmul(bank[32 * r:32 * r + 32, :], xc[:, u, 4 * k + r, 0, :],
                                      toeplitz[:, u, 4 * k + r, :], start=True, stop=False,
                                      tile_position=(0, 32 * r), skip_group_check=True)
                        for r in range(4):
                            ins = pe.matmul(bank[32 * r:32 * r + 32, 0:P], xc[:, u, 4 * k + r, 1, :],
                                            toeplitz[:, u, 4 * k + r, P:T], start=False, stop=True,
                                            tile_position=(0, 32 * r), skip_group_check=True)
                    ins.then_inc(sem["convolved"], 1)
                    pe.wait_ge(sem["yb_ready"], q + 2)
                    pe.wait_ge(sem["placed"], q + 1)
                    for t in range(2):
                        for k in range(QUADS):
                            ins = pe.transpose(ps[:, 4 + t, P * k:P * k + P], yb[:, k, P * t:P * t + P], ident)
                    ins.then_inc(sem["turned"], 1)

        @block.scalar
        def _(act):
            act.sem_inc(sem["yb_ready"], 1)
            with act.Fori(0, D // CH // 2) as i:
                for u in range(2):
                    q = i * 2 + u
                    act.wait_ge(sem["convolved"], q + 3)
                    act.wait_ge(sem["turned"], q + 1)
                    act.copy(yb[:, :, :], ps[:, 2 * u:2 * u + 2, :].rearrange(
                        "p k (j t) -> p (k j) t", t=T)[:, :, ::-1]).then_inc(sem["yb_ready"], 1)

        @block.vector
        def _(dve):
            dve.sem_inc(sem["placed"], 1)
            with dve.Fori(0, D // CH) as q:
                dve.wait_ge(sem["turned"], q + 2)
                for t in range(2):
                    ins = dve.tensor_copy(y[:, t::2, bass.ds(q * CH, CH)].rearrange("p b c -> p c b"),
                                          ps[:, 4 + t, :].rearrange("p (c b) -> p c b", b=B))
                ins.then_inc(sem["placed"], 1)


def glu_and_norm(nc, a, m):
    ps, stream, ident, rows = m["ps"], m["stream"], m["ident"], m["rows"]
    y = m["xT"][:, :].rearrange("p (t h) -> p t h", h=D)
    with ExitStack() as ctx:
        def sb(name, shape, dt=F32):
            return ctx.enter_context(nc.sbuf_tensor(name, shape, dt))

        w_out = sb("w_out", [P, 2 * D])
        ys = sb("ys", [P, 2, GROUP, D])
        yT = sb("yT", [P, 2, GN])
        glu = sb("glu", [P, 4, GROUP, 2 * D])
        stats, mv, rstd = sb("stats2", [P, 4, GROUP, 6]), sb("mv2", [P, 4, GROUP, 2]), sb("rstd2", [P, 4, GROUP])
        z = sb("z2", [P, 2, GROUP, D])
        sem, block = ctx.enter_context(stage(nc, "g_",
            ("loaded", "staged", "turned", "yT_ready", "projected", "biased", "tanh", "gated",
                "stats", "moments", "raised", "rstd",
                "normal", "shifted", "scaled", "scaled_seen", "added")))
        wide = lambda first, n: rows[:, first:first + n].unsqueeze(1).broadcast_to([P, GROUP, n])

        @block.sync
        def _(sp):
            sp.dma_start(w_out[:, :], a["w_out"]).then_inc(sem["loaded"], 16)

        @block.gpsimd
        def _(pool):
            def shift(g, u):
                tiles = stream[:, bass.ds(g * GROUP, GROUP), :]
                pool.tensor_tensor(tiles, tiles, wide(R_BETA, D), ALU.add).then_inc(sem["shifted"], 1)

            def root(g, u):
                inverse_root(pool, sem, g, rstd[:, u], m["power"])

            def add(g, u):
                pool.wait_ge(sem["shifted"], g + 1)
                pool.wait_ge(sem["scaled"], g + 1)
                pool.sem_inc(sem["scaled_seen"], 1)
                tiles = stream[:, bass.ds(g * GROUP, GROUP), :]
                pool.tensor_tensor(tiles, tiles, z[:, u % 2, :, :], ALU.add).then_inc(sem["added"], 1)

            pool.sem_inc(sem["added"], 1)
            staggered(pool, [(root, 1), (add, 2), (shift, 0)], GROUPS, 4)

        @block.tensor
        def _(pe):
            pe.wait_ge(sem["loaded"], 16)

            def turn(g, u):
                pe.wait_ge(sem["staged"], g + 1)
                wait_from(pe, sem["yT_ready"], g - 1)
                for k in range(GROUP):
                    ins = pe.transpose(ps[:, u % 2, P * k:P * k + P], ys[:, u % 2, k, :], ident)
                ins.then_inc(sem["turned"], 1)

            def project(g, u):
                pe.wait_ge(sem["yT_ready"], g + 1)
                wait_from(pe, sem["biased"], g - 1)
                for k in range(GROUP):
                    ins = pe.matmul(ps[:, 2 + 2 * (u % 2) + k // 2, (k % 2) * 2 * D:(k % 2) * 2 * D + 2 * D],
                                    yT[:, u % 2, P * k:P * k + P], w_out[:, :], start=True, stop=True)
                ins.then_inc(sem["projected"], 1)

            staggered(pe, [(turn, 0), (project, 1)], GROUPS, 4)

        @block.scalar
        def _(act):
            def fix(g, u):
                wait_from(act, sem["turned"], g - 1)
                act.copy(ys[:, u % 2, :, :], y[:, bass.ds(g * GROUP, GROUP), :]).then_inc(sem["staged"], 1)

            def take_yT(g, u):
                act.wait_ge(sem["turned"], g + 1)
                wait_from(act, sem["projected"], g - 1)
                act.activation(yT[:, u % 2, :], ps[:, u % 2, :], ACT.Gelu_apprx_tanh).then_inc(sem["yT_ready"], 1)

            def gate(g, u):
                act.wait_ge(sem["biased"], g + 1)
                act.activation(glu[:, u, :, D:2 * D], glu[:, u, :, D:2 * D], ACT.Tanh, scale=0.5)\
                   .then_inc(sem["tanh"], 1)

            staggered(act, [(fix, 0), (take_yT, 1), (gate, 2)], GROUPS, 4)

        @block.vector
        def _(dve):
            def add_bias(g, u):
                wait_from(dve, sem["scaled"], g - 3)
                dve.wait_ge(sem["projected"], g + 1)
                dve.tensor_tensor(glu[:, u, :, :],
                                  ps[:, 2 + 2 * (u % 2):4 + 2 * (u % 2), :]
                                  .rearrange("p k (j d) -> p (k j) d", d=2 * D),
                                  wide(R_BOUT, 2 * D), ALU.add).then_inc(sem["biased"], 1)

            def gate_and_measure(g, u):
                dve.wait_ge(sem["tanh"], g + 1)
                v = glu[:, u, :, 0:D]
                dve.scalar_tensor_tensor(v, glu[:, u, :, D:2 * D], 1.0, v, ALU.add, ALU.mult)\
                    .then_inc(sem["gated"], 1)
                dve.wait_ge(sem["gated"], g + 1)
                moments(dve, sem, g, v, 0, stats[:, u], mv[:, u], rstd[:, u], m["post"], 4 * EPS)

            def normalise(g, u):
                dve.wait_ge(sem["rstd"], g + 1)
                wait_from(dve, sem["added"], g)
                for k in range(GROUP):
                    ins = dve.tensor_scalar(z[:, u % 2, k, :], glu[:, u, k, 0:D], mv[:, u, k, 0:1],
                                            rstd[:, u, k:k + 1], ALU.subtract, ALU.mult)
                ins.then_inc(sem["normal"], 1)

            def scale(g, u):
                dve.wait_ge(sem["normal"], g + 1)
                dve.tensor_tensor(z[:, u % 2, :, :], z[:, u % 2, :, :], wide(R_GAMMA, D), ALU.mult)\
                   .then_inc(sem["scaled"], 1)

            staggered(dve, [(normalise, 3), (gate_and_measure, 2), (scale, 3), (add_bias, 0)], GROUPS, 4)


def norm_and_gate1(nc, a, m):
    ps, stream, xn, xT, ident = m["ps"], m["stream"], m["xn"], m["xT"], m["ident"]
    with ExitStack() as ctx:
        def sb(name, shape, dt=F32):
            return ctx.enter_context(nc.sbuf_tensor(name, shape, dt))

        wg = sb("wg", [P, E + 2])
        nwb = sb("nwb", [P, 2])
        stats, mv, rstd = sb("stats3", [P, 2, GROUP, 6]), sb("mv3", [P, 2, GROUP, 2]), sb("rstd3", [P, 2, GROUP])
        z = sb("z3", [P, 2, GROUP, D])
        aT = sb("aT", [P, 2, GN])
        sem, block = ctx.enter_context(stage(nc, "q_",
            ("loaded", "stats", "moments", "raised", "rstd", "normal", "turned", "aT_ready",
                "kept", "kept_seen", "logits", "taken")))

        @block.sync
        def _(sp):
            sp.dma_start(wg[:, :], a["wg"]).then_inc(sem["loaded"], 16)
            sp.dma_start(nwb[:, :], a["nwb"]).then_inc(sem["loaded"], 16)

        @block.gpsimd
        def _(pool):
            def root(g, u):
                inverse_root(pool, sem, g, rstd[:, u], m["power"])

            def add_residual(g, u):
                tiles = stream[:, bass.ds(g * GROUP, GROUP), :]
                pool.tensor_tensor(tiles, tiles, xn[:, bass.ds(g * GROUP, GROUP), :], ALU.add)\
                    .then_inc(sem["kept"], 1)

            staggered(pool, [(root, 0), (add_residual, 0)])

        @block.vector
        def _(dve):
            def measure(g, u):
                moments(dve, sem, g, xn, g * GROUP, stats[:, u], mv[:, u], rstd[:, u], m["post"], EPS_NW)

            def normalise(g, u):
                dve.wait_ge(sem["rstd"], g + 1)
                wait_from(dve, sem["turned"], g - 1)
                for k in range(GROUP):
                    ins = dve.tensor_scalar(z[:, u, k, :], tile_of(xn, g * GROUP + k), mv[:, u, k, 0:1],
                                            rstd[:, u, k:k + 1], ALU.subtract, ALU.mult)
                ins.then_inc(sem["normal"], 1)

            def keep(g, u):
                dve.wait_ge(sem["normal"], g + 1)
                dve.wait_ge(sem["kept"], g + 1)
                dve.sem_inc(sem["kept_seen"], 1)
                dve.tensor_copy(xn[:, bass.ds(g * GROUP, GROUP), :], z[:, u, :, :])

            def take_logits(g, u):
                dve.wait_ge(sem["logits"], g + 1)
                dve.tensor_copy(m["weights"][:, bass.ds(g * GROUP, GROUP), 0:E + 2],
                                ps[:, 2 + u, 0:GROUP * (E + 2)].rearrange("p (k e) -> p k e", e=E + 2))\
                   .then_inc(sem["taken"], 1)

            staggered(dve, [(normalise, 2), (measure, 0), (keep, 2), (take_logits, 4)])

        @block.tensor
        def _(pe):
            pe.wait_ge(sem["loaded"], 32)

            def turn(g, u):
                pe.wait_ge(sem["normal"], g + 1)
                wait_from(pe, sem["aT_ready"], g - 1)
                for k in range(GROUP):
                    ins = pe.transpose(ps[:, u, P * k:P * k + P], z[:, u, k, :], ident)
                ins.then_inc(sem["turned"], 1)

            def make_logits(g, u):
                pe.wait_ge(sem["aT_ready"], g + 1)
                wait_from(pe, sem["taken"], g - 1)
                for k in range(GROUP):
                    ins = pe.matmul(ps[:, 2 + u, (E + 2) * k:(E + 2) * (k + 1)], aT[:, u, P * k:P * k + P],
                                    wg[:, :], start=True, stop=True)
                ins.then_inc(sem["logits"], 1)

            staggered(pe, [(turn, 0), (make_logits, 1)])

        @block.scalar
        def _(act):
            act.wait_ge(sem["loaded"], 32)

            def take_aT(g, u):
                act.wait_ge(sem["turned"], g + 1)
                wait_from(act, sem["logits"], g - 1)
                act.activation(xT[:, bass.ds(g * GN, GN)], ps[:, u, :], ACT.Identity, bias=nwb[:, 1:2],
                               scale=nwb[:, 0:1])
                act.activation(aT[:, u, :], ps[:, u, :], ACT.Identity, bias=nwb[:, 1:2],
                               scale=nwb[:, 0:1]).then_inc(sem["aT_ready"], 1)

            staggered(act, [(take_aT, 0)])


def top1(nc, a, m):
    ps, cst, weights = m["ps"], m["cst"], m["weights"]
    with ExitStack() as ctx:
        def sb(name, shape, dt=F32):
            return ctx.enter_context(nc.sbuf_tensor(name, shape, dt))

        z, mask = sb("z4", [P, TILES, E]), sb("mask4", [P, TILES, E])
        place, before = sb("place", [P, TILES, E]), sb("before", [P, E, TILES])
        coef = sb("coef", [P, TILES, 2])
        slot = sb("slot4", [P, TILES, E])
        total = sb("total4", [P, E])
        token = cst[:, C_TOKEN:C_TOKEN + TILES]
        ones = sb("ones", [P, P])
        v = [sb(f"w{i}", [P, TILES]) for i in range(4)]
        sem, block = ctx.enter_context(stage(nc, "o_",
            ("args", "expo", "mask", "counts", "chain")))
        jrev = cst[:, C_JREV:C_JREV + E].unsqueeze(1).broadcast_to([P, TILES, E])
        wide = lambda t: t.unsqueeze(2).broadcast_to([P, TILES, E])

        @block.scalar
        def _(act):
            act.wait_ge(sem["args"], 1)
            act.activation(z[:, :, :], z[:, :, :], ACT.Exp).then_inc(sem["expo"], 1)
            act.wait_ge(sem["args"], 2)
            act.activation(coef[:, :, :], coef[:, :, :], ACT.Exp).then_inc(sem["expo"], 1)

        @block.tensor
        def _(pe):
            count(pe, m, sem, mask, ones)

        @block.vector
        def _(dve):
            c = Chain(dve, sem["chain"])
            tt = dve.tensor_tensor
            c.did(dve.memset(ones[:, :], 1.0))
            softmax_parts(c, dve, (sem["expo"], 1), sem["args"], weights[:, :, 0:E], v[0], z, v[1])
            softmax_parts(c, dve, (sem["expo"], 2), sem["args"], weights[:, :, E:E + 2], v[2], coef, v[3])
            first_of(c, dve, mask, z, v[0], v[1], jrev)
            dve.engine_nop().then_inc(sem["mask"], 1)
            rowbuf, ts = m["rowbuf"], dve.tensor_scalar
            c.did(ts(rowbuf[:, :, ROW_E1], v[1][:, :], -1.0, float(E), ALU.mult, ALU.add))
            c.did(ts(rowbuf[:, :, ROW_ID], token, float(TOKENS), None, ALU.add))
            c.did(dve.memset(rowbuf[:, :, ROW_W2], 0.0))
            dve.wait_ge(sem["counts"], 1)
            places(c, dve, ps, ones, before, place, total[:, :])
            c.link(tt(slot[:, :, :], mask[:, :, :], place[:, :, :], ALU.mult))
            c.link(dve.tensor_reduce(v[2][:, :], slot[:, :, :], AX.X, ALU.add))
            c.link(ts(v[3][:, :], v[2][:, :], float(CAP), None, ALU.is_lt))
            c.link(dve.scalar_tensor_tensor(v[2][:, :], rowbuf[:, :, ROW_E1], float(CAP), v[2][:, :],
                                            ALU.mult, ALU.add))
            c.link(tt(v[2][:, :], v[2][:, :], rowbuf[:, :, ROW_ID], ALU.subtract))
            c.link(tt(v[2][:, :], v[2][:, :], v[3][:, :], ALU.mult))
            c.link(tt(v[2][:, :], v[2][:, :], rowbuf[:, :, ROW_ID], ALU.add))
            c.did(dve.tensor_copy(m["slots"][:, 0, :], v[2][:, :]))
            c.did(dve.tensor_copy(m["table"][:, 0:LOTS[1]], cst[:, C_TABLE1:C_TABLE1 + LOTS[1]]))
            c.did(dve.tensor_copy(m["table_int"][:, 0:LOTS[1]], cst[:, C_TABLE1:C_TABLE1 + LOTS[1]]))
            c.link(dve.tensor_scalar(place[:, :, :], place[:, :, :], float(CAP), None, ALU.is_lt))
            c.did(tt(z[:, :, :], z[:, :, :], mask[:, :, :], ALU.mult))
            c.link(tt(place[:, :, :], place[:, :, :], wide(coef[:, :, 1]), ALU.mult))
            c.link(tt(weights[:, :, 0:E], z[:, :, :], place[:, :, :], ALU.mult))
            dve.tensor_reduce(rowbuf[:, :, ROW_DW], weights[:, :, 0:E], AX.X, ALU.add)
            dve.tensor_copy(weights[:, :, E], coef[:, :, 0])


def constants():
    c = np.zeros((P, C_END), np.float32)
    c[:, C_ID:C_ID + P] = np.eye(P)
    c[:, C_TRI:C_TRI + P] = np.triu(np.ones((P, P)), 1)
    c[:, C_JREV:C_JREV + E] = E - np.arange(E)
    down = np.arange(LOW)[::-1]
    c[:, C_LAG:C_LAG + 2 * LOW] = np.concatenate([down, LOW * down])
    c[:, C_COUNT:C_COUNT + LOTS[0]] = np.arange(LOTS[0])
    c[:, C_TOKEN:C_TOKEN + TILES] = np.arange(TILES) * P + np.arange(P)[:, None]
    c[:, C_TABLE1:C_TABLE1 + LOTS[1]] = np.arange(LOTS[1]) * LOT // CAP
    c[:, C_MASK:C_MASK + P] = np.kron(np.eye(8), np.ones((LOW, LOW)))
    return c


def arrange(i):
    def f(name):
        return np.asarray(i[name])

    def column(v):
        return v.reshape(-1, 1)

    def pack(up, shared_up, down, shared_down, bias, shared_bias, out, shared_out):
        up = np.concatenate([up, shared_up[None]]).transpose(1, 0, 2)
        down = np.concatenate([down, shared_down[None]]).reshape(EA, KI, P, D).transpose(2, 0, 1, 3)
        bias = np.concatenate([bias, shared_bias[None]]).reshape(EA, KI, P).transpose(2, 0, 1)
        out = np.broadcast_to(np.concatenate([out, shared_out[None]])[None], (P, EA, D))
        return np.concatenate([up, down.reshape(P, EA, KI * D), bias, out], axis=2)

    r = {
        "x": f("L0_attn_x").reshape(TOKENS, D),
        "cst": constants(),
        "rows": np.broadcast_to(np.concatenate([
            f("L0_attn_bq"), f("L0_attn_bk"), f("L0_attn_bv"), f("L1_attn_b_out"), f("L1_attn_gamma"),
            f("L1_attn_beta"), f("L0_attn_bo")]), (P, R_END)),
        "s4": np.concatenate([f("L1_attn_A_re"), f("L1_attn_A_im"), f("L1_attn_C_re"), f("L1_attn_C_im"),
                              column(f("L1_attn_log_dt")), column(f("L1_attn_D"))], axis=1),
        "w_router": np.concatenate([f("L0_ffn_Wr1"), f("L0_attn_Wg1").T], axis=1),
        "wr2": np.concatenate([f("L0_ffn_Wr2"), f("L0_ffn_br2")[None]]),
        "b_router": np.stack([np.pad(f("L0_ffn_br1"), (0, HG - R1)), f("L0_attn_bg1")], axis=1),
        "wg2": np.repeat(f("L0_attn_Wg2").T, DK, axis=1),
        "gate_bias": np.repeat(np.stack([f("L0_attn_bg2"), f("L0_attn_g")], axis=1), DK, axis=0),
        "wqkv": np.concatenate([f("L0_attn_Wq").T, f("L0_attn_Wk").T, f("L0_attn_Wv").T], axis=1),
        "wo": f("L0_attn_Wo").T,
        "experts0": pack(*(f("L0_ffn_" + n) for n in ("We1", "Ws1", "We2", "Ws2", "be1", "bs1", "be2", "bs2"))),
        "w_out": f("L1_attn_W_out"),
        "wg": np.concatenate([f("L1_ffn_wg"), f("L1_ffn_res_coef")], axis=1),
        "nwb": np.stack([f("L1_ffn_attn_nw"), f("L1_ffn_attn_nb")], axis=1),
        "experts1": pack(*(f("L1_ffn_" + n) for n in ("inter_w", "res_inter_w", "output_w", "res_output_w",
                                                       "inter_b", "res_inter_b", "output_b",
                                                       "res_output_b"))),
    }
    return {k: np.ascontiguousarray(v) for k, v in r.items()}


def kernel(**inputs):
    import concourse.bacc as bacc
    from concourse.bass_utils import run_bass_kernel_spmd

    arrays = arrange(inputs)
    nc = bacc.Bacc("TRN2", target_bir_lowering=False, num_devices=1)
    a = {k: nc.dram_tensor("in_" + k, v.shape, F32, kind="ExternalInput").ap() for k, v in arrays.items()}
    out = nc.dram_tensor("out", (TOKENS, D), F32, kind="ExternalOutput").ap()
    build(nc, a, out)
    r = run_bass_kernel_spmd(nc, [{"in_" + k: v for k, v in arrays.items()}], core_ids=[0])
    return np.asarray(r.results[0]["out"]).reshape(B, T, D)
```
